# Optimizing a Trainium2 kernel written in Bass

```python
import numpy as np
import jax
import jax.numpy as jnp

def _softmax(x, axis=-1):
    return jax.nn.softmax(x, axis=axis)

def _gelu(x):
    return jax.nn.gelu(x, approximate=True)

def _silu(x):
    return jax.nn.silu(x)

def _sigmoid(x):
    return jax.nn.sigmoid(x)

def _layernorm(x, axis=-1, eps=1e-05):
    m = jnp.mean(x, axis=axis, keepdims=True)
    v = jnp.var(x, axis=axis, keepdims=True)
    return (x - m) / jnp.sqrt(v + eps)

def _scatter_add(tgt, idx, src, axis=0):
    return tgt.at[idx].add(src)

def _segment_sum(src, seg, n):
    return jax.ops.segment_sum(src, seg, n)
kernel_name = 'mk_gnn_ffn_d4_gnn_r8_af9ec4'

def setup_inputs(seed: int=0):
    np.random.seed(seed)
    _w = jnp.asarray

    def _rec_inputs():
        import jax
        import jax.numpy as jnp
        _gk = jax.random.key(seed)
        x = -0.001003 + 1 * jax.random.normal(jax.random.fold_in(_gk, 1), (384, 512), jnp.float32)
        src = jax.random.randint(jax.random.fold_in(_gk, 2), (6144,), 0, 384, jnp.int32)
        dst = jnp.minimum((384 * jax.random.uniform(jax.random.fold_in(_gk, 3), (6144,)) ** 2.0).astype(jnp.int32), 3071)
        _o = jnp.argsort(dst, stable=True)
        src = src[_o]
        dst = dst[_o]
        return (x, src, dst)
    x, src, dst = _rec_inputs()

    def _L0_gnn_setup():
        import jax, jax.numpy as jnp
        import numpy as np
        N = 384
        HID = 512
        H = 8
        HD = HID // H
        E = 12288
        LN_EPS = 1e-05
        key = jax.random.key(seed)
        ks = jax.random.split(key, 12)
        x = jax.random.normal(ks[0], (N, HID), jnp.float32)
        lin = jax.random.permutation(ks[1], N * N)[:E]
        edges = jnp.stack([lin // N, lin % N]).astype(jnp.int32)
        s = 0.02
        Wv = jax.random.normal(ks[2], (HID, HID), jnp.float32) * s
        bv = jax.random.normal(ks[3], (HID,), jnp.float32) * s
        Ww = jax.random.normal(ks[4], (2 * HID, 2 * HID), jnp.float32) * s
        bw = jax.random.normal(ks[5], (2 * HID,), jnp.float32) * s
        Wa = jax.random.normal(ks[6], (2 * HD, 1), jnp.float32) * s
        ba = jax.random.normal(ks[7], (1,), jnp.float32) * s
        gamma = jnp.ones((HID,), jnp.float32)
        beta = jnp.zeros((HID,), jnp.float32)
        return dict(x=x, edges=edges, Wv=Wv, bv=bv, Ww=Ww, bw=bw, Wa=Wa, ba=ba, gamma=gamma, beta=beta)
    _L0_gnn_all = _L0_gnn_setup()
    _L0_gnn_in = {k: v for k, v in _L0_gnn_all.items() if k in ('Wv', 'bv', 'Ww', 'bw', 'Wa', 'ba', 'gamma', 'beta')}
    del _L0_gnn_all

    def _L0_ffn_setup():
        import jax, jax.numpy as jnp
        import numpy as np
        MARK_AX = 0
        OPCODE_BASE = 16
        OP_SHL = OPCODE_BASE + 23
        OP_SHR = OPCODE_BASE + 24
        ALU_LO = 64
        ALU_HI = 80
        AX_CARRY_LO = 96
        OUTPUT_LO = 128
        OUTPUT_HI = 144
        B, SEQ, D = (8, 4096, 512)
        key = jax.random.key(seed)
        ks = jax.random.split(key, 6)
        x = jax.random.uniform(ks[0], (B, SEQ, D), dtype=jnp.float32) * 0.4
        mark = (jax.random.uniform(ks[1], (B, SEQ)) < 0.75).astype(jnp.float32)
        op_sel = jax.random.randint(ks[2], (B, SEQ), 0, 3)
        lo = jax.random.randint(ks[3], (B, SEQ), 0, 16)
        hi = jax.random.randint(ks[4], (B, SEQ), 0, 16)
        sa = jax.random.randint(ks[5], (B, SEQ), 0, 16)
        oh = lambda idx: jax.nn.one_hot(idx, 16, dtype=jnp.float32)
        x = x.at[..., MARK_AX].set(mark)
        x = x.at[..., OP_SHL].set((op_sel == 1).astype(jnp.float32))
        x = x.at[..., OP_SHR].set((op_sel == 2).astype(jnp.float32))
        x = x.at[..., ALU_LO:ALU_LO + 16].set(oh(lo))
        x = x.at[..., ALU_HI:ALU_HI + 16].set(oh(hi))
        x = x.at[..., AX_CARRY_LO:AX_CARRY_LO + 16].set(oh(sa))
        return {'x_bd': x}
    _L0_ffn_all = _L0_ffn_setup()
    _L0_ffn_in = {k: v for k, v in _L0_ffn_all.items() if k in ()}
    del _L0_ffn_all

    def _L1_gnn_setup():
        import jax, jax.numpy as jnp
        import numpy as np
        EPS = 1e-05

        def gcn_conv(x, src, dst, W, b):
            n = x.shape[0]
            xw = x @ W
            deg = jax.ops.segment_sum(jnp.ones(src.shape[0], x.dtype), dst, num_segments=n) + 1.0
            dinv = jax.lax.rsqrt(deg)
            coef = (dinv[src] * dinv[dst])[:, None]
            agg = jax.ops.segment_sum(xw[src] * coef, dst, num_segments=n)
            agg = agg + xw * (dinv * dinv)[:, None]
            return agg + b

        def graph_norm(x, weight, bias, mean_scale):
            mean = x.mean(axis=0, keepdims=True)
            out = x - mean * mean_scale
            var = (out * out).mean(axis=0, keepdims=True)
            return weight * out * jax.lax.rsqrt(var + EPS) + bias
        key = jax.random.key(seed)
        ks = jax.random.split(key, 9)
        N, E, d = (5000, 80000, 512)
        x = jax.random.normal(ks[0], (N, d), jnp.float32)
        edge_index = jax.random.randint(ks[1], (2, E), 0, N)
        inp = {'x': x, 'edge_index': edge_index}
        for i in range(3):
            inp[f'W{i}'] = jax.random.normal(ks[2 + i], (d, d), jnp.float32) / np.sqrt(d).astype(np.float32)
            inp[f'b{i}'] = jax.random.normal(ks[5 + i], (d,), jnp.float32) * 0.01
        inp['gn_weight'] = jnp.ones((d,), jnp.float32)
        inp['gn_bias'] = jnp.zeros((d,), jnp.float32)
        inp['gn_mean_scale'] = jnp.ones((d,), jnp.float32)
        return inp
    _L1_gnn_all = _L1_gnn_setup()
    _L1_gnn_in = {k: v for k, v in _L1_gnn_all.items() if k in ('W0', 'b0', 'W1', 'b1', 'W2', 'b2', 'gn_weight', 'gn_bias', 'gn_mean_scale')}
    del _L1_gnn_all

    def _L1_ffn_setup():
        import jax, jax.numpy as jnp
        import numpy as np
        EPS = 1e-05

        def _bitlinear(x, w):
            w_scale = jnp.clip(jnp.mean(jnp.abs(w)), EPS, None)
            w_q = jnp.clip(jnp.round(w / w_scale), -1.0, 1.0) * w_scale
            w_eff = w + jax.lax.stop_gradient(w_q - w)
            x_scale = 127.0 / jnp.clip(jnp.max(jnp.abs(x), axis=-1, keepdims=True), EPS, None)
            x_q = jnp.clip(jnp.round(x * x_scale), -128.0, 127.0) / x_scale
            x_eff = x + jax.lax.stop_gradient(x_q - x)
            return jnp.einsum('bsi,oi->bso', x_eff, w_eff)

        def _ste_round_clamp_int8(h):
            h_q = jnp.clip(jnp.round(h), -128.0, 127.0)
            return h + jax.lax.stop_gradient(h_q - h)
        key = jax.random.key(seed)
        k1, k2, k3 = jax.random.split(key, 3)
        B, S, D, F = (8, 1024, 512, 256)
        x = jax.random.normal(k1, (B, S, D), dtype=jnp.float32)
        w_up = jax.random.normal(k2, (F, D), dtype=jnp.float32) * (1.0 / np.sqrt(D))
        w_down = jax.random.normal(k3, (D, F), dtype=jnp.float32) * (1.0 / np.sqrt(F))
        return {'x': x, 'w_up': w_up, 'w_down': w_down}
    _L1_ffn_all = _L1_ffn_setup()
    _L1_ffn_in = {k: v for k, v in _L1_ffn_all.items() if k in ('w_up', 'w_down')}
    del _L1_ffn_all

    def _L2_gnn_setup():
        import jax, jax.numpy as jnp
        import numpy as np
        N_NODES = 6250
        N_EDGES = 50000
        IN_DIM = 512
        OUT_DIM = 512
        key = jax.random.key(seed)
        k1, k2, k3, k4 = jax.random.split(key, 4)
        x = jax.random.normal(k1, (N_NODES, IN_DIM), dtype=jnp.float32)
        edge_index = jax.random.randint(k2, (2, N_EDGES), 0, N_NODES, dtype=jnp.int64)
        W = jax.random.normal(k3, (OUT_DIM, IN_DIM), dtype=jnp.float32) / np.sqrt(IN_DIM)
        b = jax.random.normal(k4, (OUT_DIM,), dtype=jnp.float32) * 0.01
        return {'x': x, 'edge_index': edge_index, 'W': W, 'b': b}
    _L2_gnn_all = _L2_gnn_setup()
    _L2_gnn_in = {k: v for k, v in _L2_gnn_all.items() if k in ('W', 'b')}
    del _L2_gnn_all

    def _L2_ffn_setup():
        import jax, jax.numpy as jnp
        import numpy as np
        EPS = 1e-09
        LN_EPS = 1e-05

        def _layernorm(x, gamma):
            x = x.astype(jnp.float32)
            mu = jnp.mean(x, axis=-1, keepdims=True)
            var = jnp.var(x, axis=-1, keepdims=True)
            return (x - mu) * jax.lax.rsqrt(var + LN_EPS) * gamma
        key = jax.random.key(seed)
        ks = jax.random.split(key, 5)
        b, n, d, e, h = (4, 1024, 512, 6, 256)
        x = jax.random.normal(ks[0], (b, n, d), dtype=jnp.float32)
        w_gating = jax.random.normal(ks[1], (d, e), dtype=jnp.float32)
        std1 = 1.0 / np.sqrt(h)
        std2 = 1.0 / np.sqrt(d)
        w1 = jax.random.uniform(ks[2], (e, d, h), jnp.float32, -std1, std1)
        w2 = jax.random.uniform(ks[3], (e, h, d), jnp.float32, -std2, std2)
        gamma = jnp.ones((d,), dtype=jnp.float32)
        return {'x': x, 'w_gating': w_gating, 'gamma': gamma, 'w1': w1, 'w2': w2}
    _L2_ffn_all = _L2_ffn_setup()
    _L2_ffn_in = {k: v for k, v in _L2_ffn_all.items() if k in ('w_gating', 'gamma', 'w1', 'w2')}
    del _L2_ffn_all

    def _L3_gnn_setup():
        import jax, jax.numpy as jnp
        import numpy as np
        N_NODES = 1250
        N_EDGES = 20000
        IN_DIM = 512
        OUT_DIM = 512
        LN_EPS = 1e-05
        key = jax.random.key(seed)
        k_x, k_src, k_ws, k_wn = jax.random.split(key, 4)
        x = jax.random.normal(k_x, (N_NODES, IN_DIM), dtype=jnp.float32)
        edge_src = jax.random.randint(k_src, (N_EDGES,), 0, N_NODES, dtype=jnp.int32)
        edge_dst = jnp.repeat(jnp.arange(N_NODES, dtype=jnp.int32), N_EDGES // N_NODES)
        deg = jnp.full((N_NODES,), float(N_EDGES // N_NODES), dtype=jnp.float32)
        scale = 1.0 / np.sqrt(IN_DIM)
        W_self = jax.random.normal(k_ws, (OUT_DIM, IN_DIM), dtype=jnp.float32) * scale
        W_neigh = jax.random.normal(k_wn, (OUT_DIM, IN_DIM), dtype=jnp.float32) * scale
        bias = jnp.zeros((OUT_DIM,), dtype=jnp.float32)
        gamma = jnp.ones((OUT_DIM,), dtype=jnp.float32)
        beta = jnp.zeros((OUT_DIM,), dtype=jnp.float32)
        return {'x': x, 'edge_src': edge_src, 'edge_dst': edge_dst, 'deg': deg, 'W_self': W_self, 'W_neigh': W_neigh, 'bias': bias, 'gamma': gamma, 'beta': beta}
    _L3_gnn_all = _L3_gnn_setup()
    _L3_gnn_in = {k: v for k, v in _L3_gnn_all.items() if k in ('W_self', 'W_neigh', 'bias', 'gamma', 'beta')}
    del _L3_gnn_all

    def _L3_ffn_setup():
        import jax, jax.numpy as jnp
        import numpy as np
        DIM = 512
        MOE_DIM = 256
        E = 64
        G = 8
        TOPK_G = 4
        K = 8
        SCALE = 2.5
        CAP = 1024

        def _gate(x2, gate_w, gate_b):
            T = x2.shape[0]
            scores = jax.nn.sigmoid(x2 @ gate_w.T)
            s = (scores + gate_b).reshape(T, G, E // G)
            group_scores = jax.lax.top_k(s, 2)[0].sum(-1)
            top_groups = jax.lax.top_k(group_scores, TOPK_G)[1]
            gmask = jnp.zeros((T, G), bool).at[jnp.arange(T)[:, None], top_groups].set(True)
            s = jnp.where(gmask[..., None], s, -jnp.inf).reshape(T, E)
            idx = jax.lax.top_k(s, K)[1]
            w = jnp.take_along_axis(scores, idx, axis=1)
            w = w / w.sum(-1, keepdims=True) * SCALE
            return (w, idx)

        def _moe_forward(x, gate_w, gate_b, w1, w3, w2):
            shape = x.shape
            x2 = x.reshape(-1, DIM)
            T = x2.shape[0]
            w, idx = _gate(x2, gate_w, gate_b)
            flat_e = idx.reshape(-1)
            oh = (flat_e[:, None] == jnp.arange(E)[None, :]).astype(jnp.int32)
            pos = (jnp.cumsum(oh, axis=0) * oh).sum(-1) - 1
            x_rep = jnp.repeat(x2, K, axis=0)
            xb = jnp.zeros((E, CAP, DIM), x2.dtype).at[flat_e, pos].set(x_rep, mode='drop')
            h = jax.nn.silu(jnp.einsum('ecd,edm->ecm', xb, w1)) * jnp.einsum('ecd,edm->ecm', xb, w3)
            yb = jnp.einsum('ecm,emd->ecd', h, w2)
            y = yb.at[flat_e, pos].get(mode='fill', fill_value=0.0) * w.reshape(-1)[:, None]
            return y.reshape(T, K, DIM).sum(1).reshape(shape)
        key = jax.random.key(seed)
        ks = jax.random.split(key, 6)
        x = jax.random.normal(ks[0], (4, 512, DIM), jnp.float32)
        gate_w = jax.random.normal(ks[1], (E, DIM), jnp.float32) / np.sqrt(DIM).astype(np.float32)
        gate_b = jax.random.normal(ks[2], (E,), jnp.float32) * 0.01
        w1 = jax.random.normal(ks[3], (E, DIM, MOE_DIM), jnp.float32) / np.sqrt(DIM).astype(np.float32)
        w3 = jax.random.normal(ks[4], (E, DIM, MOE_DIM), jnp.float32) / np.sqrt(DIM).astype(np.float32)
        w2 = jax.random.normal(ks[5], (E, MOE_DIM, DIM), jnp.float32) / np.sqrt(MOE_DIM).astype(np.float32)
        return {'x': x, 'gate_w': gate_w, 'gate_b': gate_b, 'w1': w1, 'w3': w3, 'w2': w2}
    _L3_ffn_all = _L3_ffn_setup()
    _L3_ffn_in = {k: v for k, v in _L3_ffn_all.items() if k in ('gate_w', 'gate_b', 'w1', 'w3', 'w2')}
    del _L3_ffn_all
    return {'x': x, 'src': src, 'dst': dst, 'L0_gnn_Wv': _L0_gnn_in['Wv'], 'L0_gnn_bv': _L0_gnn_in['bv'], 'L0_gnn_Ww': _L0_gnn_in['Ww'], 'L0_gnn_bw': _L0_gnn_in['bw'], 'L0_gnn_Wa': _L0_gnn_in['Wa'], 'L0_gnn_ba': _L0_gnn_in['ba'], 'L0_gnn_gamma': _L0_gnn_in['gamma'], 'L0_gnn_beta': _L0_gnn_in['beta'], 'L1_gnn_W0': _L1_gnn_in['W0'], 'L1_gnn_b0': _L1_gnn_in['b0'], 'L1_gnn_W1': _L1_gnn_in['W1'], 'L1_gnn_b1': _L1_gnn_in['b1'], 'L1_gnn_W2': _L1_gnn_in['W2'], 'L1_gnn_b2': _L1_gnn_in['b2'], 'L1_gnn_gn_weight': _L1_gnn_in['gn_weight'], 'L1_gnn_gn_bias': _L1_gnn_in['gn_bias'], 'L1_gnn_gn_mean_scale': _L1_gnn_in['gn_mean_scale'], 'L1_ffn_w_up': _L1_ffn_in['w_up'], 'L1_ffn_w_down': _L1_ffn_in['w_down'], 'L2_gnn_W': _L2_gnn_in['W'], 'L2_gnn_b': _L2_gnn_in['b'], 'L2_ffn_w_gating': _L2_ffn_in['w_gating'], 'L2_ffn_gamma': _L2_ffn_in['gamma'], 'L2_ffn_w1': _L2_ffn_in['w1'], 'L2_ffn_w2': _L2_ffn_in['w2'], 'L3_gnn_W_self': _L3_gnn_in['W_self'], 'L3_gnn_W_neigh': _L3_gnn_in['W_neigh'], 'L3_gnn_bias': _L3_gnn_in['bias'], 'L3_gnn_gamma': _L3_gnn_in['gamma'], 'L3_gnn_beta': _L3_gnn_in['beta'], 'L3_ffn_gate_w': _L3_ffn_in['gate_w'], 'L3_ffn_gate_b': _L3_ffn_in['gate_b'], 'L3_ffn_w1': _L3_ffn_in['w1'], 'L3_ffn_w3': _L3_ffn_in['w3'], 'L3_ffn_w2': _L3_ffn_in['w2']}

def reference(x, src, dst, L0_gnn_Wv, L0_gnn_bv, L0_gnn_Ww, L0_gnn_bw, L0_gnn_Wa, L0_gnn_ba, L0_gnn_gamma, L0_gnn_beta, L1_gnn_W0, L1_gnn_b0, L1_gnn_W1, L1_gnn_b1, L1_gnn_W2, L1_gnn_b2, L1_gnn_gn_weight, L1_gnn_gn_bias, L1_gnn_gn_mean_scale, L1_ffn_w_up, L1_ffn_w_down, L2_gnn_W, L2_gnn_b, L2_ffn_w_gating, L2_ffn_gamma, L2_ffn_w1, L2_ffn_w2, L3_gnn_W_self, L3_gnn_W_neigh, L3_gnn_bias, L3_gnn_gamma, L3_gnn_beta, L3_ffn_gate_w, L3_ffn_gate_b, L3_ffn_w1, L3_ffn_w3, L3_ffn_w2):
    import jax
    import jax.numpy as jnp

    def _L0_gnn_ref(x, edges, Wv, bv, Ww, bw, Wa, ba, gamma, beta):
        import jax, jax.numpy as jnp
        import numpy as np
        N = 384
        HID = 512
        H = 8
        HD = HID // H
        E = 12288
        LN_EPS = 1e-05
        residual = x
        n = x.shape[0]
        out = (x @ Wv + bv).reshape(n, H, HD).transpose(1, 0, 2)
        x1 = x[edges[0]]
        x2 = x[edges[1]]
        e = jnp.concatenate([x1, x2], axis=1) @ Ww + bw
        e = e.reshape(-1, H, 2 * HD).transpose(1, 0, 2)
        e = jax.nn.leaky_relu(e, 0.01)
        w = (e @ Wa + ba)[..., 0]
        mat = jnp.full((H, n, n), -jnp.inf, jnp.float32)
        mat = mat.at[:, edges[0], edges[1]].set(w)
        mat = jax.nn.softmax(mat, axis=-1)
        mat = jnp.nan_to_num(mat)
        y = jnp.matmul(mat, out).transpose(1, 0, 2)
        y = jax.nn.elu(y).reshape(n, HID) + residual
        mu = jnp.mean(y, axis=-1, keepdims=True)
        var = jnp.var(y, axis=-1, keepdims=True)
        y = (y - mu) / jnp.sqrt(var + LN_EPS) * gamma + beta
        return y

    def _L0_ffn_ref(x_bd):
        import jax, jax.numpy as jnp
        import numpy as np
        MARK_AX = 0
        OPCODE_BASE = 16
        OP_SHL = OPCODE_BASE + 23
        OP_SHR = OPCODE_BASE + 24
        ALU_LO = 64
        ALU_HI = 80
        AX_CARRY_LO = 96
        OUTPUT_LO = 128
        OUTPUT_HI = 144
        B, SEQ, D = (8, 4096, 512)
        hot = x_bd > 0.5
        first16 = lambda off: jnp.argmax(hot[..., off:off + 16], axis=-1).astype(jnp.int32)
        lo = first16(ALU_LO)
        hi = first16(ALU_HI)
        sa = first16(AX_CARRY_LO)
        val = lo + 16 * hi
        shl = jnp.left_shift(val, sa) & 255
        shr = jnp.right_shift(val, sa)
        mark = hot[..., MARK_AX]
        is_shl = hot[..., OP_SHL]
        is_shr = jnp.logical_and(hot[..., OP_SHR], jnp.logical_not(is_shl))
        act_shl = jnp.logical_and(mark, is_shl)
        act_shr = jnp.logical_and(mark, is_shr)
        active = jnp.logical_or(act_shl, act_shr)
        res = jnp.where(act_shl, shl, jnp.where(act_shr, shr, 0))
        res = jnp.clip(res, 0, 255)
        rlo = res & 15
        rhi = res >> 4
        amp = 2.0 * active.astype(x_bd.dtype)
        add_lo = amp[..., None] * jax.nn.one_hot(rlo, 16, dtype=x_bd.dtype)
        add_hi = amp[..., None] * jax.nn.one_hot(rhi, 16, dtype=x_bd.dtype)
        out = x_bd.at[..., OUTPUT_LO:OUTPUT_LO + 16].add(add_lo)
        out = out.at[..., OUTPUT_HI:OUTPUT_HI + 16].add(add_hi)
        return out

    def _L1_gnn_ref(x, edge_index, W0, b0, W1, b1, W2, b2, gn_weight, gn_bias, gn_mean_scale):
        import jax, jax.numpy as jnp
        import numpy as np
        EPS = 1e-05

        def gcn_conv(x, src, dst, W, b):
            n = x.shape[0]
            xw = x @ W
            deg = jax.ops.segment_sum(jnp.ones(src.shape[0], x.dtype), dst, num_segments=n) + 1.0
            dinv = jax.lax.rsqrt(deg)
            coef = (dinv[src] * dinv[dst])[:, None]
            agg = jax.ops.segment_sum(xw[src] * coef, dst, num_segments=n)
            agg = agg + xw * (dinv * dinv)[:, None]
            return agg + b

        def graph_norm(x, weight, bias, mean_scale):
            mean = x.mean(axis=0, keepdims=True)
            out = x - mean * mean_scale
            var = (out * out).mean(axis=0, keepdims=True)
            return weight * out * jax.lax.rsqrt(var + EPS) + bias
        src, dst = (edge_index[0], edge_index[1])
        h = x
        for W, b in ((W0, b0), (W1, b1), (W2, b2)):
            h = gcn_conv(h, src, dst, W, b)
            h = jax.nn.relu(h)
            h = graph_norm(h, gn_weight, gn_bias, gn_mean_scale)
        return h

    def _L1_ffn_ref(x, w_up, w_down):
        import jax, jax.numpy as jnp
        import numpy as np
        EPS = 1e-05

        def _bitlinear(x, w):
            w_scale = jnp.clip(jnp.mean(jnp.abs(w)), EPS, None)
            w_q = jnp.clip(jnp.round(w / w_scale), -1.0, 1.0) * w_scale
            w_eff = w + jax.lax.stop_gradient(w_q - w)
            x_scale = 127.0 / jnp.clip(jnp.max(jnp.abs(x), axis=-1, keepdims=True), EPS, None)
            x_q = jnp.clip(jnp.round(x * x_scale), -128.0, 127.0) / x_scale
            x_eff = x + jax.lax.stop_gradient(x_q - x)
            return jnp.einsum('bsi,oi->bso', x_eff, w_eff)

        def _ste_round_clamp_int8(h):
            h_q = jnp.clip(jnp.round(h), -128.0, 127.0)
            return h + jax.lax.stop_gradient(h_q - h)
        h = _bitlinear(x, w_up)
        h = jax.nn.relu(h)
        h = _ste_round_clamp_int8(h)
        return _bitlinear(h, w_down)

    def _L2_gnn_ref(x, edge_index, W, b):
        import jax, jax.numpy as jnp
        import numpy as np
        N_NODES = 6250
        N_EDGES = 50000
        IN_DIM = 512
        OUT_DIM = 512
        n = x.shape[0]
        loops = jnp.arange(n, dtype=edge_index.dtype)
        row = jnp.concatenate([edge_index[0], loops])
        col = jnp.concatenate([edge_index[1], loops])
        deg = jax.ops.segment_sum(jnp.ones(row.shape[0], dtype=x.dtype), row, num_segments=n)
        dis = jax.lax.rsqrt(deg)
        norm = dis[row] * dis[col]
        h = x @ W.T + b
        out = jax.ops.segment_sum(norm[:, None] * h[row], col, num_segments=n)
        return jax.nn.relu(out)

    def _L2_ffn_ref(x, w_gating, gamma, w1, w2):
        import jax, jax.numpy as jnp
        import numpy as np
        EPS = 1e-09
        LN_EPS = 1e-05

        def _layernorm(x, gamma):
            x = x.astype(jnp.float32)
            mu = jnp.mean(x, axis=-1, keepdims=True)
            var = jnp.var(x, axis=-1, keepdims=True)
            return (x - mu) * jax.lax.rsqrt(var + LN_EPS) * gamma
        b, n, d = x.shape
        E = w_gating.shape[-1]
        C = max(min(n, int(n * 6.0 / E)), 4)
        raw = jnp.einsum('bnd,de->bne', x, w_gating)
        probs = jax.nn.softmax(raw, axis=-1)
        gate1 = jnp.max(probs, axis=-1)
        idx1 = jnp.argmax(probs, axis=-1)
        mask1 = jax.nn.one_hot(idx1, E, dtype=jnp.float32)
        gates_wo1 = probs * (1.0 - mask1)
        gate2 = jnp.max(gates_wo1, axis=-1)
        denom = gate1 + gate2 + EPS
        gate1 = gate1 / denom
        pos1 = (jnp.cumsum(mask1, axis=-2) - mask1) * mask1
        mask1 = mask1 * (pos1 < float(C)).astype(jnp.float32)
        mask1_flat = jnp.sum(mask1, axis=-1)
        pos1_flat = jnp.sum(pos1, axis=-1).astype(jnp.int32)
        gate1 = gate1 * mask1_flat
        combine = gate1[..., None, None] * mask1_flat[..., None, None] * jax.nn.one_hot(idx1, E, dtype=jnp.float32)[..., None] * jax.nn.one_hot(pos1_flat, C, dtype=jnp.float32)[..., None, :]
        dispatch = (combine != 0).astype(jnp.float32)
        expert_in = jnp.einsum('bnd,bnec->ebcd', x, dispatch)
        xn = _layernorm(expert_in, gamma)
        hidden = jax.nn.gelu(jnp.einsum('ebcd,edh->ebch', xn, w1), approximate=False)
        expert_out = jnp.einsum('ebch,ehd->ebcd', hidden, w2)
        out = jnp.einsum('ebcd,bnec->bnd', expert_out, combine)
        return out

    def _L3_gnn_ref(x, edge_src, edge_dst, deg, W_self, W_neigh, bias, gamma, beta):
        import jax, jax.numpy as jnp
        import numpy as np
        N_NODES = 1250
        N_EDGES = 20000
        IN_DIM = 512
        OUT_DIM = 512
        LN_EPS = 1e-05
        n = x.shape[0]
        h_self = jnp.einsum('nd,od->no', x, W_self)
        neigh_sum = jax.ops.segment_sum(x[edge_src], edge_dst, num_segments=n)
        neigh_mean = neigh_sum / jnp.maximum(deg, 1.0)[:, None]
        h_neigh = jnp.einsum('nd,od->no', neigh_mean, W_neigh)
        h = h_self + h_neigh + bias
        mu = jnp.mean(h, axis=-1, keepdims=True)
        var = jnp.mean(jnp.square(h - mu), axis=-1, keepdims=True)
        h = (h - mu) * jax.lax.rsqrt(var + LN_EPS)
        return h * gamma + beta

    def _L3_ffn_ref(x, gate_w, gate_b, w1, w3, w2):
        import jax, jax.numpy as jnp
        import numpy as np
        DIM = 512
        MOE_DIM = 256
        E = 64
        G = 8
        TOPK_G = 4
        K = 8
        SCALE = 2.5
        CAP = 1024

        def _gate(x2, gate_w, gate_b):
            T = x2.shape[0]
            scores = jax.nn.sigmoid(x2 @ gate_w.T)
            s = (scores + gate_b).reshape(T, G, E // G)
            group_scores = jax.lax.top_k(s, 2)[0].sum(-1)
            top_groups = jax.lax.top_k(group_scores, TOPK_G)[1]
            gmask = jnp.zeros((T, G), bool).at[jnp.arange(T)[:, None], top_groups].set(True)
            s = jnp.where(gmask[..., None], s, -jnp.inf).reshape(T, E)
            idx = jax.lax.top_k(s, K)[1]
            w = jnp.take_along_axis(scores, idx, axis=1)
            w = w / w.sum(-1, keepdims=True) * SCALE
            return (w, idx)

        def _moe_forward(x, gate_w, gate_b, w1, w3, w2):
            shape = x.shape
            x2 = x.reshape(-1, DIM)
            T = x2.shape[0]
            w, idx = _gate(x2, gate_w, gate_b)
            flat_e = idx.reshape(-1)
            oh = (flat_e[:, None] == jnp.arange(E)[None, :]).astype(jnp.int32)
            pos = (jnp.cumsum(oh, axis=0) * oh).sum(-1) - 1
            x_rep = jnp.repeat(x2, K, axis=0)
            xb = jnp.zeros((E, CAP, DIM), x2.dtype).at[flat_e, pos].set(x_rep, mode='drop')
            h = jax.nn.silu(jnp.einsum('ecd,edm->ecm', xb, w1)) * jnp.einsum('ecd,edm->ecm', xb, w3)
            yb = jnp.einsum('ecm,emd->ecd', h, w2)
            y = yb.at[flat_e, pos].get(mode='fill', fill_value=0.0) * w.reshape(-1)[:, None]
            return y.reshape(T, K, DIM).sum(1).reshape(shape)
        return _moe_forward(x, gate_w, gate_b, w1, w3, w2)
    edge_index = jnp.stack([src, dst])
    deg = jnp.maximum(jax.ops.segment_sum(jnp.ones(dst.shape, jnp.float32), dst, num_segments=384), 1.0)
    x = x + _L0_gnn_ref(_layernorm(x, axis=-1), edge_index, L0_gnn_Wv, L0_gnn_bv, L0_gnn_Ww, L0_gnn_bw, L0_gnn_Wa, L0_gnn_ba, L0_gnn_gamma, L0_gnn_beta)
    x = x + _L0_ffn_ref(_layernorm(x, axis=-1)[None])[0]
    x = x + _L1_gnn_ref(_layernorm(x, axis=-1), edge_index, L1_gnn_W0, L1_gnn_b0, L1_gnn_W1, L1_gnn_b1, L1_gnn_W2, L1_gnn_b2, L1_gnn_gn_weight, L1_gnn_gn_bias, L1_gnn_gn_mean_scale)
    x = x + _L1_ffn_ref(_layernorm(x, axis=-1)[None], L1_ffn_w_up, L1_ffn_w_down)[0]
    x = x + _L2_gnn_ref(_layernorm(x, axis=-1), edge_index, L2_gnn_W, L2_gnn_b)
    x = x + _L2_ffn_ref(_layernorm(x, axis=-1)[None], L2_ffn_w_gating, L2_ffn_gamma, L2_ffn_w1, L2_ffn_w2)[0]
    x = x + _L3_gnn_ref(_layernorm(x, axis=-1), src, dst, deg, L3_gnn_W_self, L3_gnn_W_neigh, L3_gnn_bias, L3_gnn_gamma, L3_gnn_beta)
    x = x + _L3_ffn_ref(_layernorm(x, axis=-1)[None], L3_ffn_gate_w, L3_ffn_gate_b, L3_ffn_w1, L3_ffn_w3, L3_ffn_w2)[0]
    return x

_drawn_inputs = setup_inputs


def setup_inputs(seed=0):
    import zlib

    import numpy as np

    out = dict(_drawn_inputs(seed))
    spreads = {'L0_gnn_gamma': (1.0, 0.2),
     'L0_gnn_beta': (0.0, 0.1),
     'L1_gnn_gn_weight': (1.0, 0.2),
     'L1_gnn_gn_bias': (0.0, 0.1),
     'L1_gnn_gn_mean_scale': (1.0, 0.2),
     'L2_ffn_gamma': (1.0, 0.6),
     'L3_gnn_bias': (0.0, 0.1),
     'L3_gnn_gamma': (1.0, 0.2),
     'L3_gnn_beta': (0.0, 0.1)}
    factors = {'L0_gnn_Ww': 2.833,
     'L0_gnn_bw': 27.733,
     'L0_gnn_Wa': 3.036,
     'L1_gnn_b2': 2.844,
     'L2_gnn_b': 6.722}
    for name, (base, spread) in spreads.items():
        noise = np.random.default_rng([zlib.crc32(name.encode()), seed]).standard_normal(out[name].shape)
        drawn = base * np.exp(spread * noise) if base else spread * noise
        out[name] = jnp.asarray(drawn.astype(out[name].dtype))
    for name, factor in factors.items():
        out[name] = (out[name] * factor).astype(out[name].dtype)
    return out
```

```python
from contextlib import ExitStack

import concourse.bass as bass
from concourse import mybir

N = 384
D = 512
E = 6144
P = 128
NT = N // P
KD = D // P
ET = E // P
H = 8
HD = D // H
HW = 2 * HD
F1 = 256
E2, F2 = 6, 256
E3, F3 = 64, 256
G3, TOPG, K3 = 8, 4, 8
ROUTED_SCALE = 2.5
LN_EPS = 1e-5
EPS = 1e-5
NEG = -3.0e38
NEG_FLOOR = -1.0e37
ROUND = 1.5 * 2.0 ** 23
SLOPE = 0.01
ROW = 2 * D + H
NGA = 4
NWB = 5
NXG = 3

f32 = mybir.dt.float32
bf16 = mybir.dt.bfloat16
f16 = mybir.dt.float16
i32 = mybir.dt.int32
u32 = mybir.dt.uint32
NORMS = ("1", "3", "5", "6", "6b", "7", "8")


def nth(norm, tiles):
    return NT * NORMS.index(norm) + tiles


ALU = mybir.AluOpType
ACT = mybir.ActivationFunctionType
AX = mybir.AxisListType.X


def build(nc, a, out):
    ctx = ExitStack()
    with ctx:
        def sb(name, cols, dt=f32):
            return ctx.enter_context(nc.sbuf_tensor(name, [P, cols], dt))

        sems = {}

        def S(name):
            if name not in sems:
                sems[name] = ctx.enter_context(nc.semaphore(name))
            return sems[name]

        tab_src = nc.dram_tensor("tab_src", (N, ROW), f32, kind="Internal").ap()
        tab_dst = nc.dram_tensor("tab_dst", (N, ROW), f32, kind="Internal").ap()
        score = nc.dram_tensor("score", (N * N, H), f32, kind="Internal").ap()
        tok_tab = nc.dram_tensor("tok_tab", (N, D), f32, kind="Internal").ap()
        slot_tab = nc.dram_tensor("slot_tab", (N * E3, 4), i32, kind="Internal").ap()
        pick_out = nc.dram_tensor("pick_out", (N * K3, D), f32, kind="Internal").ap()

        R1 = sb("R1", 18432)
        R2 = sb("R2", 18688)
        WK = R1[:, 15360:18432]
        x_s = sb("x_s", NT * D)
        xn_s = sb("xn_s", NT * D)
        xT_s = sb("xT_s", KD * N)
        cnt_s = sb("cnt_s", NT * N)
        cntI_s = sb("cntI_s", NT * N)
        rows = sb("rows", 4 * D)
        cols = sb("cols", 28)
        gateb = sb("gateb", E3)
        ident = sb("ident", P)
        ident16 = sb("ident16", 2 * P, f16)
        identb = sb("identb", P, bf16)
        ones = sb("ones", P)
        onesb = sb("onesb", P, bf16)
        tri = sb("tri", P)
        trib = sb("trib", P, bf16)
        iota_h = sb("iota_h", N, f16)
        iota64 = sb("iota64", E3)
        fall48 = sb("fall48", 48)
        wq = sb("wq", 2 * KD * F1, bf16)
        dinv_bc = sb("dinv_bc", N)
        rdeg_bc = sb("rdeg_bc", N)
        e_i = sb("e_i", 3 * ET, i32)
        e_f = sb("e_f", 4 * ET)
        e_h = sb("e_h", 2 * ET, f16)
        w_e = sb("w_e", ET * H)
        slot0 = sb("slot0", E3 * 4, i32)
        rest_rec = sb("rest_rec", 4, i32)
        most = sb("most", 1, i32)
        rec = sb("rec", NT * K3 * 4, i32)
        sm = sb("sm", 1024)
        smi = sb("smi", 32, u32)

        x3 = x_s[:, :].rearrange("p (t d) -> p t d", t=NT)
        xn3 = xn_s[:, :].rearrange("p (t d) -> p t d", t=NT)
        xT = xT_s[:, :].rearrange("p (k n) -> p k n", k=KD)
        cnt = cnt_s[:, :].rearrange("p (t n) -> p t n", t=NT)
        cntI = cntI_s[:, :].rearrange("p (t n) -> p t n", t=NT)
        src_i, dst_i, row_i = (e_i[:, j * ET:(j + 1) * ET] for j in range(3))
        src_f, dst_f, key_f, dup_f = (e_f[:, j * ET:(j + 1) * ET] for j in range(4))
        src_h, dst_h = e_h[:, 0:ET], e_h[:, ET:2 * ET]
        w_e3 = w_e[:, :].rearrange("p (t h) -> p t h", h=H)
        rec4 = rec[:, :].rearrange("p (t k c) -> p t k c", t=NT, k=K3)

        def r1(o, n, **kw):
            return R1[:, o:o + n]

        Ww = r1(0, 8192).rearrange("p (c n) -> p c n", c=8)
        Wv = r1(8192, 2048).rearrange("p (k n) -> p k n", k=KD)
        ga = [r1(10240 + ROW * j, ROW) for j in range(NGA)]
        ab = [r1(16320 + ROW * j, ROW) for j in range(2)]
        lsc = r1(14400, 1024)
        mt = [r1(3072 * j, 3072).rearrange("p (n h) -> p n h", h=H) for j in range(NT)]
        probs = [r1(10240 + N * h, N) for h in range(H)]
        probsT = [r1(10240 + 3072 + N * h, N) for h in range(H)]
        w13 = [r1(3072 * j, 2048).rearrange("p (k n) -> p k n", k=KD) for j in range(NWB)]
        w2e = [r1(3072 * j + 2048, 1024).rearrange("p (c n) -> p c n", c=2) for j in range(NWB)]
        ypick = [r1(4096 * j, 4096) for j in range(NT)]
        L1W = R2[:, 0:6144].rearrange("p (l k n) -> p l k n", l=3, k=KD)
        F2W2 = R2[:, 0:6144].rearrange("p (e c n) -> p e c n", e=E2, c=2)
        F2W1 = R2[:, 6144:12288].rearrange("p (e k n) -> p e k n", e=E2, k=KD)
        L2W = R2[:, 12288:14336].rearrange("p (k n) -> p k n", k=KD)
        L3S = R2[:, 14336:16384].rearrange("p (k n) -> p k n", k=KD)
        L3N = R2[:, 16384:18432].rearrange("p (k n) -> p k n", k=KD)
        gateW = R2[:, 18432:18688].rearrange("p (k n) -> p k n", k=KD)
        B0 = 6144
        V = R2[:, B0:B0 + 1536].rearrange("p (t d) -> p t d", t=NT)
        wu = R2[:, B0 + 1536:B0 + 2560]
        wd = R2[:, B0 + 2560:B0 + 3584]
        bvr = R2[:, B0 + 3584:B0 + 4096]
        g0r = R2[:, B0 + 4096:B0 + 4608]
        b0r = R2[:, B0 + 4608:B0 + 5120]
        bwr = R2[:, B0 + 5120:B0 + 6144]
        oh = R2[:, 0:768].bitcast(bf16).rearrange("p (b s n) -> p b s n", b=2, s=2)
        war = R2[:, 768:896]
        bar = R2[:, 896:897]
        y0 = R2[:, 1024:2560].rearrange("p (t d) -> p t d", t=NT)
        ye = R2[:, 2560:4096].rearrange("p (t d) -> p t d", t=NT)
        yr = R2[:, 4096:5632].rearrange("p (t d) -> p t d", t=NT)
        xws = WK[:, 0:1536].rearrange("p (t d) -> p t d", t=NT)
        gT = WK[:, 1536:3072].rearrange("p (k n) -> p k n", k=KD)
        y6 = R2[:, 12288:13824].rearrange("p (t d) -> p t d", t=NT)
        hid = [WK[:, 768 * j:768 * j + 768].rearrange("p (c n) -> p c n", c=2) for j in range(2)]
        xg = [R2[:, D * j:D * j + D] for j in range(NXG)]
        xeT = [R2[:, 2048 + D * j:2048 + D * j + D].rearrange("p (k n) -> p k n", k=KD) for j in range(2)]
        act = [R2[:, 3072 + F3 * j:3072 + F3 * j + F3] for j in range(2)]
        hmid = [R2[:, 3584 + F3 * j:3584 + F3 * j + F3] for j in range(2)]
        hT = [R2[:, 4096 + F3 * j:4096 + F3 * j + F3] for j in range(2)]
        ysb = [R2[:, 4608 + D * j:4608 + D * j + D] for j in range(3)]

        b2r, b3r, g3r, be3r = (rows[:, D * j:D * j + D] for j in range(4))
        bcol = [cols[:, KD * j:KD * j + KD] for j in range(7)]

        xq = WK[:, 0:768].bitcast(bf16).rearrange("p (t d) -> p t d", t=NT)
        xqT = WK[:, 768:1536].bitcast(bf16).rearrange("p (k n) -> p k n", k=KD)
        hb = WK[:, 1536:2304].rearrange("p (t f) -> p t f", t=NT)
        hq = WK[:, 2304:2688].bitcast(bf16).rearrange("p (t f) -> p t f", t=NT)
        hqT = WK[:, 2688:3072].bitcast(bf16).rearrange("p (c n) -> p c n", c=2)
        hr, hd = (xT_s[:, 768 * j:768 * j + 768].rearrange("p (t f) -> p t f", t=NT) for j in range(2))
        wuq = wq[:, 0:1024].rearrange("p (k n) -> p k n", k=KD)
        wdq = wq[:, 1024:2048].rearrange("p (c n) -> p c n", c=2)
        wg_s = sb("wg_s", KD * E2)
        wg = wg_s[:, :].rearrange("p (k n) -> p k n", k=KD)
        tri8 = sb("tri8", G3 * G3)
        te = "p (t e) -> p t e"
        scores8, biased, masked, replaced, selw, place = (
            WK[:, o:o + NT * E3].rearrange(te, t=NT) for o in (0, 192, 704, 896, 1088, 1280))
        top_in_group = WK[:, 384:576].rearrange("p (g m) -> p g m", m=8)
        beats, ties = WK[:, 576:640], WK[:, 640:704]
        scr64 = WK[:, 1472:1536]
        picked = WK[:, 1536:1632].bitcast(bf16).rearrange(te, t=NT)
        pick_row_f = WK[:, 1632:1656]
        pick_row = WK[:, 1664:1688].bitcast(i32)
        pb = [ctx.enter_context(nc.psum_tensor(f"bank{j}", [P, 512], f32)) for j in range(8)]

        pbh = [b[:, :].bitcast(bf16) for b in pb]
        sq_scr = pb[7][:, 0:N]

        small = {}
        used = [0]

        def V_(name, n):
            if name not in small:
                small[name] = sm[:, used[0]:used[0] + n]
                used[0] += n
                assert used[0] <= 1024
            return small[name]

        xin, srcd, dstd = a["x"], a["src"], a["dst"]
        tiles = "(t p) d -> p t d"
        chunks = "(k p) n -> p k n"
        def rest(eng, one_expert, after=None):
            eng.wait_ge(S("most_ready"), 1)
            fullest = eng.value_load(most[0:1, 0:1], min_val=0, max_val=N)
            with eng.If(fullest > P):
                for s in range(1, NT):
                    with eng.Fori(0, E3) as e:
                        one_expert(eng, s, e, e + (E3 * (s - 1) + 1))
                if after is not None:
                    after()

        block = ctx.enter_context(nc.Block())

        @block.sync
        def _(sp):
            sp.dma_start(x3, xin.rearrange(tiles, p=P)).then_inc(S("x_loaded"), 16)
            sp.dma_start(src_i, srcd.rearrange("(p t) -> p t", p=P)).then_inc(S("edges_loaded"), 16)
            sp.dma_start(dst_i, dstd.rearrange("(p t) -> p t", p=P)).then_inc(S("edges_loaded"), 16)
            ww = a["L0_Ww"].rearrange("(c p) n -> p c n", p=P)
            sp.dma_start(Ww[:, 0:4, :], ww[:, 0:4, :]).then_inc(S("Ww_loaded_src"), 16)
            sp.dma_start(Ww[:, 4:8, :], ww[:, 4:8, :]).then_inc(S("Ww_loaded_dst"), 16)
            for row, name in ((bwr, "L0_bw"), (bvr, "L0_bv"), (g0r, "L0_gamma"), (b0r, "L0_beta"),
                              (war, "L0_Wa"), (bar, "L0_ba")):
                sp.dma_start(row, a[name].partition_broadcast(P)).then_inc(S("rows0_loaded"), 16)
            sp.dma_start(Wv, a["L0_Wv"].rearrange(chunks, p=P)).then_inc(S("Wv_loaded"), 16)
            sp.dma_start(wu.rearrange("p (k n) -> p k n", k=KD), a["L1_wu"].rearrange(chunks, p=P)).then_inc(S("bit_w_loaded"), 16)
            sp.dma_start(wd.rearrange("p (k n) -> p k n", k=2), a["L1_wd"].rearrange(chunks, p=P)).then_inc(S("bit_w_loaded"), 16)
            sp.wait_ge(S("no_edge_ready"), 1)
            fill = score.rearrange("n h -> (n h)").rearrange("(q p c) -> q p c", p=P, c=1024)
            for q in range(9):
                sp.dma_start(fill[q], ga[0][:, 0:1024]).then_inc(S("score_filled"), 16)
            sp.wait_ge(S("no_token_ready"), 4)
            slots = slot_tab.rearrange("(s p e) c -> s p (e c)", s=NT, p=P)
            for q in range(NT):
                sp.dma_start(slots[q], slot0[:, :]).then_inc(S("slots_filled"), 16)
            for t in range(NT):
                sp.wait_ge(S("src_rows_ready"), t + 1)
                sp.dma_start(tab_src[P * t:P * t + P, :], ab[0]).then_inc(S("src_rows_stored"), 16)
                sp.wait_ge(S("dst_rows_ready"), t + 1)
                sp.dma_start(tab_dst[P * t:P * t + P, :], ab[1]).then_inc(S("dst_rows_stored"), 16)
            for j, name in enumerate(("L2_b", "L3_bias", "L3_gamma", "L3_beta")):
                sp.dma_start(rows[:, D * j:D * j + D], a[name].partition_broadcast(P)).then_inc(S("rows_loaded"), 16)
            sp.dma_start(gateb[:, :], a["L3_gate_b"].partition_broadcast(P)).then_inc(S("rows_loaded"), 16)
            sp.dma_start(wg, a["L2_w_gating"].rearrange(chunks, p=P)).then_inc(S("wg_loaded"), 16)
            sp.dma_start(cols[:, :], a["fcols"]).then_inc(S("rows_loaded"), 16)
            sp.dma_start(L2W, a["L2_W"].rearrange(chunks, p=P)).then_inc(S("L2W_loaded"), 16)
            sp.dma_start(L3S, a["L3_self"].rearrange(chunks, p=P)).then_inc(S("L3W_loaded"), 16)
            sp.dma_start(L3N, a["L3_neigh"].rearrange(chunks, p=P)).then_inc(S("L3W_loaded"), 16)
            sp.dma_start(gateW, a["L3_gate_w"].rearrange(chunks, p=P)).then_inc(S("gateW_loaded"), 16)
            sp.wait_ge(S("V_ready"), NT)
            sp.wait_ge(S("scores_stored"), 16 * ET)
            for i in range(NT):
                sp.dma_start(mt[i], score[N * P * i:N * P * (i + 1), :].rearrange("(p n) h -> p n h", p=P)).then_inc(S(f"scores_loaded{i}"), 16)
            sp.wait_ge(S("x_ready"), NT * 0 + NT)
            for l in range(3):
                sp.dma_start(L1W[:, l], a[f"L1_W{l}"].rearrange(chunks, p=P)).then_inc(S(f"L1W{l}_loaded"), 16)
            sp.dma_start(F2W1, a["L2_w1"].rearrange("e (k p) n -> p e k n", p=P)).then_inc(S("F2W1_loaded"), 16)

            def load_expert(e):
                j = e % NWB
                for c, name in enumerate(("L3_w1", "L3_w3")):
                    sp.dma_start(w13[j][:, :, F3 * c:F3 * c + F3], a[name][e].rearrange(chunks, p=P)).then_inc(S(f"expert_w{j}"), 16)
                sp.dma_start(w2e[j], a["L3_w2"][e].rearrange("(c p) n -> p c n", p=P)).then_inc(S(f"expert_w{j}"), 16)

            for e in range(NWB):
                load_expert(e)
            sp.wait_ge(S("h_out_psum"), NT)
            sp.dma_start(F2W2, a["L2_w2"].rearrange("e (c p) n -> p e c n", p=P)).then_inc(S("F2W2_loaded"), 16)
            for t in range(NT):
                sp.wait_ge(S("xn_ready"), nth("8", t + 1))
                sp.dma_start(tok_tab[P * t:P * t + P, :], xn3[:, t]).then_inc(S("tokens_stored"), 16)
            sp.wait_ge(S("slots_written"), 16 * NT * K3)
            sp.dma_start(slot0[:, :], slots[0]).then_inc(S("slot0_loaded"), 16)
            for e in range(NWB, E3):
                sp.wait_ge(S("y_psum"), e - NWB + 1)
                load_expert(e)
            sp.wait_ge(S("y_psum"), E3)

            def load_rest(sp, s, e, nth_):
                sp.wait_ge(S("rest_turn"), nth_)
                sp.dma_start(rest_rec[:, :], slot_tab.rearrange("(s p e) c -> s p e c", s=NT, p=P)[s, :, bass.ds(e, 1), :]).then_inc(S("rest_loaded"), 16)
                for c, name in enumerate(("L3_w1", "L3_w3")):
                    sp.dma_start(w13[0][:, :, F3 * c:F3 * c + F3], a[name][bass.ds(e, 1)].rearrange("e (k p) n -> p (e k) n", p=P)).then_inc(S("rest_loaded"), 16)
                sp.dma_start(w2e[0], a["L3_w2"][bass.ds(e, 1)].rearrange("e (c p) n -> p (e c) n", p=P)).then_inc(S("rest_loaded"), 16)

            rest(sp, load_rest, lambda: sp.wait_ge(S("rest_turn"), E3 * (NT - 1) + 1))
            for j in range(3):
                sp.wait_ge(S(f"picks_stored{j}"), 16 * len(range(j, E3, 3)))
            sp.wait_ge(S("y_psum"), E3)
            for t in range(NT):
                sp.dma_start(ypick[t], pick_out[P * K3 * t:P * K3 * (t + 1), :].rearrange("(p k) d -> p (k d)", k=K3)).then_inc(S(f"picks_loaded{t}"), 16)
            for t in range(NT):
                sp.wait_ge(S("x_ready"), NT * 7 + t + 1)
                sp.dma_start(out[P * t:P * t + P, :], x3[:, t]).then_inc(S("out_stored"), 16)
            sp.wait_ge(S("out_stored"), 16 * NT)

        @block.gpsimd
        def _(pool):
            done = [0]

            def step(ins):
                done[0] += 1
                ins.then_inc(S("pool_step"), 1)
                pool.wait_ge(S("pool_step"), done[0])

            imprecise = dict(allow_small_or_imprecise_dtypes=True)
            pool.memset(ga[0], NEG).then_inc(S("no_edge_ready"), 1)
            step(pool.memset(ident[:, :], 0.0))
            step(pool.affine_select(out=ident[:, :], in_=ident[:, :], compare_op=ALU.not_equal, fill=1.0, base=0,
                                    pattern=[[-1, P]], channel_multiplier=1))
            step(pool.memset(ones[:, :], 1.0))
            step(pool.affine_select(out=tri[:, :], in_=ones[:, :], compare_op=ALU.is_gt, fill=0.0, base=0,
                                    pattern=[[-1, P]], channel_multiplier=1))
            step(pool.affine_select(out=trib[:, :], in_=ones[:, :], compare_op=ALU.is_gt, fill=0.0, base=0,
                                    pattern=[[1, P]], channel_multiplier=-1))
            step(pool.tensor_copy(identb[:, :], ident[:, :]))
            step(pool.tensor_copy(onesb[:, :], ones[:, :]))
            step(pool.iota(iota_h[:, :], pattern=[[1, N]], base=0, channel_multiplier=0, **imprecise))
            step(pool.iota(iota64[:, :], pattern=[[1, E3]], base=0, channel_multiplier=0, **imprecise))
            step(pool.iota(fall48[:, :], pattern=[[0, 3], [-1, 16]], base=16, channel_multiplier=0, **imprecise))
            step(pool.memset(tri8[:, :], 1.0))
            t8 = tri8[:, :].rearrange("p (g m) -> p g m", g=G3)
            step(pool.affine_select(out=t8, in_=t8, compare_op=ALU.is_gt, fill=0.0, base=0,
                                    pattern=[[1, G3], [-1, G3]], channel_multiplier=0))
            s4 = slot0[:, :].rearrange("p (e c) -> p e c", c=4)
            for c, value in enumerate((N, N * K3, 0, 0)):
                pool.memset(s4[:, :, c], value).then_inc(S("no_token_ready"), 1)
            step(pool.memset(rec[:, :], 0))
            step(pool.memset(V_("zero", 1), 0.0))
            step(pool.iota(rec4[:, :, :, 0], pattern=[[P, NT], [0, K3]], base=0, channel_multiplier=1))
            pool.iota(rec4[:, :, :, 1], pattern=[[P * K3, NT], [1, K3]], base=0, channel_multiplier=K3).then_inc(S("consts_ready"), 1)

            pool.wait_ge(S("edge_idx_ready"), 1)
            pool.wait_ge(S("score_filled"), 16 * 9)
            pool.wait_ge(S("src_rows_stored"), 16 * NT)

            def gather_src(t):
                j = t % NGA
                if t >= NGA:
                    pool.wait_ge(S("edge_sum_used"), t - NGA + 1)
                pool.indirect_dma_start(out=ga[j], out_offset=None, in_=tab_src[:, :],
                                        in_offset=bass.IndirectOffsetOnAxis(ap=src_i[:, t:t + 1], axis=0)).then_inc(S(f"src_gathered{j}"), 16)

            def add_dst(t):
                j = t % NGA
                pool.wait_ge(S(f"src_gathered{j}"), 16 * (t // NGA + 1))
                pool.indirect_dma_start(out=ga[j], out_offset=None, in_=tab_dst[:, :],
                                        in_offset=bass.IndirectOffsetOnAxis(ap=dst_i[:, t:t + 1], axis=0),
                                        compute_op=ALU.add).then_inc(S(f"dst_added{j}"), 16)

            def scatter_score(t):
                pool.wait_ge(S("w_ready"), t + 1)
                if t:
                    pool.wait_ge(S("scores_stored"), 16 * t)
                pool.indirect_dma_start(out=score[:, :], out_offset=bass.IndirectOffsetOnAxis(ap=row_i[:, t:t + 1], axis=0),
                                        in_=w_e3[:, t, :], in_offset=None, bounds_check=N * N - 1,
                                        oob_is_err=False).then_inc(S("scores_stored"), 16)

            gather_src(0)
            gather_src(1)
            pool.wait_ge(S("dst_rows_stored"), 16 * NT)
            for t in range(ET):
                if t + 2 < ET:
                    gather_src(t + 2)
                add_dst(t)
                if t >= 3:
                    scatter_score(t - 3)
            for t in range(ET - 3, ET):
                scatter_score(t)
            pool.wait_ge(S("x6_done"), 1)
            for j in range(NXG):
                pool.memset(xg[j], 0.0).then_inc(S("xg_cleared"), 1)
            pool.wait_ge(S("slots_filled"), 16 * NT)
            pool.wait_ge(S("picks_ready"), 1)
            for t in range(NT):
                for k in range(K3):
                    c = t * K3 + k
                    pool.indirect_dma_start(out=slot_tab[:, :], out_offset=bass.IndirectOffsetOnAxis(ap=pick_row[:, c:c + 1], axis=0),
                                            in_=rec4[:, t, k, :], in_offset=None).then_inc(S("slots_written"), 16)
            pool.wait_ge(S("slot0_loaded"), 16)
            pool.wait_ge(S("tokens_stored"), 16 * NT)
            pool.wait_ge(S("xg_cleared"), NXG)

            def gather_tokens(e):
                j = e % NXG
                if e >= NXG:
                    pool.wait_ge(S("xe_psum"), e - NXG + 1)
                pool.indirect_dma_start(out=xg[j], out_offset=None, in_=tok_tab[:, :],
                                        in_offset=bass.IndirectOffsetOnAxis(ap=s4[:, e, 0:1], axis=0),
                                        bounds_check=N - 1, oob_is_err=False).then_inc(S(f"tokens_gathered{j}"), 16)

            def scatter_picks(e):
                j = e % 3
                pool.wait_ge(S("ye_ready"), e + 1)
                pool.indirect_dma_start(out=pick_out[:, :], out_offset=bass.IndirectOffsetOnAxis(ap=s4[:, e, 1:2], axis=0),
                                        in_=ysb[j], in_offset=None, bounds_check=N * K3 - 1,
                                        oob_is_err=False).then_inc(S(f"picks_stored{j}"), 16)

            gather_tokens(0)
            gather_tokens(1)
            for e in range(E3):
                if e + 2 < E3:
                    gather_tokens(e + 2)
                if e >= 1:
                    scatter_picks(e - 1)
            scatter_picks(E3 - 1)

            def hold(j):
                return pool.tensor_tensor(out=V_("held", 3)[:, j:j + 1], in0=V_("zero", 1), in1=V_("zero", 1), op=ALU.add)

            def move_rest(pool, s, e, nth_):
                pool.wait_ge(S("rest_loaded"), nth_ * 64)
                hold(0)
                pool.indirect_dma_start(out=xg[0], out_offset=None, in_=tok_tab[:, :],
                                        in_offset=bass.IndirectOffsetOnAxis(ap=rest_rec[:, 0:1], axis=0),
                                        bounds_check=N - 1, oob_is_err=False).then_inc(S("rest_gathered"), 16)
                pool.wait_ge(S("rest_weighed"), nth_)
                hold(1)
                pool.indirect_dma_start(out=pick_out[:, :], out_offset=bass.IndirectOffsetOnAxis(ap=rest_rec[:, 1:2], axis=0),
                                        in_=ysb[0], in_offset=None, bounds_check=N * K3 - 1,
                                        oob_is_err=False).then_inc(S("rest_stored"), 16)
                pool.wait_ge(S("rest_stored"), nth_ * 16)
                hold(2).then_inc(S("rest_turn"), 1)

            for j in range(3):
                pool.wait_ge(S(f"picks_stored{j}"), 16 * len(range(j, E3, 3)))
            pool.wait_ge(S("xe_psum"), E3)
            hold(2).then_inc(S("rest_turn"), 1)
            rest(pool, move_rest)


        @block.tensor
        def _(pe):
            def transposes(norm, t, src=xn3):
                pe.wait_ge(S("xn_ready"), nth(norm, t + 1))
                for k in range(KD):
                    last = pe.transpose(pb[t][:, P * k:P * k + P], src[:, t, P * k:P * k + P], ident[:, :])
                return last

            def project(t, bank, lhsT, rhs, cols_=slice(0, 512), chunks_=range(KD)):
                for k in chunks_:
                    last = pe.matmul(pb[bank][:, cols_], lhsT[:, k, P * t:P * t + P], rhs[:, k, :],
                                     start=(k == chunks_[0]), stop=(k == chunks_[-1]))
                return last

            pe.wait_ge(S("consts_ready"), 1)
            for t in range(NT):
                transposes("1", t).then_inc(S("xT_psum"), 1)
            pe.wait_ge(S("edge_h_ready"), 1)
            for t in range(NT):
                for b in range(4):
                    half = b % 2
                    rows_ready = S("src_half_ready") if b < 2 else S("dst_half_ready")
                    if t == 0 and half == 0:
                        pe.wait_ge(S("Ww_loaded_src") if b < 2 else S("Ww_loaded_dst"), 16)
                    if b == 3 and t == 0:
                        pe.wait_ge(S("xT_ready"), nth("1", NT))
                    pe.wait_ge(S("xT_ready"), nth("1", t + 1))
                    if t:
                        pe.wait_ge(rows_ready, 2 * (t - 1) + half + 1)
                    w = Ww[:, 4 * (b // 2):4 * (b // 2) + 4, D * half:D * half + D]
                    project(t, (3, 4, 5, 0)[b], xT, w).then_inc(S("src_rows_psum") if b < 2 else S("dst_rows_psum"), 1)
                    g = 4 * t + b
                    if g >= 2:
                        pe.wait_ge(S("dup_used"), g - 1)
                    for j in range(4):
                        e = 4 * g + j
                        o = pb[6 + g % 2][:, P * j:P * j + P]
                        pe.matmul(o, src_h[:, e:e + 1].to_broadcast([P, P]), ident16[:, 0:P], start=True, stop=False)
                        last = pe.matmul(o, dst_h[:, e:e + 1].to_broadcast([P, P]), ident16[:, P:2 * P], start=False, stop=True)
                    last.then_inc(S("key_psum"), 1)
            pe.wait_ge(S("Wv_loaded"), 16)
            pe.wait_ge(S("src_half_ready"), 2 * NT)
            pe.wait_ge(S("dst_half_ready"), 2 * NT)
            for t in range(NT):
                project(t, 3 + t, xT, Wv).then_inc(S("V_psum"), 1)
            for e in range(ET):
                pe.wait_ge(S("onehot_ready"), e + 1)
                for s in range(NT):
                    last = pe.matmul(pb[s][:, 0:N], oh[:, e % 2, 0, P * s:P * s + P], oh[:, e % 2, 1, :],
                                     start=(e == 0), stop=(e == ET - 1))
                last.then_inc(S("onehot_used"), 1)
            pe.wait_ge(S("cnt_ready"), 1)
            pe.wait_ge(S("dup_used"), 12)
            for t in range(NT):
                for s in range(NT):
                    pe.matmul(pb[6][:, t:t + 1], cnt[:, s, P * t:P * t + P], ones[:, 0:1], start=(s == 0), stop=(s == NT - 1))
            for s in range(NT):
                pe.matmul(pb[7][:, 0:N], ones[:, :], cnt[:, s, :], start=(s == 0), stop=(s == NT - 1))
            pe.wait_ge(S("bit_abs_ready"), 1)
            pe.matmul(pb[6][:, 8:10], ones[:, :], V_("wabs", 2), start=True, stop=True).then_inc(S("deg_psum"), 1)
            pe.wait_ge(S("V_ready"), NT)

            def transpose_probs(u):
                pe.wait_ge(S("probs_ready"), u + 1)
                if u >= 3:
                    pe.wait_ge(S("probsT_ready"), u - 2)
                for c in range(NT):
                    last = pe.transpose(pb[u % 3][:, P * c:P * c + P], probs[u % H][:, P * c:P * c + P], ident[:, :])
                last.then_inc(S("probsT_psum"), 1)

            def attend(u):
                i, h = divmod(u, H)
                pe.wait_ge(S("probsT_ready"), u + 1)
                for c in range(NT):
                    last = pe.matmul(pb[3 + i][:, HD * h:HD * h + HD], probsT[h][:, P * c:P * c + P], V[:, c, HD * h:HD * h + HD],
                                     start=(c == 0), stop=(c == NT - 1))
                last.then_inc(S("attended_psum"), 1)

            transpose_probs(0)
            for u in range(NT * H):
                if u + 1 < NT * H:
                    transpose_probs(u + 1)
                attend(u)

            for t in range(NT):
                transposes("3", t).then_inc(S("xT_psum"), 1)
            for l in range(3):
                pe.wait_ge(S(f"L1W{l}_loaded"), 16)
                for t in range(NT):
                    if l == 0:
                        pe.wait_ge(S("xT_ready"), nth("3", t + 1))
                    for k in range(KD):
                        if l:
                            pe.wait_ge(S("hT_ready"), KD * (l - 1) + k + 1)
                        last = pe.matmul(pb[3 + t][:, :], xT[:, k, P * t:P * t + P], L1W[:, l, k, :], start=(k == 0), stop=(k == KD - 1))
                    last.then_inc(S("hw_psum"), 1)
                pe.wait_ge(S("hw_ready"), NT * (l + 1))
                for k in range(KD):
                    for s in range(NT):
                        last = pe.matmul(pb[(0, 1, 2, 6)[k]][:, 0:N], xws[:, s, P * k:P * k + P], cntI[:, s, :],
                                         start=(s == 0), stop=(s == NT - 1))
                    last.then_inc(S("agg_psum"), 1)
            for t in range(NT):
                pe.wait_ge(S("hT_ready"), 3 * KD)
                for k in range(KD):
                    last = pe.transpose(pb[3 + t][:, P * k:P * k + P], xT[:, k, P * t:P * t + P], ident[:, :])
                last.then_inc(S("h_out_psum"), 1)

            for t in range(NT):
                pe.wait_ge(S("xq_ready"), t + 1)
                for k in range(KD):
                    last = pe.transpose(pbh[t][:, P * k:P * k + P], xq[:, t, P * k:P * k + P], identb[:, :])
                last.then_inc(S("xqT_psum"), 1)
            pe.wait_ge(S("wq_ready"), 1)
            for t in range(NT):
                pe.wait_ge(S("xqT_ready"), t + 1)
                if t == 0:
                    pe.wait_ge(S("x_ready"), NT * 2 + NT)
                for k in range(KD):
                    last = pe.matmul(pb[3 + t][:, 0:F1], xqT[:, k, P * t:P * t + P], wuq[:, k, :], start=(k == 0), stop=(k == KD - 1))
                last.then_inc(S("up_bit_psum"), 1)
            for t in range(NT):
                pe.wait_ge(S("hq_ready"), t + 1)
                for c in range(2):
                    last = pe.transpose(pbh[t][:, P * c:P * c + P], hq[:, t, P * c:P * c + P], identb[:, :])
                last.then_inc(S("hqT_psum"), 1)
            for t in range(NT):
                pe.wait_ge(S("hqT_ready"), t + 1)
                for c in range(2):
                    last = pe.matmul(pb[3 + t][:, :], hqT[:, c, P * t:P * t + P], wdq[:, c, :], start=(c == 0), stop=(c == 1))
                last.then_inc(S("down_bit_psum"), 1)

            for t in range(NT):
                transposes("5", t).then_inc(S("xT_psum"), 1)
            pe.wait_ge(S("L2W_loaded"), 16)
            pe.wait_ge(S("x_ready"), NT * 3 + NT)
            for t in range(NT):
                pe.wait_ge(S("xT_ready"), nth("5", t + 1))
                project(t, 3 + t, xT, L2W).then_inc(S("hw5_psum"), 1)
            pe.wait_ge(S("hw5_ready"), NT)
            for t in range(NT):
                for s in range(NT):
                    last = pe.matmul(pb[t][:, :], cntI[:, s, P * t:P * t + P], xws[:, s, :], start=(s == 0), stop=(s == NT - 1))
                last.then_inc(S("agg5_psum"), 1)

            pe.wait_ge(S("rows_loaded"), 96)
            pe.wait_ge(S("wg_loaded"), 16)
            for t in range(NT):
                if t == 0:
                    pe.wait_ge(S("x_ready"), NT * 4 + NT)
                transposes("6", t).then_inc(S("xT_psum"), 1)
            for t in range(NT):
                pe.wait_ge(S("xT_ready"), nth("6", t + 1))
                for k in range(KD):
                    last = pe.matmul(pb[6][:, 8 * t:8 * t + E2], xT[:, k, P * t:P * t + P], wg[:, k, :], start=(k == 0), stop=(k == KD - 1))
            last.then_inc(S("gate6_psum"), 1)
            for t in range(NT):
                transposes("6b", t, y6).then_inc(S("xT_psum"), 1)
            pe.wait_ge(S("F2W1_loaded"), 16)
            pe.wait_ge(S("xT_ready"), nth("6b", NT))

            def hidden6(e):
                for c in range(2):
                    j = 2 * e + c
                    if j >= 3:
                        pe.wait_ge(S("hid6_ready"), j - 2)
                    for k in range(KD):
                        last = pe.matmul(pb[j % 3][:, 0:N], F2W1[:, e, k, P * c:P * c + P], xT[:, k, :], start=(k == 0), stop=(k == KD - 1))
                    last.then_inc(S("hid6_psum"), 1)

            hidden6(0)
            for e in range(E2):
                if e + 1 < E2:
                    hidden6(e + 1)
                if e == 0:
                    pe.wait_ge(S("F2W2_loaded"), 16)
                pe.wait_ge(S("hid6_ready"), 2 * e + 2)
                for t in range(NT):
                    j = NT * e + t
                    if j >= 4:
                        pe.wait_ge(S("out6_used"), j - 3)
                    for c in range(2):
                        last = pe.matmul(pb[(3, 4, 5, 7)[j % 4]][:, :], hid[e % 2][:, c, P * t:P * t + P], F2W2[:, e, c, :], start=(c == 0), stop=(c == 1))
                    last.then_inc(S("out6_psum"), 1)

            for t in range(NT):
                transposes("7", t).then_inc(S("xT_psum"), 1)
            pe.wait_ge(S("gate_done6"), 1)
            for k in range(KD):
                for s in range(NT):
                    last = pe.matmul(pb[3 + k][:, 0:N], xn3[:, s, P * k:P * k + P], cnt[:, s, :], start=(s == 0), stop=(s == NT - 1))
                last.then_inc(S("neigh_psum"), 1)
            pe.wait_ge(S("L3W_loaded"), 32)
            pe.wait_ge(S("xT_ready"), nth("7", NT))
            for t in range(NT):
                for k in range(KD):
                    pe.matmul(pb[t][:, :], xT[:, k, P * t:P * t + P], L3S[:, k, :], start=(k == 0), stop=False)
                for k in range(KD):
                    pe.wait_ge(S("neighT_ready"), k + 1)
                    last = pe.matmul(pb[t][:, :], gT[:, k, P * t:P * t + P], L3N[:, k, :], start=False, stop=(k == KD - 1))
                last.then_inc(S("sage_psum"), 1)

            for t in range(NT):
                if t == 0:
                    pe.wait_ge(S("sage_used"), NT)
                transposes("8", t).then_inc(S("xT_psum"), 1)
            pe.wait_ge(S("gateW_loaded"), 16)
            for t in range(NT):
                pe.wait_ge(S("xT_ready"), nth("8", t + 1))
                for k in range(KD):
                    last = pe.matmul(pb[3][:, E3 * t:E3 * t + E3], xT[:, k, P * t:P * t + P], gateW[:, k, :], start=(k == 0), stop=(k == KD - 1))
            last.then_inc(S("logits_psum"), 1)
            pe.wait_ge(S("picked_ready"), 1)
            for t in range(NT):
                for s in range(t + 1):
                    last = pe.matmul(pb[4][:, E3 * t:E3 * t + E3], (trib if s == t else onesb)[:, :], picked[:, s, :], start=(s == 0), stop=(s == t))
            for s in range(NT):
                last = pe.matmul(pb[4][:, E3 * NT:E3 * NT + E3], onesb[:, :], picked[:, s, :], start=(s == 0), stop=(s == NT - 1))
            last.then_inc(S("place_psum"), 1)
            pe.wait_ge(S("picks_ready"), 1)

            def transpose_tokens(e):
                pe.wait_ge(S(f"tokens_gathered{e % NXG}"), 16 * (e // NXG + 1))
                if e >= 2:
                    pe.wait_ge(S("xeT_ready"), e - 1)
                for k in range(KD):
                    last = pe.transpose(pb[e % 2][:, P * k:P * k + P], xg[e % NXG][:, P * k:P * k + P], ident[:, :])
                last.then_inc(S("xe_psum"), 1)

            def up(e):
                pe.wait_ge(S(f"expert_w{e % NWB}"), 48 * (e // NWB + 1))
                pe.wait_ge(S("xeT_ready"), e + 1)
                if e >= 2:
                    pe.wait_ge(S("hmid_ready"), e - 1)
                for k in range(KD):
                    last = pe.matmul(pb[2 + e % 2][:, :], xeT[e % 2][:, k, :], w13[e % NWB][:, k, :], start=(k == 0), stop=(k == KD - 1))
                last.then_inc(S("up_psum"), 1)

            def transpose_hidden(e):
                pe.wait_ge(S("hmid_ready"), e + 1)
                if e >= 2:
                    pe.wait_ge(S("hT8_ready"), e - 1)
                for c in range(2):
                    last = pe.transpose(pb[4 + e % 2][:, P * c:P * c + P], hmid[e % 2][:, P * c:P * c + P], ident[:, :])
                last.then_inc(S("hT_psum"), 1)

            def down(e):
                pe.wait_ge(S("hT8_ready"), e + 1)
                if e >= 2:
                    pe.wait_ge(S("ye_ready"), e - 1)
                for c in range(2):
                    last = pe.matmul(pb[6 + e % 2][:, :], hT[e % 2][:, P * c:P * c + P], w2e[e % NWB][:, c, :], start=(c == 0), stop=(c == 1))
                last.then_inc(S("y_psum"), 1)

            transpose_tokens(0)
            for e in range(E3 + 1):
                if e + 1 < E3:
                    transpose_tokens(e + 1)
                if e >= 1:
                    transpose_hidden(e - 1)
                if e < E3:
                    up(e)
                if e >= 1:
                    down(e - 1)

            def multiply_rest(pe, s, e, nth_):
                pe.wait_ge(S("rest_gathered"), nth_ * 16)
                for k in range(KD):
                    last = pe.transpose(pb[0][:, P * k:P * k + P], xg[0][:, P * k:P * k + P], ident[:, :])
                last.then_inc(S("rest_xe_psum"), 1)
                pe.wait_ge(S("rest_xeT"), nth_)
                for k in range(KD):
                    last = pe.matmul(pb[2][:, :], xeT[0][:, k, :], w13[0][:, k, :], start=(k == 0), stop=(k == KD - 1))
                last.then_inc(S("rest_up_psum"), 1)
                pe.wait_ge(S("rest_hmid"), nth_)
                for c in range(2):
                    last = pe.transpose(pb[4][:, P * c:P * c + P], hmid[0][:, P * c:P * c + P], ident[:, :])
                last.then_inc(S("rest_hT_psum"), 1)
                pe.wait_ge(S("rest_hT"), nth_)
                for c in range(2):
                    last = pe.matmul(pb[6][:, :], hT[0][:, P * c:P * c + P], w2e[0][:, c, :], start=(c == 0), stop=(c == 1))
                last.then_inc(S("rest_y_psum"), 1)

            pe.wait_ge(S("ye_ready"), E3)
            rest(pe, multiply_rest)

        @block.scalar
        def _(act_):
            def copy_T(norm, t):
                act_.wait_ge(S("xT_psum"), nth(norm, t + 1))
                act_.activation(xT[:, :, P * t:P * t + P], pb[t][:, :].rearrange("p (k n) -> p k n", k=KD), ACT.Copy).then_inc(S("xT_ready"), 1)

            rooted = [0]

            def roots(*values):
                rooted[0] += 1
                act_.wait_ge(S("root_asked"), rooted[0])
                for n_, (o, v, plus) in enumerate(values):
                    last = act_.activation(o, v, ACT.Sqrt, bias=plus)
                    if n_ < len(values) - 1:
                        last.then_inc(S("early_roots"), 1)
                if len(values) > 1:
                    act_.wait_ge(S("early_roots"), len(values) - 1)
                last.then_inc(S("root_ready"), 1)

            def row_roots():
                roots((V_("rstd", 3), V_("mv", 6).rearrange("p (t c) -> p t c", t=NT)[:, :, 1], LN_EPS))

            row_roots()
            for t in range(NT):
                copy_T("1", t)
            for t in range(NT):
                for half in range(2):
                    act_.wait_ge(S("src_rows_psum"), 2 * t + half + 1)
                    if t and half == 0:
                        act_.wait_ge(S("src_rows_stored"), 16 * t)
                    act_.activation(ab[0][:, D * half:D * half + D], pb[3 + half][:, :], ACT.Copy).then_inc(S("src_half_ready"), 1)
            dv = V_("dis", 3), V_("dinv", 3), dinv_bc[:, :]
            roots(*((v, v, 1.0) for v in dv))
            for u in range(NT * H):
                i, h = divmod(u, H)
                act_.wait_ge(S("row_max_ready"), i + 1)
                if u >= H:
                    act_.wait_ge(S("probsT_psum"), u - H + 1)
                act_.activation(probs[h], mt[i][:, :, h], ACT.Exp, bias=V_("nmax", 24)[:, u:u + 1],
                                accum_out=V_("psum_", 24)[:, u:u + 1]).then_inc(S("probs_ready"), 1)
            for t in range(NT):
                act_.wait_ge(S("ymin_ready"), t + 1)
                act_.activation(ye[:, t], ye[:, t], ACT.Exp).then_inc(S("yexp_ready"), 1)
            row_roots()
            row_roots()
            row_roots()
            for t in range(NT):
                copy_T("3", t)
            for l in range(3):
                for k in range(KD):
                    act_.wait_ge(S("scaled_ready"), KD * l + k + 1)
                    act_.activation(gT[:, k, :], gT[:, k, :], ACT.Relu, bias=bcol[l][:, k:k + 1],
                                    accum_out=V_("gsum", 4)[:, k:k + 1]).then_inc(S("relu_ready"), 1)
                for k in range(KD):
                    act_.wait_ge(S("shift_ready"), KD * l + k + 1)
                    act_.activation(sq_scr[:, :], gT[:, k, :], ACT.Square, bias=V_("nshift", 4)[:, k:k + 1],
                                    accum_out=V_("gsq", 4)[:, k:k + 1]).then_inc(S("square_ready"), 1)
                    act_.wait_ge(S("square_ready"), KD * l + k + 1)
                roots((V_("gmul", 4), V_("gmul", 4), EPS))
            row_roots()
            for t in range(NT):
                act_.wait_ge(S("xqT_psum"), t + 1)
                act_.activation(xqT[:, :, P * t:P * t + P], pbh[t][:, 0:512].rearrange("p (k n) -> p k n", k=KD), ACT.Copy).then_inc(S("xqT_ready"), 1)
            for t in range(NT):
                act_.wait_ge(S("hqT_psum"), t + 1)
                act_.activation(hqT[:, :, P * t:P * t + P], pbh[t][:, 0:256].rearrange("p (k n) -> p k n", k=2), ACT.Copy).then_inc(S("hqT_ready"), 1)
            row_roots()
            for t in range(NT):
                copy_T("5", t)
            row_roots()
            for t in range(NT):
                copy_T("6", t)
            row_roots()
            act_.wait_ge(S("raw6_ready"), 1)
            for t in range(NT):
                act_.activation(V_("ex6", 24)[:, 8 * t:8 * t + E2], V_("raw6", 24)[:, 8 * t:8 * t + E2], ACT.Exp,
                                bias=V_("nm6", 3)[:, t:t + 1], accum_out=V_("es6", 3)[:, t:t + 1]).then_inc(S("ex6_ready"), 1)
            for t in range(NT):
                act_.wait_ge(S("xT_psum"), nth("6b", t + 1))
                act_.wait_ge(S("gate6_psum"), 1)
                for k in range(KD):
                    last = act_.activation(xT[:, k, P * t:P * t + P], pb[t][:, P * k:P * k + P], ACT.Copy, scale=bcol[6][:, k:k + 1])
                last.then_inc(S("xT_ready"), 1)
            for e in range(E2):
                for c in range(2):
                    j = 2 * e + c
                    act_.wait_ge(S("hid6_psum"), j + 1)
                    if e >= 2:
                        act_.wait_ge(S("out6_psum"), NT * (e - 1))
                    act_.activation(hid[e % 2][:, c, :], pb[j % 3][:, 0:N], ACT.Gelu).then_inc(S("hid6_ready"), 1)
            row_roots()
            for t in range(NT):
                copy_T("7", t)
            row_roots()
            row_roots()
            for t in range(NT):
                copy_T("8", t)
            act_.wait_ge(S("logits_psum"), 1)
            act_.activation(scores8[:, :, :], pb[3][:, 0:NT * E3].rearrange("p (t e) -> p t e", t=NT), ACT.Sigmoid).then_inc(S("sigmoid_ready"), 1)
            act_.wait_ge(S("slot0_loaded"), 16)
            s4f = slot0[:, :].bitcast(f32).rearrange("p (e c) -> p e c", c=4)

            def copy_hT(e):
                act_.wait_ge(S("hT_psum"), e + 1)
                if e >= 2:
                    act_.wait_ge(S("y_psum"), e - 1)
                act_.activation(hT[e % 2], pb[4 + e % 2][:, 0:F3], ACT.Copy).then_inc(S("hT8_ready"), 1)

            def silu(e):
                act_.wait_ge(S("up_psum"), e + 1)
                if e >= 2:
                    act_.wait_ge(S("hmid_ready"), e - 1)
                act_.activation(act[e % 2], pb[2 + e % 2][:, 0:F3], ACT.Silu).then_inc(S("silu_ready"), 1)

            def weigh(e):
                act_.wait_ge(S("y_psum"), e + 1)
                if e >= 3:
                    act_.wait_ge(S(f"picks_stored{e % 3}"), 16 * (e // 3))
                act_.activation(ysb[e % 3], pb[6 + e % 2][:, :], ACT.Copy, scale=s4f[:, e, 2:3]).then_inc(S("ye_ready"), 1)

            for e in range(E3 + 1):
                if e >= 1:
                    copy_hT(e - 1)
                if e < E3:
                    silu(e)
                if e >= 1:
                    weigh(e - 1)

            rest_w = rest_rec[:, 2:3].bitcast(f32)

            def evacuate_rest(act_, s, e, nth_):
                act_.wait_ge(S("rest_xe_psum"), nth_)
                act_.activation(xeT[0], pb[0][:, :].rearrange("p (k n) -> p k n", k=KD), ACT.Copy).then_inc(S("rest_xeT"), 1)
                act_.wait_ge(S("rest_up_psum"), nth_)
                act_.activation(act[0], pb[2][:, 0:F3], ACT.Silu).then_inc(S("rest_silu"), 1)
                act_.wait_ge(S("rest_hT_psum"), nth_)
                act_.activation(hT[0], pb[4][:, 0:F3], ACT.Copy).then_inc(S("rest_hT"), 1)
                act_.wait_ge(S("rest_y_psum"), nth_)
                act_.activation(ysb[0], pb[6][:, :], ACT.Copy, scale=rest_w).then_inc(S("rest_weighed"), 1)

            rest(act_, evacuate_rest)

        @block.vector
        def _(dve):
            issued = [0]

            def go(ins):
                issued[0] += 1
                return ins.then_inc(S("dve_step"), 1)

            def settle():
                dve.wait_ge(S("dve_step"), issued[0])

            def one(ins):
                go(ins)
                settle()

            def bc(ap, shape):
                return ap.to_broadcast(shape)

            ts, tt, stt = dve.tensor_scalar, dve.tensor_tensor, dve.scalar_tensor_tensor
            st = V_("st", 18).rearrange("p (t c) -> p t c", t=NT)
            mv = V_("mv", 6).rearrange("p (t c) -> p t c", t=NT)
            rstd = V_("rstd", 3)

            asked = [0]

            def roots(ins):
                asked[0] += 1
                ins.then_inc(S("root_asked"), 1)
                settle()
                dve.wait_ge(S("root_ready"), asked[0])

            def layernorm(src, dst, norm=None):
                for t in range(NT):
                    go(dve.bn_stats(st[:, t, :], src[:, t, :]))
                settle()
                for t in range(NT):
                    last = dve.bn_aggr(mv[:, t, :], st[:, t, :])
                    if t < NT - 1:
                        go(last)
                roots(last)
                one(dve.reciprocal(rstd, rstd))
                for t in range(NT):
                    ins = ts(dst[:, t, :], src[:, t, :], mv[:, t, 0:1], rstd[:, t:t + 1], ALU.subtract, ALU.mult)
                    if norm is None:
                        go(ins)
                    else:
                        ins.then_inc(S("xn_ready"), 1)
                if norm is None:
                    settle()
                else:
                    dve.wait_ge(S("xn_ready"), nth(norm, NT))

            dve.wait_ge(S("edges_loaded"), 32)
            go(dve.tensor_copy(src_f, src_i))
            go(dve.tensor_copy(dst_f, dst_i))
            go(dve.tensor_copy(src_h, src_i))
            go(dve.tensor_copy(dst_h, dst_i))
            settle()
            one(stt(key_f, src_f, float(N), dst_f, ALU.mult, ALU.add))
            dve.wait_ge(S("consts_ready"), 1)
            go(ts(ident16[:, 0:P], ident[:, :], float(N), None, ALU.mult))
            dve.tensor_copy(ident16[:, P:2 * P], ident[:, :]).then_inc(S("ident16_ready"), 1)
            settle()
            dve.wait_ge(S("ident16_ready"), 1)
            dve.engine_nop().then_inc(S("edge_h_ready"), 1)
            dve.engine_nop().then_inc(S("edge_idx_ready"), 1)
            dve.wait_ge(S("x_loaded"), 16)
            layernorm(x3, xn3, "1")
            dve.wait_ge(S("rows0_loaded"), 96)
            waL, waR = V_("waL", P), V_("waR", P)
            go(ts(waL, war, SLOPE, None, ALU.mult))
            go(ts(waR, war, 1.0 - SLOPE, None, ALU.mult))
            settle()
            heads = "p (h c) -> p h c"
            lsc3 = lsc.rearrange(heads, h=H)
            waL3 = bc(waL[:, None, :], [P, H, P])

            def linear_part(row, bias, ready):
                one(tt(lsc3, row[:, 0:2 * D].rearrange(heads, h=H), waL3, ALU.mult))
                one(dve.tensor_reduce(row[:, 2 * D:ROW], lsc3, AX, ALU.add))
                if bias is not None:
                    one(ts(row[:, 2 * D:ROW], row[:, 2 * D:ROW], bias, None, ALU.add))
                dve.engine_nop().then_inc(ready, 1)

            for t in range(NT):
                for b in range(4):
                    if b >= 2:
                        half = b - 2
                        dve.wait_ge(S("dst_rows_psum"), 2 * t + half + 1)
                        if t and half == 0:
                            dve.wait_ge(S("dst_rows_stored"), 16 * t)
                        tt(ab[1][:, D * half:D * half + D], pb[(5, 0)[half]][:, :], bwr[:, D * half:D * half + D], ALU.add).then_inc(S("dst_half_ready"), 1)
                    g = 4 * t + b
                    dve.wait_ge(S("key_psum"), g + 1)
                    for j in range(4):
                        e = 4 * g + j
                        go(stt(lsc[:, P * j:P * j + P], pb[6 + g % 2][:, P * j:P * j + P], key_f[:, e:e + 1], tri[:, :],
                               ALU.is_equal, ALU.mult, accum_out=dup_f[:, e:e + 1]))
                    settle()
                    dve.engine_nop().then_inc(S("dup_used"), 1)
                    if b == 1:
                        dve.wait_ge(S("src_half_ready"), 2 * t + 2)
                        linear_part(ab[0], None, S("src_rows_ready"))
                    if b == 3:
                        dve.wait_ge(S("dst_half_ready"), 2 * t + 2)
                        linear_part(ab[1], bar, S("dst_rows_ready"))
            one(stt(row_i, dup_f, 262144.0, key_f, ALU.mult, ALU.add))
            for t in range(NT):
                dve.wait_ge(S("V_psum"), t + 1)
                tt(V[:, t, :], pb[3 + t][:, :], bvr, ALU.add).then_inc(S("V_ready"), 1)
            dve.wait_ge(S("bit_w_loaded"), 32)
            wabs = V_("wabs", 2)
            go(dve.tensor_reduce(wabs[:, 0:1], wu, AX, ALU.add, apply_absolute_value=True))
            dve.tensor_reduce(wabs[:, 1:2], wd, AX, ALU.add, apply_absolute_value=True).then_inc(S("bit_abs_last"), 1)
            settle()
            dve.wait_ge(S("bit_abs_last"), 1)
            dve.engine_nop().then_inc(S("bit_abs_ready"), 1)
            for t in range(ET):
                if t >= 2:
                    dve.wait_ge(S("onehot_used"), t - 1)
                go(ts(oh[:, t % 2, 0, :], iota_h[:, :], src_f[:, t:t + 1], None, ALU.is_equal))
                settle()
                ts(oh[:, t % 2, 1, :], iota_h[:, :], dst_f[:, t:t + 1], None, ALU.is_equal).then_inc(S("onehot_ready"), 1)
                j = t % NGA
                dve.wait_ge(S(f"dst_added{j}"), 16 * (t // NGA + 1))
                for h in range(H):
                    go(stt(lsc[:, P * h:P * h + P], ga[j][:, P * h:P * h + P], 0.0, waR, ALU.max, ALU.mult,
                           accum_out=w_e3[:, t, h:h + 1]))
                settle()
                one(tt(w_e3[:, t, :], w_e3[:, t, :], ga[j][:, 2 * D:ROW], ALU.add))
                dve.engine_nop().then_inc(S("edge_sum_used"), 1)
                dve.engine_nop().then_inc(S("w_ready"), 1)
            dve.wait_ge(S("onehot_used"), ET)
            for s in range(NT):
                go(dve.tensor_copy(cnt[:, s, :], pb[s][:, 0:N]))
            settle()
            go(dve.tensor_copy(cntI_s[:, :], cnt_s[:, :]))
            outdeg = V_("outdeg", 3)
            go(dve.tensor_reduce(outdeg, cnt, AX, ALU.add))
            settle()
            for s in range(NT):
                go(tt(cntI[:, s, P * s:P * s + P], cntI[:, s, P * s:P * s + P], ident[:, :], ALU.add))
            settle()
            dve.engine_nop().then_inc(S("cnt_ready"), 1)
            dis, dinv, wsc = V_("dis", 3), V_("dinv", 3), V_("wsc", 2)
            go(dve.tensor_copy(dis, outdeg))
            settle()
            dve.wait_ge(S("deg_psum"), 1)
            go(dve.tensor_copy(dinv, pb[6][:, 0:3]))
            roots(dve.tensor_copy(dinv_bc[:, :], pb[7][:, 0:N]))
            go(dve.reciprocal(dis, dis))
            go(dve.reciprocal(dinv, dinv))
            go(dve.reciprocal(dinv_bc[:, :], dinv_bc[:, :]))
            go(ts(rdeg_bc[:, :], pb[7][:, 0:N], 1.0, None, ALU.max))
            go(ts(wsc, pb[6][:, 8:10], 1.0 / (D * F1), EPS, ALU.mult, ALU.max))
            settle()
            go(dve.reciprocal(rdeg_bc[:, :], rdeg_bc[:, :]))
            half_sc = V_("half_sc", 4)
            go(ts(half_sc[:, 0:2], wsc, 0.5, None, ALU.mult))
            go(ts(half_sc[:, 2:4], wsc, -0.5, None, ALU.mult))
            settle()
            for j, w in enumerate((wu, wd)):
                q = wq[:, 1024 * j:1024 * j + 1024]
                go(ts(q, w, half_sc[:, j:j + 1], None, ALU.is_gt))
                one(ts(w, w, half_sc[:, 2 + j:3 + j], None, ALU.is_lt))
                go(tt(q, q, w, ALU.subtract))
            settle()
            dve.engine_nop().then_inc(S("wq_ready"), 1)
            nmax, psum_ = V_("nmax", 24), V_("psum_", 24)

            def row_max(i):
                dve.wait_ge(S(f"scores_loaded{i}"), 16)
                m = nmax[:, H * i:H * i + H]
                one(dve.tensor_reduce(m, mt[i].rearrange("p n h -> p h n"), AX, ALU.max))
                ts(m, m, NEG_FLOOR, -1.0, ALU.max, ALU.mult).then_inc(S("row_max_ready"), 1)

            row_max(0)
            rs = V_("rs", 24)
            for i in range(NT):
                if i + 1 < NT:
                    row_max(i + 1)
                for h in range(H):
                    u = H * i + h
                    dve.wait_ge(S("probsT_psum"), u + 1)
                    if u >= H:
                        dve.wait_ge(S("attended_psum"), u - H + 1)
                    dve.tensor_copy(probsT[h], pb[u % 3][:, 0:N]).then_inc(S("probsT_ready"), 1)
                dve.wait_ge(S("attended_psum"), H * (i + 1))
                r = rs[:, H * i:H * i + H]
                one(ts(r, psum_[:, H * i:H * i + H], 1e-30, None, ALU.max))
                one(dve.reciprocal(r, r))
                one(tt(y0[:, i, :].rearrange(heads, h=H), pb[3 + i][:, :].rearrange(heads, h=H), bc(r[:, :, None], [P, H, HD]), ALU.mult))
                ts(ye[:, i, :], y0[:, i, :], 0.0, None, ALU.min).then_inc(S("ymin_ready"), 1)
                go(ts(yr[:, i, :], y0[:, i, :], 0.0, None, ALU.max))
            settle()
            for t in range(NT):
                dve.wait_ge(S("yexp_ready"), t + 1)
                go(stt(y0[:, t, :], ye[:, t, :], -1.0, yr[:, t, :], ALU.add, ALU.add))
            settle()
            go(tt(R2[:, 1024:2560], R2[:, 1024:2560], xn_s[:, :], ALU.add))
            settle()
            layernorm(y0, ye)
            for t in range(NT):
                go(tt(ye[:, t, :], ye[:, t, :], g0r, ALU.mult))
            settle()
            for t in range(NT):
                go(tt(ye[:, t, :], ye[:, t, :], b0r, ALU.add))
            settle()
            for t in range(NT):
                tt(x3[:, t, :], x3[:, t, :], ye[:, t, :], ALU.add).then_inc(S("x_ready"), 1)
            dve.wait_ge(S("x_ready"), NT * 0 + NT)

            layernorm(x3, xn3)
            first = V_("first", 144).rearrange("p (t c) -> p t c", t=NT)
            for t in range(NT):
                go(stt(first[:, t, :], xn3[:, t, 64:112], 0.5, fall48[:, :], ALU.is_gt, ALU.mult))
            settle()
            far, idx = V_("far", 9), V_("idx", 9)
            one(dve.tensor_reduce(far, V_("first", 144).rearrange("p (c i) -> p c i", i=16), AX, ALU.max))
            one(ts(idx, far, -1.0, 16.0, ALU.mult, ALU.add))
            one(stt(idx, far, 0.0, idx, ALU.is_gt, ALU.mult))
            idx3 = idx.rearrange("p (t c) -> p t c", t=NT)
            idx_i = V_("idx_i", 9).bitcast(i32)
            one(dve.tensor_copy(idx_i, idx))
            ii = idx_i.rearrange("p (t c) -> p t c", t=NT)
            val, left, right = (V_(n_, 3).bitcast(i32) for n_ in ("val", "left", "right"))
            sa_i = V_("sa_i", 3).bitcast(i32)
            mark, shl, shr, both, amp = (V_(n_, 3) for n_ in ("mark", "shl", "shr", "both", "amp"))
            go(dve.tensor_copy(sa_i, ii[:, :, 2]))
            go(ts(mark, xn3[:, :, 0], 0.5, None, ALU.is_gt))
            go(ts(shl, xn3[:, :, 39], 0.5, None, ALU.is_gt))
            go(ts(shr, xn3[:, :, 40], 0.5, None, ALU.is_gt))
            one(ts(val, ii[:, :, 1], 4, None, ALU.logical_shift_left))
            one(tt(val, val, ii[:, :, 0], ALU.bitwise_or))
            go(tt(left, val, sa_i, ALU.logical_shift_left))
            go(tt(right, val, sa_i, ALU.logical_shift_right))
            go(tt(both, shl, shr, ALU.mult))
            settle()
            go(tt(shr, shr, both, ALU.subtract))
            go(tt(shl, shl, mark, ALU.mult))
            go(ts(left, left, 255, None, ALU.bitwise_and))
            settle()
            go(tt(shr, shr, mark, ALU.mult))
            leftf, rightf, res = (V_(n_, 3) for n_ in ("leftf", "rightf", "res"))
            go(dve.tensor_copy(leftf, left))
            go(dve.tensor_copy(rightf, right))
            settle()
            go(tt(leftf, leftf, shl, ALU.mult))
            go(tt(rightf, rightf, shr, ALU.mult))
            go(tt(amp, shl, shr, ALU.add))
            settle()
            go(tt(res, leftf, rightf, ALU.add))
            go(ts(amp, amp, 2.0, None, ALU.mult))
            settle()
            one(dve.tensor_copy(val, res))
            go(ts(left, val, 15, None, ALU.bitwise_and))
            go(ts(right, val, 4, None, ALU.logical_shift_right))
            settle()
            rlo, rhi = V_("rlo", 3), V_("rhi", 3)
            go(dve.tensor_copy(rlo, left))
            go(dve.tensor_copy(rhi, right))
            settle()
            for t in range(NT):
                for o, nib in ((0, rlo), (16, rhi)):
                    go(ts(first[:, t, o:o + 16], iota64[:, 0:16], nib[:, t:t + 1], amp[:, t:t + 1], ALU.is_equal, ALU.mult))
            settle()
            go(tt(xn3[:, :, 128:160], xn3[:, :, 128:160], first[:, :, 0:32], ALU.add))
            settle()
            for t in range(NT):
                tt(x3[:, t, :], x3[:, t, :], xn3[:, t, :], ALU.add).then_inc(S("x_ready"), 1)
            dve.wait_ge(S("x_ready"), NT * 1 + NT)

            layernorm(x3, xn3, "3")
            dve.wait_ge(S("rows_loaded"), 96)
            nshift, gsum, gsq, gmul, gadd = (V_(n_, 4) for n_ in ("nshift", "gsum", "gsq", "gmul", "gadd"))
            for l in range(3):
                for t in range(NT):
                    dve.wait_ge(S("hw_psum"), NT * l + t + 1)
                    if l and t == 0:
                        dve.wait_ge(S("agg_psum"), KD * l)
                    ts(xws[:, t, :], pb[3 + t][:, :], dinv[:, t:t + 1], None, ALU.mult).then_inc(S("hw_ready"), 1)
                for k in range(KD):
                    dve.wait_ge(S("agg_psum"), KD * l + k + 1)
                    tt(gT[:, k, :], pb[(0, 1, 2, 6)[k]][:, 0:N], dinv_bc[:, :], ALU.mult).then_inc(S("scaled_ready"), 1)
                for k in range(KD):
                    dve.wait_ge(S("relu_ready"), KD * l + k + 1)
                    stt(nshift[:, k:k + 1], gsum[:, k:k + 1], -1.0 / N, bcol[5][:, k:k + 1], ALU.mult, ALU.mult).then_inc(S("shift_ready"), 1)
                dve.wait_ge(S("square_ready"), KD * (l + 1))
                roots(ts(gmul, gsq, 1.0 / N, None, ALU.mult))
                one(dve.reciprocal(gmul, gmul))
                one(tt(gmul, gmul, bcol[3], ALU.mult))
                one(tt(gadd, nshift, gmul, ALU.mult))
                one(tt(gadd, gadd, bcol[4], ALU.add))
                for k in range(KD):
                    ts(xT[:, k, :], gT[:, k, :], gmul[:, k:k + 1], gadd[:, k:k + 1], ALU.mult, ALU.add).then_inc(S("hT_ready"), 1)
            for t in range(NT):
                dve.wait_ge(S("h_out_psum"), t + 1)
                tt(x3[:, t, :], x3[:, t, :], pb[3 + t][:, :], ALU.add).then_inc(S("x_ready"), 1)
            dve.wait_ge(S("x_ready"), NT * 2 + NT)

            layernorm(x3, xn3)
            amax, xsc, isc, amax2, hsc = (V_(n_, 3) for n_ in ("amax", "xsc", "isc", "amax2", "hsc"))

            def quantise(v3, m, scale, q3, top_ready, f):
                one(dve.tensor_reduce(m, v3, AX, ALU.max, apply_absolute_value=True))
                one(ts(m, m, EPS, None, ALU.max))
                one(dve.reciprocal(scale, m))
                one(ts(scale, scale, 127.0, None, ALU.mult))
                for t in range(NT):
                    go(ts(v3[:, t, :], v3[:, t, :], scale[:, t:t + 1], ROUND, ALU.mult, ALU.add))
                settle()
                for t in range(NT):
                    go(ts(v3[:, t, :], v3[:, t, :], ROUND, 127.0, ALU.subtract, ALU.min))
                settle()
                for t in range(NT):
                    ts(q3[:, t, :], v3[:, t, :], -128.0, None, ALU.max).then_inc(top_ready, 1)

            quantise(xn3, amax, xsc, xq, S("xq_ready"), D)
            one(dve.reciprocal(isc, xsc))
            one(ts(isc, isc, wsc[:, 0:1], None, ALU.mult))
            for t in range(NT):
                dve.wait_ge(S("up_bit_psum"), t + 1)
                go(ts(hb[:, t, :], pb[3 + t][:, 0:F1], isc[:, t:t + 1], 0.0, ALU.mult, ALU.max))
            settle()
            hb2 = WK[:, 1536:2304]
            hr2, hd2 = xT_s[:, 0:768], xT_s[:, 768:1536]
            one(ts(hr2, hb2, ROUND, None, ALU.add))
            one(ts(hr2, hr2, ROUND, 127.0, ALU.subtract, ALU.min))
            one(tt(hd2, hr2, hb2, ALU.subtract))
            one(tt(hb2, hb2, hd2, ALU.add))
            quantise(hb, amax2, hsc, hq, S("hq_ready"), F1)
            one(dve.reciprocal(isc, hsc))
            one(ts(isc, isc, wsc[:, 1:2], None, ALU.mult))
            for t in range(NT):
                dve.wait_ge(S("down_bit_psum"), t + 1)
                stt(x3[:, t, :], pb[3 + t][:, :], isc[:, t:t + 1], x3[:, t, :], ALU.mult, ALU.add).then_inc(S("x_ready"), 1)
            dve.wait_ge(S("x_ready"), NT * 3 + NT)

            layernorm(x3, xn3, "5")
            for t in range(NT):
                dve.wait_ge(S("hw5_psum"), t + 1)
                one(tt(xws[:, t, :], pb[3 + t][:, :], b2r, ALU.add))
                ts(xws[:, t, :], xws[:, t, :], dis[:, t:t + 1], None, ALU.mult).then_inc(S("hw5_ready"), 1)
            for t in range(NT):
                dve.wait_ge(S("agg5_psum"), t + 1)
                one(ts(xn3[:, t, :], pb[t][:, :], dis[:, t:t + 1], 0.0, ALU.mult, ALU.max))
                tt(x3[:, t, :], x3[:, t, :], xn3[:, t, :], ALU.add).then_inc(S("x_ready"), 1)
            dve.wait_ge(S("x_ready"), NT * 4 + NT)

            layernorm(x3, xn3, "6")
            dve.wait_ge(S("gate6_psum"), 1)
            raw6, nm6, ex6, es6 = V_("raw6", 24), V_("nm6", 3), V_("ex6", 24), V_("es6", 3)
            t8_ = "p (t e) -> p t e"
            one(dve.tensor_copy(raw6.rearrange(t8_, t=NT)[:, :, 0:E2], pb[6][:, 0:24].rearrange(t8_, t=NT)[:, :, 0:E2]))
            go(dve.memset(ex6, -1.0))
            one(dve.tensor_reduce(nm6, raw6.rearrange(t8_, t=NT)[:, :, 0:E2], AX, ALU.max, negate=True))
            dve.engine_nop().then_inc(S("raw6_ready"), 1)
            layernorm(xn3, y6, "6b")
            dve.wait_ge(S("ex6_ready"), NT)
            one(dve.reciprocal(es6, es6))
            top6, gm6, den6 = V_("top6", 24), V_("gm6", 24), V_("den6", 3)
            for t in range(NT):
                e8 = ex6[:, 8 * t:8 * t + 8]
                one(ts(e8, e8, es6[:, t:t + 1], None, ALU.mult))
                one(dve.max(top6[:, 8 * t:8 * t + 8], e8))
                one(dve.max_index(smi[:, 8 * t:8 * t + 8], top6[:, 8 * t:8 * t + 8], e8))
                one(tt(den6[:, t:t + 1], top6[:, 8 * t:8 * t + 1], top6[:, 8 * t + 1:8 * t + 2], ALU.add))
                one(ts(den6[:, t:t + 1], den6[:, t:t + 1], 1e-9, None, ALU.add))
                one(dve.reciprocal(den6[:, t:t + 1], den6[:, t:t + 1]))
                one(tt(den6[:, t:t + 1], den6[:, t:t + 1], top6[:, 8 * t:8 * t + 1], ALU.mult))
                go(dve.tensor_copy(idx[:, t:t + 1], smi[:, 8 * t:8 * t + 1]))
                settle()
                one(ts(gm6[:, 8 * t:8 * t + 8], iota64[:, 0:8], idx[:, t:t + 1], den6[:, t:t + 1], ALU.is_equal, ALU.mult))
            for e in range(E2):
                for t in range(NT):
                    j = NT * e + t
                    dve.wait_ge(S("out6_psum"), j + 1)
                    stt(x3[:, t, :], pb[(3, 4, 5, 7)[j % 4]][:, :], gm6[:, 8 * t + e:8 * t + e + 1], x3[:, t, :],
                        ALU.mult, ALU.add).then_inc(S("out6_used"), 1)
                    dve.wait_ge(S("out6_used"), j + 1)
            for t in range(NT):
                dve.engine_nop().then_inc(S("x_ready"), 1)
            dve.engine_nop().then_inc(S("x6_done"), 1)

            layernorm(x3, xn3, "7")
            dve.engine_nop().then_inc(S("gate_done6"), 1)
            for k in range(KD):
                dve.wait_ge(S("neigh_psum"), k + 1)
                tt(gT[:, k, :], pb[3 + k][:, 0:N], rdeg_bc[:, :], ALU.mult).then_inc(S("neighT_ready"), 1)
            for t in range(NT):
                dve.wait_ge(S("sage_psum"), t + 1)
                tt(y6[:, t, :], pb[t][:, :], b3r, ALU.add).then_inc(S("sage_used"), 1)
            dve.wait_ge(S("sage_used"), NT)
            layernorm(y6, y6)
            for t in range(NT):
                go(tt(y6[:, t, :], y6[:, t, :], g3r, ALU.mult))
            settle()
            for t in range(NT):
                go(tt(y6[:, t, :], y6[:, t, :], be3r, ALU.add))
            settle()
            for t in range(NT):
                tt(x3[:, t, :], x3[:, t, :], y6[:, t, :], ALU.add).then_inc(S("x_ready"), 1)
            dve.wait_ge(S("x_ready"), NT * 6 + NT)

            layernorm(x3, xn3, "8")
            dve.wait_ge(S("sigmoid_ready"), 1)
            one(tt(biased, scores8, bc(gateb[:, None, :], [P, NT, E3]), ALU.add))
            b2 = WK[:, 192:384]
            for g in range(NT * G3):
                go(dve.max(top_in_group[:, g, :], b2[:, 8 * g:8 * g + 8]))
            settle()
            gsc, rank = V_("gsc", 24), V_("rank", 24)
            one(tt(gsc, top_in_group[:, :, 0], top_in_group[:, :, 1], ALU.add))
            be, ti = (v.rearrange("p (g m) -> p g m", g=G3) for v in (beats, ties))
            for t in range(NT):
                g8 = gsc[:, G3 * t:G3 * t + G3]
                other, own = bc(g8[:, None, :], [P, G3, G3]), bc(g8[:, :, None], [P, G3, G3])
                go(tt(be, other, own, ALU.is_gt))
                one(tt(ti, other, own, ALU.is_equal))
                one(tt(ties, ties, tri8[:, :], ALU.mult))
                one(tt(beats, beats, ties, ALU.add))
                one(dve.tensor_reduce(rank[:, G3 * t:G3 * t + G3], be, AX, ALU.add))
            one(ts(rank, rank, float(TOPG), 1e30, ALU.is_ge, ALU.mult))
            grp = "p (g m) -> p g m"
            one(tt(WK[:, 704:896].rearrange(grp, m=8), b2.rearrange(grp, m=8), bc(rank[:, :, None], [P, NT * G3, 8]), ALU.subtract))
            top8, idx8f = V_("top8", 24), V_("idx8f", 24)
            for t in range(NT):
                v8 = top8[:, 8 * t:8 * t + 8]
                one(dve.max(v8, masked[:, t, :]))
                go(dve.max_index(smi[:, 8 * t:8 * t + 8], v8, masked[:, t, :]))
                go(dve.match_replace(replaced[:, t, :], v8, masked[:, t, :], NEG))
            settle()
            go(dve.tensor_copy(idx8f, smi[:, 0:24]))
            go(ts(WK[:, 1088:1280], WK[:, 896:1088], -2e38, None, ALU.is_lt))
            settle()
            dve.tensor_copy(WK[:, 1536:1632].bitcast(bf16), WK[:, 1088:1280]).then_inc(S("picked_ready"), 1)
            one(tt(WK[:, 1088:1280], WK[:, 1088:1280], WK[:, 0:192], ALU.mult))
            wsum = V_("wsum", 3)
            one(dve.tensor_reduce(wsum, selw, AX, ALU.add))
            one(dve.reciprocal(wsum, wsum))
            for t in range(NT):
                go(ts(selw[:, t, :], selw[:, t, :], wsum[:, t:t + 1], ROUTED_SCALE, ALU.mult, ALU.mult))
            settle()
            dve.wait_ge(S("place_psum"), 1)
            for t in range(NT):
                go(stt(place[:, t, :], pb[4][:, E3 * t:E3 * t + E3], float(E3), iota64[:, :], ALU.mult, ALU.add))
            settle()
            one(dve.tensor_reduce(V_("most", 1), pb[4][:, E3 * NT:E3 * NT + E3], AX, ALU.max))
            dve.tensor_copy(most[:, :], V_("most", 1)).then_inc(S("most_ready"), 1)
            recf = rec[:, :].bitcast(f32).rearrange("p (t k c) -> p t k c", t=NT, k=K3)
            for t in range(NT):
                for k in range(K3):
                    c = K3 * t + k
                    go(stt(scr64, iota64[:, :], idx8f[:, c:c + 1], place[:, t, :], ALU.is_equal, ALU.mult, accum_out=pick_row_f[:, c:c + 1]))
                    settle()
                    go(stt(scr64, iota64[:, :], idx8f[:, c:c + 1], selw[:, t, :], ALU.is_equal, ALU.mult, accum_out=recf[:, t, k, 2:3]))
                    settle()
            one(dve.tensor_copy(pick_row, pick_row_f))
            dve.engine_nop().then_inc(S("picks_ready"), 1)

            def copy_xeT(e):
                dve.wait_ge(S("xe_psum"), e + 1)
                if e >= 2:
                    dve.wait_ge(S("up_psum"), e - 1)
                dve.tensor_copy(R2[:, 2048 + D * (e % 2):2048 + D * (e % 2) + D], pb[e % 2][:, :]).then_inc(S("xeT_ready"), 1)

            def gate_hidden(e):
                dve.wait_ge(S("silu_ready"), e + 1)
                if e >= 2:
                    dve.wait_ge(S("hT_psum"), e - 1)
                tt(hmid[e % 2], act[e % 2], pb[2 + e % 2][:, F3:2 * F3], ALU.mult).then_inc(S("hmid_ready"), 1)

            copy_xeT(0)
            for e in range(E3):
                if e + 1 < E3:
                    copy_xeT(e + 1)
                gate_hidden(e)

            def gate_rest(dve, s, e, nth_):
                dve.wait_ge(S("rest_silu"), nth_)
                tt(hmid[0], act[0], pb[2][:, F3:2 * F3], ALU.mult).then_inc(S("rest_hmid"), 1)

            rest(dve, gate_rest)
            for t in range(NT):
                dve.wait_ge(S(f"picks_loaded{t}"), 16)
                y = ypick[t]
                for w in (4, 2, 1):
                    one(tt(y[:, 0:D * w], y[:, 0:D * w], y[:, D * w:2 * D * w], ALU.add))
                tt(x3[:, t, :], x3[:, t, :], y[:, 0:D], ALU.add).then_inc(S("x_ready"), 1)


def kernel(x, src, dst, **w):
    import numpy as np
    import concourse.bacc as bacc
    from concourse.bass_utils import run_bass_kernel_spmd as run

    def col(v):
        return np.asarray(v).reshape(KD, P).T

    g = {k: np.asarray(v) for k, v in w.items()}
    arrays = {
        "x": np.asarray(x), "src": np.asarray(src), "dst": np.asarray(dst),
        "L0_Ww": g["L0_gnn_Ww"], "L0_bw": g["L0_gnn_bw"], "L0_Wv": g["L0_gnn_Wv"], "L0_bv": g["L0_gnn_bv"],
        "L0_gamma": g["L0_gnn_gamma"], "L0_beta": g["L0_gnn_beta"], "L0_Wa": g["L0_gnn_Wa"].reshape(-1), "L0_ba": g["L0_gnn_ba"],
        "L1_W0": g["L1_gnn_W0"], "L1_W1": g["L1_gnn_W1"], "L1_W2": g["L1_gnn_W2"],
        "L1_wu": g["L1_ffn_w_up"].T, "L1_wd": g["L1_ffn_w_down"].T,
        "L2_W": g["L2_gnn_W"].T, "L2_b": g["L2_gnn_b"],
        "L2_w_gating": g["L2_ffn_w_gating"], "L2_w1": g["L2_ffn_w1"], "L2_w2": g["L2_ffn_w2"],
        "L3_self": g["L3_gnn_W_self"].T, "L3_neigh": g["L3_gnn_W_neigh"].T,
        "L3_bias": g["L3_gnn_bias"], "L3_gamma": g["L3_gnn_gamma"], "L3_beta": g["L3_gnn_beta"],
        "L3_gate_w": g["L3_ffn_gate_w"].T, "L3_gate_b": g["L3_ffn_gate_b"],
        "L3_w1": g["L3_ffn_w1"], "L3_w3": g["L3_ffn_w3"], "L3_w2": g["L3_ffn_w2"],
        "fcols": np.concatenate([col(g[k]) for k in (
            "L1_gnn_b0", "L1_gnn_b1", "L1_gnn_b2", "L1_gnn_gn_weight", "L1_gnn_gn_bias", "L1_gnn_gn_mean_scale",
            "L2_ffn_gamma")], axis=1),
    }
    arrays = {k: np.ascontiguousarray(v) for k, v in arrays.items()}
    nc = bacc.Bacc("TRN2", target_bir_lowering=False, num_devices=1)
    ins = {k: nc.dram_tensor(k, v.shape, mybir.dt.from_np(v.dtype), kind="ExternalInput").ap() for k, v in arrays.items()}
    out = nc.dram_tensor("out", (N, D), f32, kind="ExternalOutput").ap()
    build(nc, ins, out)
    r = run(nc, [arrays], core_ids=[0])
    return r.results[0]["out"]
```

```python
from contextlib import ExitStack

import concourse.bass as bass
from concourse import mybir

N = 384
D = 512
E = 6144
P = 128
NT = N // P
KD = D // P
ET = E // P
H = 8
HD = D // H
HW = 2 * HD
F1 = 256
E2, F2 = 6, 256
E3, F3 = 64, 256
G3, TOPG, K3 = 8, 4, 8
ROUTED_SCALE = 2.5
LN_EPS = 1e-5
EPS = 1e-5
NEG = -3.0e38
NEG_FLOOR = -1.0e37
ROUND = 1.5 * 2.0 ** 23
SLOPE = 0.01
ROW = 2 * D + H
NGA = 6
NWB = 8
NYB = 4
EF = 9
NPR = 6
NXG = 6

f32 = mybir.dt.float32
bf16 = mybir.dt.bfloat16
f16 = mybir.dt.float16
i32 = mybir.dt.int32
u32 = mybir.dt.uint32
NORMS = ("1", "3", "5", "6", "6b", "7", "8")


def nth(norm, tiles):
    return NT * NORMS.index(norm) + tiles


ALU = mybir.AluOpType
ACT = mybir.ActivationFunctionType
AX = mybir.AxisListType.X


def build(nc, a, out):
    ctx = ExitStack()
    with ctx:
        def sb(name, cols, dt=f32):
            return ctx.enter_context(nc.sbuf_tensor(name, [P, cols], dt))

        sems = {}

        def S(name):
            if name not in sems:
                sems[name] = ctx.enter_context(nc.semaphore(name))
            return sems[name]

        tab_src = nc.dram_tensor("tab_src", (N, ROW), f32, kind="Internal").ap()
        tab_dst = nc.dram_tensor("tab_dst", (N, ROW), f32, kind="Internal").ap()
        score = nc.dram_tensor("score", (N * N, H), f32, kind="Internal").ap()
        tok_tab = nc.dram_tensor("tok_tab", (N, D), f32, kind="Internal").ap()
        slot_tab = nc.dram_tensor("slot_tab", (N * E3, 4), i32, kind="Internal").ap()
        pick_out = nc.dram_tensor("pick_out", (N * K3, D), f32, kind="Internal").ap()

        R1 = sb("R1", 18432)
        R2 = sb("R2", 18688)
        WK = R1[:, 15360:18432]
        x_s = sb("x_s", NT * D)
        xn_s = sb("xn_s", NT * D)
        xT_s = sb("xT_s", KD * N)
        cnt_s = sb("cnt_s", NT * N)
        cntI_s = sb("cntI_s", NT * N)
        rows = sb("rows", 4 * D)
        cols = sb("cols", 28)
        gateb = sb("gateb", E3)
        ident = sb("ident", P)
        ident16 = sb("ident16", 2 * P, f16)
        identb = sb("identb", P, bf16)
        onesb = sb("onesb", P, bf16)
        before_s = sb("before_s", 2 * P)
        ones, tri = before_s[:, 0:P], before_s[:, P:2 * P]
        trib = sb("trib", P, bf16)
        iota_h = sb("iota_h", N, f16)
        iota64 = sb("iota64", E3)
        fall48 = sb("fall48", 48)
        wq = sb("wq", 2 * KD * F1, bf16)
        dinv_bc = sb("dinv_bc", N)
        rdeg_bc = sb("rdeg_bc", N)
        e_i = sb("e_i", 3 * ET, i32)
        e_f = sb("e_f", 4 * ET)
        e_h = sb("e_h", 2 * ET, f16)
        w_e = sb("w_e", ET * H)
        slot0 = sb("slot0", E3 * 4, i32)
        rest_rec = sb("rest_rec", 4, i32)
        most = sb("most", 1, i32)
        rec = sb("rec", NT * K3 * 4, i32)
        sm = sb("sm", 1024)
        smi = sb("smi", 32, u32)

        x3 = x_s[:, :].rearrange("p (t d) -> p t d", t=NT)
        xn3 = xn_s[:, :].rearrange("p (t d) -> p t d", t=NT)
        xT = xT_s[:, :].rearrange("p (k n) -> p k n", k=KD)
        cnt = cnt_s[:, :].rearrange("p (t n) -> p t n", t=NT)
        cntI = cntI_s[:, :].rearrange("p (t n) -> p t n", t=NT)
        src_i, dst_i, row_i = (e_i[:, j * ET:(j + 1) * ET] for j in range(3))
        src_f, dst_f, key_f, dup_f = (e_f[:, j * ET:(j + 1) * ET] for j in range(4))
        src_h, dst_h = e_h[:, 0:ET], e_h[:, ET:2 * ET]
        w_e3 = w_e[:, :].rearrange("p (t h) -> p t h", h=H)
        rec4 = rec[:, :].rearrange("p (t k c) -> p t k c", t=NT, k=K3)

        def r1(o, n, **kw):
            return R1[:, o:o + n]

        Ww = r1(0, 8192).rearrange("p (c n) -> p c n", c=8)
        Wv = r1(8192, 2048).rearrange("p (k n) -> p k n", k=KD)
        
        ab = [r1(16320 + ROW * j, ROW) for j in range(2)]
        ga = [r1(10240 + ROW * j, ROW) for j in range(NGA - 2)] + ab
        lsc = r1(14400, 1024)
        mt = [r1(3072 * j, 3072).rearrange("p (n h) -> p n h", h=H) for j in range(NT)]
        probs = [r1(9216 + N * j, N) for j in range(3)] + [R2[:, 5632 + N * j:5632 + N * j + N] for j in (0,)] + [
            R2[:, 11264 + N * j:11264 + N * j + N] for j in range(2)]
        probsT = [v.rearrange("p (c n) -> p c n", c=NT) for v in
                  [xT_s[:, 0:NT * N]] + [r1(10368 + NT * N * j, NT * N) for j in range(H - 1)]]
        wbuf = [r1(3072 * j, 3072) for j in range(5)] + [R2[:, 7680 + 3072 * j:10752 + 3072 * j] for j in range(3)]
        w13 = [w[:, 0:2048].rearrange("p (k n) -> p k n", k=KD) for w in wbuf]
        w2e = [w[:, 2048:3072].rearrange("p (c n) -> p c n", c=2) for w in wbuf]
        ypick = [r1(4096 * j, 4096) for j in range(NT)]
        L1W = R2[:, 0:6144].rearrange("p (l k n) -> p l k n", l=3, k=KD)
        F2W2 = R2[:, 0:6144].rearrange("p (e c n) -> p e c n", e=E2, c=2)
        F2W1 = R2[:, 6144:12288].rearrange("p (e k n) -> p e k n", e=E2, k=KD)
        L2W = R2[:, 12288:14336].rearrange("p (k n) -> p k n", k=KD)
        L3S = R2[:, 14336:16384].rearrange("p (k n) -> p k n", k=KD)
        L3N = R2[:, 16384:18432].rearrange("p (k n) -> p k n", k=KD)
        gateW = R2[:, 18432:18688].rearrange("p (k n) -> p k n", k=KD)
        B0 = 6144
        V = R2[:, B0:B0 + 1536].rearrange("p (t d) -> p t d", t=NT)
        wu = R2[:, B0 + 1536:B0 + 2560]
        wd = R2[:, B0 + 2560:B0 + 3584]
        bvr = R2[:, B0 + 3584:B0 + 4096]
        g0r = R2[:, B0 + 4096:B0 + 4608]
        b0r = R2[:, B0 + 4608:B0 + 5120]
        bwr = R2[:, B0 + 5120:B0 + 6144]
        oh = R2[:, 0:768].bitcast(bf16).rearrange("p (b s n) -> p b s n", b=2, s=2)
        attT = R1[:, 0:1536].rearrange("p (k n) -> p k n", k=KD)
        war = R2[:, 768:896]
        bar = R2[:, 896:897]
        y0 = R2[:, 1024:2560].rearrange("p (t d) -> p t d", t=NT)
        ye = R2[:, 2560:4096].rearrange("p (t d) -> p t d", t=NT)
        yr = R2[:, 4096:5632].rearrange("p (t d) -> p t d", t=NT)
        xws = WK[:, 0:1536].rearrange("p (t d) -> p t d", t=NT)
        gT = WK[:, 1536:3072].rearrange("p (k n) -> p k n", k=KD)
        y6 = R2[:, 12288:13824].rearrange("p (t d) -> p t d", t=NT)
        ye7 = R2[:, 4096:5632].rearrange("p (t d) -> p t d", t=NT)
        hid = [WK[:, 768 * j:768 * j + 768].rearrange("p (c n) -> p c n", c=2) for j in range(2)]
        xg = [R2[:, D * j:D * j + D] for j in range(NXG)]
        xeT = [R2[:, 3072 + D * j:3072 + D * j + D].rearrange("p (k n) -> p k n", k=KD) for j in range(2)]
        act = [R2[:, 4096 + F3 * j:4096 + F3 * j + F3] for j in range(2)]
        hmid = [R2[:, 4608 + F3 * j:4608 + F3 * j + F3] for j in range(2)]
        hT = [R2[:, 5120 + F3 * j:5120 + F3 * j + F3] for j in range(2)]
        ysb = [R2[:, 5632 + D * j:5632 + D * j + D] for j in range(NYB)]

        b2r, b3r, g3r, be3r = (rows[:, D * j:D * j + D] for j in range(4))
        bcol = [cols[:, KD * j:KD * j + KD] for j in range(7)]

        xq = WK[:, 0:768].bitcast(bf16).rearrange("p (t d) -> p t d", t=NT)
        xqT = WK[:, 768:1536].bitcast(bf16).rearrange("p (k n) -> p k n", k=KD)
        hb = WK[:, 1536:2304].rearrange("p (t f) -> p t f", t=NT)
        hq = WK[:, 2304:2688].bitcast(bf16).rearrange("p (t f) -> p t f", t=NT)
        hqT = WK[:, 2688:3072].bitcast(bf16).rearrange("p (c n) -> p c n", c=2)
        hr, hd = (xT_s[:, 768 * j:768 * j + 768].rearrange("p (t f) -> p t f", t=NT) for j in range(2))
        wuq = wq[:, 0:1024].rearrange("p (k n) -> p k n", k=KD)
        wdq = wq[:, 1024:2048].rearrange("p (c n) -> p c n", c=2)
        wg_s = sb("wg_s", KD * E2)
        wg = wg_s[:, :].rearrange("p (k n) -> p k n", k=KD)
        first_rec = sb("first_rec", NT * EF * 4)
        first_rec4 = first_rec[:, :].rearrange("p (t e c) -> p t e c", t=NT, e=EF)
        first_slot = sb("first_slot", EF * 4, i32)
        first_slot3 = first_slot[:, :].rearrange("p (e c) -> p e c", e=EF)
        tri8 = sb("tri8", G3 * G3)
        te = "p (t e) -> p t e"
        scores8, biased, masked, replaced, selw, place = (
            WK[:, o:o + NT * E3].rearrange(te, t=NT) for o in (0, 192, 704, 896, 1088, 1280))
        top_in_group = WK[:, 384:576].rearrange("p (g m) -> p g m", m=8)
        beats, ties = WK[:, 576:640], WK[:, 640:704]
        scr64 = WK[:, 1472:1536]
        picked = WK[:, 1536:1632].bitcast(bf16).rearrange(te, t=NT)
        place1 = WK[:, 1688:1688 + NT * EF].rearrange("p (t e) -> p t e", t=NT)
        kth_s = WK[:, 1728:1728 + NT * EF * K3]
        kth = kth_s.rearrange("p (t e k) -> p t e k", t=NT, e=EF)
        first_oh = R2[:, 4096:4096 + NT * EF * P].rearrange("p (e t n) -> p e t n", e=EF, t=NT)
        pick_row_f = WK[:, 1632:1656]
        pick_row = WK[:, 1664:1688].bitcast(i32)
        pb = [ctx.enter_context(nc.psum_tensor(f"bank{j}", [P, 512], f32)) for j in range(8)]

        pbh = [b[:, :].bitcast(bf16) for b in pb]
        sq_scr = pb[7][:, 0:N]

        small = {}
        used = [0]

        def V_(name, n):
            if name not in small:
                small[name] = sm[:, used[0]:used[0] + n]
                used[0] += n
                assert used[0] <= 1024
            return small[name]

        xin, srcd, dstd = a["x"], a["src"], a["dst"]
        tiles = "(t p) d -> p t d"
        chunks = "(k p) n -> p k n"
        def rest(eng, one_expert, after=None):
            eng.wait_ge(S("most_ready"), 1)
            fullest = eng.value_load(most[0:1, 0:1], min_val=0, max_val=N)
            with eng.If(fullest > P):
                for s in range(1, NT):
                    with eng.Fori(0, E3) as e:
                        one_expert(eng, s, e, e + (E3 * (s - 1) + 1))
                if after is not None:
                    after()

        block = ctx.enter_context(nc.Block())

        @block.sync
        def _(sp):
            sp.dma_start(x3, xin.rearrange(tiles, p=P)).then_inc(S("x_loaded"), 16)
            sp.dma_start(src_i, srcd.rearrange("(p t) -> p t", p=P)).then_inc(S("edges_loaded"), 16)
            sp.dma_start(dst_i, dstd.rearrange("(p t) -> p t", p=P)).then_inc(S("edges_loaded"), 16)
            ww = a["L0_Ww"].rearrange("(c p) n -> p c n", p=P)
            sp.dma_start(Ww[:, 0:4, :], ww[:, 0:4, :]).then_inc(S("Ww_loaded_src"), 16)
            sp.dma_start(Ww[:, 4:8, :], ww[:, 4:8, :]).then_inc(S("Ww_loaded_dst"), 16)
            for row, name in ((bwr, "L0_bw"), (bvr, "L0_bv"), (g0r, "L0_gamma"), (b0r, "L0_beta"),
                              (war, "L0_Wa"), (bar, "L0_ba")):
                sp.dma_start(row, a[name].partition_broadcast(P)).then_inc(S("rows0_loaded"), 16)
            sp.dma_start(Wv, a["L0_Wv"].rearrange(chunks, p=P)).then_inc(S("Wv_loaded"), 16)
            sp.dma_start(wu.rearrange("p (k n) -> p k n", k=KD), a["L1_wu"].rearrange(chunks, p=P)).then_inc(S("bit_w_loaded"), 16)
            sp.dma_start(wd.rearrange("p (k n) -> p k n", k=2), a["L1_wd"].rearrange(chunks, p=P)).then_inc(S("bit_w_loaded"), 16)
            sp.wait_ge(S("no_edge_ready"), 1)
            fill = score.rearrange("n h -> (n h)").rearrange("(q p c) -> q p c", p=P, c=1024)
            for q in range(9):
                sp.dma_start(fill[q], ga[0][:, 0:1024]).then_inc(S("score_filled"), 16)
            sp.wait_ge(S("no_token_ready"), 4)
            slots = slot_tab.rearrange("(s p e) c -> s p (e c)", s=NT, p=P)
            for q in range(NT):
                sp.dma_start(slots[q], slot0[:, :]).then_inc(S("slots_filled"), 16)
            for t in range(NT):
                sp.wait_ge(S("src_rows_ready"), t + 1)
                sp.dma_start(tab_src[P * t:P * t + P, :], ab[0]).then_inc(S("src_rows_stored"), 16)
                sp.wait_ge(S("dst_rows_ready"), t + 1)
                sp.dma_start(tab_dst[P * t:P * t + P, :], ab[1]).then_inc(S("dst_rows_stored"), 16)
            sp.wait_ge(S("V_ready"), NT)
            for j in range(2):
                sp.wait_ge(S(f"scores_stored{j}"), 8 * ET)
            for i in range(NT):
                sp.dma_start(mt[i], score[N * P * i:N * P * (i + 1), :].rearrange("(p n) h -> p n h", p=P)).then_inc(S(f"read_back{i}"), 16)
            for j, name in enumerate(("L2_b", "L3_bias", "L3_gamma", "L3_beta")):
                sp.dma_start(rows[:, D * j:D * j + D], a[name].partition_broadcast(P)).then_inc(S("rows_loaded"), 16)
            sp.dma_start(gateb[:, :], a["L3_gate_b"].partition_broadcast(P)).then_inc(S("rows_loaded"), 16)
            sp.dma_start(wg, a["L2_w_gating"].rearrange(chunks, p=P)).then_inc(S("wg_loaded"), 16)
            sp.dma_start(cols[:, :], a["fcols"]).then_inc(S("rows_loaded"), 16)
            sp.dma_start(L2W, a["L2_W"].rearrange(chunks, p=P)).then_inc(S("L2W_loaded"), 16)
            sp.dma_start(L3S, a["L3_self"].rearrange(chunks, p=P)).then_inc(S("L3W_loaded"), 16)
            sp.dma_start(L3N, a["L3_neigh"].rearrange(chunks, p=P)).then_inc(S("L3W_loaded"), 16)
            sp.dma_start(gateW, a["L3_gate_w"].rearrange(chunks, p=P)).then_inc(S("gateW_loaded"), 16)
            sp.wait_ge(S("x_ready"), NT * 0 + NT)
            for l in range(3):
                sp.dma_start(L1W[:, l], a[f"L1_W{l}"].rearrange(chunks, p=P)).then_inc(S(f"L1W{l}_loaded"), 16)
            sp.dma_start(F2W1, a["L2_w1"].rearrange("e (k p) n -> p e k n", p=P)).then_inc(S("F2W1_loaded"), 16)

            def load_expert(e):
                j = e % NWB
                for c, name in enumerate(("L3_w1", "L3_w3")):
                    sp.dma_start(w13[j][:, :, F3 * c:F3 * c + F3], a[name][e].rearrange(chunks, p=P)).then_inc(S(f"expert_w{j}"), 16)
                sp.dma_start(w2e[j], a["L3_w2"][e].rearrange("(c p) n -> p c n", p=P)).then_inc(S(f"expert_w{j}"), 16)

            for e in range(5):
                load_expert(e)
            sp.wait_ge(S("h_out_psum"), NT)
            sp.dma_start(F2W2, a["L2_w2"].rearrange("e (c p) n -> p e c n", p=P)).then_inc(S("F2W2_loaded"), 16)
            sp.wait_ge(S("x_ready"), NT * 7)
            for e in range(5, NWB):
                load_expert(e)
            for t in range(NT):
                sp.wait_ge(S("xn_ready"), nth("8", t + 1))
                sp.dma_start(tok_tab[P * t:P * t + P, :], xn3[:, t]).then_inc(S("tokens_stored"), 16)
            for e in range(NWB, E3):
                if e == EF + 4:
                    sp.wait_ge(S("slots_written"), 16 * NT * K3)
                    sp.dma_start(slot0[:, :], slots[0]).then_inc(S("slot0_loaded"), 16)
                sp.wait_ge(S("y_psum"), e - NWB + 1)
                if e - 4 >= EF:
                    sp.wait_ge(S(f"tokens_gathered{(e - 4) % NXG}"), 16 * ((e - 4) // NXG + 1))
                load_expert(e)
            sp.wait_ge(S("y_psum"), E3)

            def load_rest(sp, s, e, nth_):
                sp.wait_ge(S("rest_turn"), nth_)
                sp.dma_start(rest_rec[:, :], slot_tab.rearrange("(s p e) c -> s p e c", s=NT, p=P)[s, :, bass.ds(e, 1), :]).then_inc(S("rest_loaded"), 16)
                for c, name in enumerate(("L3_w1", "L3_w3")):
                    sp.dma_start(w13[0][:, :, F3 * c:F3 * c + F3], a[name][bass.ds(e, 1)].rearrange("e (k p) n -> p (e k) n", p=P)).then_inc(S("rest_loaded"), 16)
                sp.dma_start(w2e[0], a["L3_w2"][bass.ds(e, 1)].rearrange("e (c p) n -> p (e c) n", p=P)).then_inc(S("rest_loaded"), 16)

            rest(sp, load_rest, lambda: sp.wait_ge(S("rest_turn"), E3 * (NT - 1) + 1))
            for j in range(NYB):
                sp.wait_ge(S(f"picks_stored{j}"), 16 * len(range(j, E3, NYB)))
            sp.wait_ge(S("y_psum"), E3)
            for t in range(NT):
                sp.dma_start(ypick[t], pick_out[P * K3 * t:P * K3 * (t + 1), :].rearrange("(p k) d -> p (k d)", k=K3)).then_inc(S(f"read_back{t}"), 16)
            for t in range(NT):
                sp.wait_ge(S("x_ready"), NT * 7 + t + 1)
                sp.dma_start(out[P * t:P * t + P, :], x3[:, t]).then_inc(S("out_stored"), 16)
            sp.wait_ge(S("out_stored"), 16 * NT)

        @block.gpsimd
        def _(pool):
            done = [0]

            def step(ins):
                done[0] += 1
                ins.then_inc(S("pool_step"), 1)
                pool.wait_ge(S("pool_step"), done[0])

            imprecise = dict(allow_small_or_imprecise_dtypes=True)
            pool.memset(ga[0], NEG).then_inc(S("no_edge_ready"), 1)
            step(pool.memset(ident[:, :], 0.0))
            step(pool.affine_select(out=ident[:, :], in_=ident[:, :], compare_op=ALU.not_equal, fill=1.0, base=0,
                                    pattern=[[-1, P]], channel_multiplier=1))
            step(pool.memset(ones[:, :], 1.0))
            step(pool.affine_select(out=tri[:, :], in_=ones[:, :], compare_op=ALU.is_gt, fill=0.0, base=0,
                                    pattern=[[-1, P]], channel_multiplier=1))
            step(pool.affine_select(out=trib[:, :], in_=ones[:, :], compare_op=ALU.is_gt, fill=0.0, base=0,
                                    pattern=[[1, P]], channel_multiplier=-1))
            step(pool.tensor_copy(identb[:, :], ident[:, :]))
            step(pool.tensor_copy(onesb[:, :], ones[:, :]))
            step(pool.iota(iota_h[:, :], pattern=[[1, N]], base=0, channel_multiplier=0, **imprecise))
            step(pool.iota(iota64[:, :], pattern=[[1, E3]], base=0, channel_multiplier=0, **imprecise))
            step(pool.iota(fall48[:, :], pattern=[[0, 3], [-1, 16]], base=16, channel_multiplier=0, **imprecise))
            step(pool.memset(tri8[:, :], 1.0))
            t8 = tri8[:, :].rearrange("p (g m) -> p g m", g=G3)
            step(pool.affine_select(out=t8, in_=t8, compare_op=ALU.is_gt, fill=0.0, base=0,
                                    pattern=[[1, G3], [-1, G3]], channel_multiplier=0))
            s4 = slot0[:, :].rearrange("p (e c) -> p e c", c=4)
            for c, value in enumerate((N, N * K3, 0, 0)):
                pool.memset(s4[:, :, c], value).then_inc(S("no_token_ready"), 1)
            step(pool.memset(rec[:, :], 0))
            step(pool.iota(first_rec4[:, :, :, 0], pattern=[[P, NT], [0, EF]], base=-N, channel_multiplier=1, **imprecise))
            step(pool.iota(first_rec4[:, :, :, 1], pattern=[[P * K3, NT], [0, EF]], base=-N * K3, channel_multiplier=K3, **imprecise))
            step(pool.memset(V_("zero", 1), 0.0))
            step(pool.iota(rec4[:, :, :, 0], pattern=[[P, NT], [0, K3]], base=0, channel_multiplier=1))
            pool.iota(rec4[:, :, :, 1], pattern=[[P * K3, NT], [1, K3]], base=0, channel_multiplier=K3).then_inc(S("consts_ready"), 1)

            pool.wait_ge(S("edge_idx_ready"), 1)
            pool.wait_ge(S("score_filled"), 16 * 9)
            pool.wait_ge(S("src_rows_stored"), 16 * NT)

            def gather_src(t):
                j = t % NGA
                if t >= NGA:
                    pool.wait_ge(S("w_ready"), t - NGA + 1)
                pool.indirect_dma_start(out=ga[j], out_offset=None, in_=tab_src[:, :],
                                        in_offset=bass.IndirectOffsetOnAxis(ap=src_i[:, t:t + 1], axis=0)).then_inc(S(f"edge_rows{j}"), 16)

            def add_dst(t):
                j = t % NGA
                pool.wait_ge(S(f"edge_rows{j}"), 32 * (t // NGA) + 16)
                pool.indirect_dma_start(out=ga[j], out_offset=None, in_=tab_dst[:, :],
                                        in_offset=bass.IndirectOffsetOnAxis(ap=dst_i[:, t:t + 1], axis=0),
                                        compute_op=ALU.add).then_inc(S(f"edge_rows{j}"), 16)

            def scatter_score(t):
                pool.wait_ge(S("w_ready"), t + 1)
                if t >= 2:
                    pool.wait_ge(S(f"scores_stored{t % 2}"), 16 * (t // 2))
                pool.indirect_dma_start(out=score[:, :], out_offset=bass.IndirectOffsetOnAxis(ap=row_i[:, t:t + 1], axis=0),
                                        in_=w_e3[:, t, :], in_offset=None, bounds_check=N * N - 1,
                                        oob_is_err=False).then_inc(S(f"scores_stored{t % 2}"), 16)

            for t in range(3):
                gather_src(t)
            pool.wait_ge(S("dst_rows_stored"), 16 * NT)
            for t in range(ET):
                if t + 3 < ET:
                    gather_src(t + 3)
                add_dst(t)
                if t >= 3:
                    scatter_score(t - 3)
            for t in range(ET - 3, ET):
                scatter_score(t)
            pool.wait_ge(S("shifter_in_ready"), 1)
            for t in range(NT):
                pool.tensor_tensor(out=x3[:, t, :], in0=x3[:, t, :], in1=xn3[:, t, :], op=ALU.add).then_inc(S("shifter_added"), 1)
            pool.wait_ge(S("x6_done"), 1)
            for j in range(NXG):
                pool.memset(xg[j], 0.0).then_inc(S("xg_cleared"), 1)
            pool.wait_ge(S("tokens_stored"), 16 * NT)
            pool.wait_ge(S("xg_cleared"), NXG)

            def slots_of(e):
                return first_slot3 if e < EF else s4

            def gather_tokens(e):
                j = e % NXG
                if e >= NXG:
                    pool.wait_ge(S("xe_psum"), e - NXG + 1)
                pool.indirect_dma_start(out=xg[j], out_offset=None, in_=tok_tab[:, :],
                                        in_offset=bass.IndirectOffsetOnAxis(ap=slots_of(e)[:, e, 0:1], axis=0),
                                        bounds_check=N - 1, oob_is_err=False).then_inc(S(f"tokens_gathered{j}"), 16)

            def scatter_picks(e):
                j = e % NYB
                pool.wait_ge(S("ye_ready"), e + 1)
                pool.indirect_dma_start(out=pick_out[:, :], out_offset=bass.IndirectOffsetOnAxis(ap=slots_of(e)[:, e, 1:2], axis=0),
                                        in_=ysb[j], in_offset=None, bounds_check=N * K3 - 1,
                                        oob_is_err=False).then_inc(S(f"picks_stored{j}"), 16)

            def scatter_records(t, k):
                if t == 0 and k == 0:
                    pool.wait_ge(S("slots_filled"), 16 * NT)
                if k == 0:
                    pool.wait_ge(S("picks_ready"), t + 1)
                c = t * K3 + k
                pool.indirect_dma_start(out=slot_tab[:, :], out_offset=bass.IndirectOffsetOnAxis(ap=pick_row[:, c:c + 1], axis=0),
                                        in_=rec4[:, t, k, :], in_offset=None).then_inc(S("slots_written"), 16)

            pool.wait_ge(S("first_slots_ready"), 1)
            for e in range(4):
                if e % 2 == 0:
                    pool.wait_ge(S("first_slots_ready"), e // 2 + 1)
                gather_tokens(e)
            for t in range(NT):
                for k in range(K3):
                    scatter_records(t, k)
                    if t == 1 and k == 5 or t == 2 and k == 3:
                        scatter_picks(t - 1)
                        gather_tokens(t + 5)
                if t == 0:
                    pool.wait_ge(S("first_slots_ready"), 3)
                    gather_tokens(4)
                    gather_tokens(5)
            scatter_picks(2)
            gather_tokens(8)
            pool.wait_ge(S("slot0_loaded"), 16)
            for e in range(EF, E3):
                gather_tokens(e)
                scatter_picks(e - NXG)
            for e in range(E3 - NXG, E3):
                scatter_picks(e)

            def hold(j):
                return pool.tensor_tensor(out=V_("held", 3)[:, j:j + 1], in0=V_("zero", 1), in1=V_("zero", 1), op=ALU.add)

            def move_rest(pool, s, e, nth_):
                pool.wait_ge(S("rest_loaded"), nth_ * 64)
                hold(0)
                pool.indirect_dma_start(out=xg[0], out_offset=None, in_=tok_tab[:, :],
                                        in_offset=bass.IndirectOffsetOnAxis(ap=rest_rec[:, 0:1], axis=0),
                                        bounds_check=N - 1, oob_is_err=False).then_inc(S("rest_gathered"), 16)
                pool.wait_ge(S("rest_evacuated"), nth_ * 4)
                hold(1)
                pool.indirect_dma_start(out=pick_out[:, :], out_offset=bass.IndirectOffsetOnAxis(ap=rest_rec[:, 1:2], axis=0),
                                        in_=ysb[0], in_offset=None, bounds_check=N * K3 - 1,
                                        oob_is_err=False).then_inc(S("rest_stored"), 16)
                pool.wait_ge(S("rest_stored"), nth_ * 16)
                hold(2).then_inc(S("rest_turn"), 1)

            for j in range(NYB):
                pool.wait_ge(S(f"picks_stored{j}"), 16 * len(range(j, E3, NYB)))
            pool.wait_ge(S("xe_psum"), E3)
            hold(2).then_inc(S("rest_turn"), 1)
            rest(pool, move_rest)


        @block.tensor
        def _(pe):
            def transposes(norm, t, src=xn3):
                pe.wait_ge(S("xn_ready"), nth(norm, t + 1))
                for k in range(KD):
                    last = pe.transpose(pb[t][:, P * k:P * k + P], src[:, t, P * k:P * k + P], ident[:, :])
                return last

            def project(t, bank, lhsT, rhs, cols_=slice(0, 512), chunks_=range(KD)):
                for k in chunks_:
                    last = pe.matmul(pb[bank][:, cols_], lhsT[:, k, P * t:P * t + P], rhs[:, k, :],
                                     start=(k == chunks_[0]), stop=(k == chunks_[-1]))
                return last

            pe.wait_ge(S("consts_ready"), 1)
            for t in range(NT):
                transposes("1", t).then_inc(S("xT_psum"), 1)
            pe.wait_ge(S("edge_h_ready"), 1)
            for t in range(NT):
                for b in range(4):
                    half = b % 2
                    rows_ready = S("src_half_ready") if b < 2 else S("dst_half_ready")
                    if t == 0 and half == 0:
                        pe.wait_ge(S("Ww_loaded_src") if b < 2 else S("Ww_loaded_dst"), 16)
                    if b == 3 and t == 0:
                        pe.wait_ge(S("xT_ready"), nth("1", NT))
                    pe.wait_ge(S("xT_ready"), nth("1", t + 1))
                    if t:
                        pe.wait_ge(rows_ready, 2 * (t - 1) + half + 1)
                    w = Ww[:, 4 * (b // 2):4 * (b // 2) + 4, D * half:D * half + D]
                    project(t, (3, 4, 5, 0)[b], xT, w).then_inc(S("src_rows_psum") if b < 2 else S("dst_rows_psum"), 1)
            pe.wait_ge(S("Wv_loaded"), 16)
            pe.wait_ge(S("src_half_ready"), 2 * NT)
            pe.wait_ge(S("dst_half_ready"), 2 * NT)
            for e in range(ET):
                if e % 4 == 0:
                    g = e // 4
                    if g >= 2:
                        pe.wait_ge(S("dup_used"), g)
                    for j in range(4):
                        o = pb[6 + g % 2][:, P * j:P * j + P]
                        pe.matmul(o, src_h[:, e + j:e + j + 1].to_broadcast([P, P]), ident16[:, 0:P], start=True, stop=False)
                        last = pe.matmul(o, dst_h[:, e + j:e + j + 1].to_broadcast([P, P]), ident16[:, P:2 * P], start=False, stop=True)
                    last.then_inc(S("key_psum"), 1)
                if e % 4 == 2 and e // 4 < NT:
                    project(e // 4, 3 + e // 4, xT, Wv).then_inc(S("V_psum"), 1)
                pe.wait_ge(S("onehot_ready"), e + 1)
                for s in range(NT):
                    last = pe.matmul(pb[s][:, 0:N], oh[:, e % 2, 0, P * s:P * s + P], oh[:, e % 2, 1, :],
                                     start=(e == 0), stop=(e == ET - 1))
                last.then_inc(S("onehot_used"), 1)
            pe.wait_ge(S("cnt_ready"), 1)
            pe.wait_ge(S("dup_used"), 12)
            for t in range(NT):
                for s in range(NT):
                    pe.matmul(pb[6][:, t:t + 1], cnt[:, s, P * t:P * t + P], ones[:, 0:1], start=(s == 0), stop=(s == NT - 1))
            for s in range(NT):
                pe.matmul(pb[7][:, 0:N], ones[:, :], cnt[:, s, :], start=(s == 0), stop=(s == NT - 1))
            pe.wait_ge(S("bit_abs_ready"), 2)
            pe.matmul(pb[6][:, 8:10], ones[:, :], V_("wabs", 2), start=True, stop=True).then_inc(S("deg_psum"), 1)
            pe.wait_ge(S("V_ready"), NT)

            def transpose_probs(u):
                i, h = divmod(u, H)
                pe.wait_ge(S("probs_ready"), u + 1)
                if u >= 3:
                    pe.wait_ge(S("probsT_ready"), u - 2)
                for c in range(NT):
                    last = pe.transpose(pb[u % 3][:, P * c:P * c + P], probs[u % NPR][:, P * c:P * c + P], ident[:, :])
                last.then_inc(S("probsT_psum"), 1)

            def attend(h):
                pe.wait_ge(S("probsT_ready"), H * (NT - 1) + h + 1)
                if h >= 3:
                    pe.wait_ge(S("attended_ready"), h - 2)
                pair = h // 2
                for c in range(NT):
                    last = pe.matmul(pb[3 + h % 3][:, 0:N], V[:, c, P * pair:P * pair + P], probsT[h][:, c, :],
                                     start=(c == 0), stop=(c == NT - 1))
                last.then_inc(S("attended_psum"), 1)

            for u in range(H * (NT - 1) + 1):
                transpose_probs(u)
            for h in range(H):
                if h + 1 < H:
                    transpose_probs(H * (NT - 1) + h + 1)
                attend(h)
            pe.wait_ge(S("attended_ready"), H)
            for t in range(NT):
                if t == 0:
                    pe.wait_ge(S("probsT_ready"), NT * H)
                for k in range(KD):
                    last = pe.transpose(pb[t][:, P * k:P * k + P], attT[:, k, P * t:P * t + P], ident[:, :])
                last.then_inc(S("attended_back"), 1)

            for t in range(NT):
                transposes("3", t).then_inc(S("xT_psum"), 1)
            for l in range(3):
                pe.wait_ge(S(f"L1W{l}_loaded"), 16)
                for t in range(NT):
                    if l == 0:
                        pe.wait_ge(S("xT_ready"), nth("3", t + 1))
                    for k in range(KD):
                        if l:
                            pe.wait_ge(S("hT_ready"), KD * (l - 1) + k + 1)
                        last = pe.matmul(pb[3 + t][:, :], xT[:, k, P * t:P * t + P], L1W[:, l, k, :], start=(k == 0), stop=(k == KD - 1))
                    last.then_inc(S("hw_psum"), 1)
                pe.wait_ge(S("hw_ready"), NT * (l + 1))
                for k in range(KD):
                    for s in range(NT):
                        last = pe.matmul(pb[(0, 1, 2, 6)[k]][:, 0:N], xws[:, s, P * k:P * k + P], cntI[:, s, :],
                                         start=(s == 0), stop=(s == NT - 1))
                    last.then_inc(S("agg_psum"), 1)
            for t in range(NT):
                pe.wait_ge(S("hT_ready"), 3 * KD)
                for k in range(KD):
                    last = pe.transpose(pb[3 + t][:, P * k:P * k + P], xT[:, k, P * t:P * t + P], ident[:, :])
                last.then_inc(S("h_out_psum"), 1)

            for t in range(NT):
                pe.wait_ge(S("xq_ready"), t + 1)
                for k in range(KD):
                    last = pe.transpose(pbh[t][:, P * k:P * k + P], xq[:, t, P * k:P * k + P], identb[:, :])
                last.then_inc(S("xqT_psum"), 1)
            pe.wait_ge(S("wq_ready"), 2)
            for t in range(NT):
                pe.wait_ge(S("xqT_ready"), t + 1)
                if t == 0:
                    pe.wait_ge(S("x_ready"), NT * 2 + NT)
                for k in range(KD):
                    last = pe.matmul(pb[3 + t][:, 0:F1], xqT[:, k, P * t:P * t + P], wuq[:, k, :], start=(k == 0), stop=(k == KD - 1))
                last.then_inc(S("up_bit_psum"), 1)
            for t in range(NT):
                pe.wait_ge(S("hq_ready"), t + 1)
                for c in range(2):
                    last = pe.transpose(pbh[t][:, P * c:P * c + P], hq[:, t, P * c:P * c + P], identb[:, :])
                last.then_inc(S("hqT_psum"), 1)
            for t in range(NT):
                pe.wait_ge(S("hqT_ready"), t + 1)
                for c in range(2):
                    last = pe.matmul(pb[3 + t][:, :], hqT[:, c, P * t:P * t + P], wdq[:, c, :], start=(c == 0), stop=(c == 1))
                last.then_inc(S("down_bit_psum"), 1)

            for t in range(NT):
                transposes("5", t).then_inc(S("xT_psum"), 1)
            pe.wait_ge(S("L2W_loaded"), 16)
            pe.wait_ge(S("x_ready"), NT * 3 + NT)
            for t in range(NT):
                pe.wait_ge(S("xT_ready"), nth("5", t + 1))
                project(t, 3 + t, xT, L2W).then_inc(S("hw5_psum"), 1)
            pe.wait_ge(S("hw5_ready"), NT)
            for t in range(NT):
                for s in range(NT):
                    last = pe.matmul(pb[t][:, :], cntI[:, s, P * t:P * t + P], xws[:, s, :], start=(s == 0), stop=(s == NT - 1))
                last.then_inc(S("agg5_psum"), 1)

            pe.wait_ge(S("rows_loaded"), 96)
            pe.wait_ge(S("wg_loaded"), 16)
            for t in range(NT):
                if t == 0:
                    pe.wait_ge(S("x_ready"), NT * 4 + NT)
                transposes("6", t).then_inc(S("xT_psum"), 1)
            for t in range(NT):
                pe.wait_ge(S("xT_ready"), nth("6", t + 1))
                for k in range(KD):
                    last = pe.matmul(pb[6][:, 8 * t:8 * t + E2], xT[:, k, P * t:P * t + P], wg[:, k, :], start=(k == 0), stop=(k == KD - 1))
            last.then_inc(S("gate6_psum"), 1)
            for t in range(NT):
                transposes("6b", t, y6).then_inc(S("xT_psum"), 1)
            pe.wait_ge(S("F2W1_loaded"), 16)
            pe.wait_ge(S("xT_ready"), nth("6b", NT))

            def hidden6(e):
                for c in range(2):
                    j = 2 * e + c
                    if j >= 3:
                        pe.wait_ge(S("hid6_ready"), j - 2)
                    for k in range(KD):
                        last = pe.matmul(pb[j % 3][:, 0:N], F2W1[:, e, k, P * c:P * c + P], xT[:, k, :], start=(k == 0), stop=(k == KD - 1))
                    last.then_inc(S("hid6_psum"), 1)

            hidden6(0)
            for e in range(E2):
                if e + 1 < E2:
                    hidden6(e + 1)
                if e == 0:
                    pe.wait_ge(S("F2W2_loaded"), 16)
                pe.wait_ge(S("hid6_ready"), 2 * e + 2)
                for t in range(NT):
                    j = NT * e + t
                    if j >= 4:
                        pe.wait_ge(S("out6_used"), j - 3)
                    for c in range(2):
                        last = pe.matmul(pb[(3, 4, 5, 7)[j % 4]][:, :], hid[e % 2][:, c, P * t:P * t + P], F2W2[:, e, c, :], start=(c == 0), stop=(c == 1))
                    last.then_inc(S("out6_psum"), 1)

            for t in range(NT):
                transposes("7", t).then_inc(S("xT_psum"), 1)
            pe.wait_ge(S("gate_done6"), 1)
            for k in range(KD):
                for s in range(NT):
                    last = pe.matmul(pb[3 + k][:, 0:N], xn3[:, s, P * k:P * k + P], cnt[:, s, :], start=(s == 0), stop=(s == NT - 1))
                last.then_inc(S("neigh_psum"), 1)
            pe.wait_ge(S("L3W_loaded"), 32)
            pe.wait_ge(S("xT_ready"), nth("7", NT))
            for t in range(NT):
                for k in range(KD):
                    pe.matmul(pb[t][:, :], xT[:, k, P * t:P * t + P], L3S[:, k, :], start=(k == 0), stop=False)
                for k in range(KD):
                    pe.wait_ge(S("neighT_ready"), k + 1)
                    last = pe.matmul(pb[t][:, :], gT[:, k, P * t:P * t + P], L3N[:, k, :], start=False, stop=(k == KD - 1))
                last.then_inc(S("sage_psum"), 1)

            for t in range(NT):
                if t == 0:
                    pe.wait_ge(S("sage_used"), NT)
                transposes("8", t).then_inc(S("xT_psum"), 1)
            pe.wait_ge(S("gateW_loaded"), 16)
            for t in range(NT):
                pe.wait_ge(S("xT_ready"), nth("8", t + 1))
                for k in range(KD):
                    last = pe.matmul(pb[3][:, E3 * t:E3 * t + E3], xT[:, k, P * t:P * t + P], gateW[:, k, :], start=(k == 0), stop=(k == KD - 1))
            last.then_inc(S("logits_psum"), 1)
            pe.wait_ge(S("picked_ready"), 1)
            for t in range(NT):
                for s in range(t + 1):
                    last = pe.matmul(pb[4][:, E3 * t:E3 * t + E3], (trib if s == t else onesb)[:, :], picked[:, s, :], start=(s == 0), stop=(s == t))
            for s in range(NT):
                last = pe.matmul(pb[4][:, E3 * NT:E3 * NT + E3], onesb[:, :], picked[:, s, :], start=(s == 0), stop=(s == NT - 1))
            last.then_inc(S("place_psum"), 1)
            def first_slots(lo, hi):
                for e in range(lo, hi):
                    pe.wait_ge(S("first_onehot"), NT * (e + 1))
                    for t in range(NT):
                        last = pe.matmul(pb[5][:, 4 * e:4 * e + 3], first_oh[:, e, t, :], first_rec4[:, t, e, 0:3], start=(t == 0), stop=(t == NT - 1))
                    last.then_inc(S("first_slots_psum"), 1)

            def transpose_tokens(e):
                pe.wait_ge(S(f"tokens_gathered{e % NXG}"), 16 * (e // NXG + 1))
                if e >= 2:
                    pe.wait_ge(S("xeT_ready"), e - 1)
                for k in range(KD):
                    last = pe.transpose(pb[e % 2][:, P * k:P * k + P], xg[e % NXG][:, P * k:P * k + P], ident[:, :])
                last.then_inc(S("xe_psum"), 1)

            def up(e):
                pe.wait_ge(S(f"expert_w{e % NWB}"), 48 * (e // NWB + 1))
                pe.wait_ge(S("xeT_ready"), e + 1)
                if e >= 2:
                    pe.wait_ge(S("hmid_ready"), e - 1)
                for k in range(KD):
                    last = pe.matmul(pb[2 + e % 2][:, :], xeT[e % 2][:, k, :], w13[e % NWB][:, k, :], start=(k == 0), stop=(k == KD - 1))
                last.then_inc(S("up_psum"), 1)

            def transpose_hidden(e):
                pe.wait_ge(S("hmid_ready"), e + 1)
                if e >= 2:
                    pe.wait_ge(S("hT8_ready"), e - 1)
                for c in range(2):
                    last = pe.transpose(pb[4 + e % 2][:, P * c:P * c + P], hmid[e % 2][:, P * c:P * c + P], ident[:, :])
                last.then_inc(S("hT_psum"), 1)

            def down(e):
                pe.wait_ge(S("hT8_ready"), e + 1)
                if e >= 2:
                    pe.wait_ge(S("ye_ready"), e - 1)
                for c in range(2):
                    last = pe.matmul(pb[6 + e % 2][:, :], hT[e % 2][:, P * c:P * c + P], w2e[e % NWB][:, c, :], start=(c == 0), stop=(c == 1))
                last.then_inc(S("y_psum"), 1)

            first_slots(0, 4)
            transpose_tokens(0)
            for e in range(E3 + 1):
                if e + 1 < E3:
                    transpose_tokens(e + 1)
                if e >= 1:
                    transpose_hidden(e - 1)
                if e < E3:
                    up(e)
                if e == 0:
                    first_slots(4, EF)
                if e >= 1:
                    down(e - 1)

            def multiply_rest(pe, s, e, nth_):
                pe.wait_ge(S("rest_gathered"), nth_ * 16)
                for k in range(KD):
                    last = pe.transpose(pb[0][:, P * k:P * k + P], xg[0][:, P * k:P * k + P], ident[:, :])
                last.then_inc(S("rest_psum"), 1)
                pe.wait_ge(S("rest_evacuated"), nth_ * 4 - 3)
                for k in range(KD):
                    last = pe.matmul(pb[2][:, :], xeT[0][:, k, :], w13[0][:, k, :], start=(k == 0), stop=(k == KD - 1))
                last.then_inc(S("rest_psum"), 1)
                pe.wait_ge(S("rest_hmid"), nth_)
                for c in range(2):
                    last = pe.transpose(pb[4][:, P * c:P * c + P], hmid[0][:, P * c:P * c + P], ident[:, :])
                last.then_inc(S("rest_psum"), 1)
                pe.wait_ge(S("rest_evacuated"), nth_ * 4 - 1)
                for c in range(2):
                    last = pe.matmul(pb[6][:, :], hT[0][:, P * c:P * c + P], w2e[0][:, c, :], start=(c == 0), stop=(c == 1))
                last.then_inc(S("rest_psum"), 1)

            pe.wait_ge(S("ye_ready"), E3)
            rest(pe, multiply_rest)

        @block.scalar
        def _(act_):
            def copy_T(norm, t):
                act_.wait_ge(S("xT_psum"), nth(norm, t + 1))
                act_.activation(xT[:, :, P * t:P * t + P], pb[t][:, :].rearrange("p (k n) -> p k n", k=KD), ACT.Copy).then_inc(S("xT_ready"), 1)

            rooted = [0]

            def roots(*values):
                rooted[0] += 1
                act_.wait_ge(S("root_asked"), rooted[0])
                for n_, (o, v, plus) in enumerate(values):
                    last = act_.activation(o, v, ACT.Sqrt, bias=plus)
                    if n_ < len(values) - 1:
                        last.then_inc(S("early_roots"), 1)
                if len(values) > 1:
                    act_.wait_ge(S("early_roots"), len(values) - 1)
                last.then_inc(S("root_ready"), 1)

            def row_roots():
                roots((V_("rstd", 3), V_("mv", 6).rearrange("p (t c) -> p t c", t=NT)[:, :, 1], LN_EPS))

            row_roots()
            for t in range(NT):
                copy_T("1", t)
            for t in range(NT):
                for half in range(2):
                    act_.wait_ge(S("src_rows_psum"), 2 * t + half + 1)
                    if t and half == 0:
                        act_.wait_ge(S("src_rows_stored"), 16 * t)
                    act_.activation(ab[0][:, D * half:D * half + D], pb[3 + half][:, :], ACT.Copy).then_inc(S("src_half_ready"), 1)
            for u in range(NT * H):
                i, h = divmod(u, H)
                act_.wait_ge(S("row_max_ready"), i + 1)
                if u >= NPR:
                    act_.wait_ge(S("probsT_psum"), u - NPR + 1)
                act_.activation(probs[u % NPR], mt[i][:, :, h], ACT.Exp, bias=V_("nmax", 24)[:, u:u + 1],
                                accum_out=V_("psum_", 24)[:, u:u + 1]).then_inc(S("probs_ready"), 1)
            dv = V_("dis", 3), V_("dinv", 3), dinv_bc[:, :]
            roots(*((v, v, 1.0) for v in dv))
            for h in range(H):
                act_.wait_ge(S("attended_psum"), h + 1)
                own = slice(HD * (h % 2), HD * (h % 2) + HD)
                act_.activation(attT[own, h // 2, :], pb[3 + h % 3][own, 0:N], ACT.Copy).then_inc(S("attended_ready"), 1)
            for t in range(NT):
                act_.wait_ge(S("ymin_ready"), t + 1)
                act_.activation(ye[:, t], ye[:, t], ACT.Exp).then_inc(S("yexp_ready"), 1)
            row_roots()
            row_roots()
            row_roots()
            for t in range(NT):
                copy_T("3", t)
            for l in range(3):
                for k in range(KD):
                    act_.wait_ge(S("scaled_ready"), KD * l + k + 1)
                    act_.activation(gT[:, k, :], gT[:, k, :], ACT.Relu, bias=bcol[l][:, k:k + 1],
                                    accum_out=V_("gsum", 4)[:, k:k + 1]).then_inc(S("relu_ready"), 1)
                for k in range(KD):
                    act_.wait_ge(S("shift_ready"), KD * l + k + 1)
                    act_.activation(sq_scr[:, :], gT[:, k, :], ACT.Square, bias=V_("nshift", 4)[:, k:k + 1],
                                    accum_out=V_("gsq", 4)[:, k:k + 1]).then_inc(S("square_ready"), 1)
                    act_.wait_ge(S("square_ready"), KD * l + k + 1)
                roots((V_("gmul", 4), V_("gmul", 4), EPS))
            row_roots()
            for t in range(NT):
                act_.wait_ge(S("xqT_psum"), t + 1)
                act_.activation(xqT[:, :, P * t:P * t + P], pbh[t][:, 0:512].rearrange("p (k n) -> p k n", k=KD), ACT.Copy).then_inc(S("xqT_ready"), 1)
            for t in range(NT):
                act_.wait_ge(S("hqT_psum"), t + 1)
                act_.activation(hqT[:, :, P * t:P * t + P], pbh[t][:, 0:256].rearrange("p (k n) -> p k n", k=2), ACT.Copy).then_inc(S("hqT_ready"), 1)
            row_roots()
            for t in range(NT):
                copy_T("5", t)
            row_roots()
            for t in range(NT):
                copy_T("6", t)
            row_roots()
            act_.wait_ge(S("raw6_ready"), 1)
            for t in range(NT):
                act_.activation(V_("ex6", 24)[:, 8 * t:8 * t + E2], V_("raw6", 24)[:, 8 * t:8 * t + E2], ACT.Exp,
                                bias=V_("nm6", 3)[:, t:t + 1], accum_out=V_("es6", 3)[:, t:t + 1]).then_inc(S("ex6_ready"), 1)
            for t in range(NT):
                act_.wait_ge(S("xT_psum"), nth("6b", t + 1))
                act_.wait_ge(S("gate6_psum"), 1)
                for k in range(KD):
                    last = act_.activation(xT[:, k, P * t:P * t + P], pb[t][:, P * k:P * k + P], ACT.Copy, scale=bcol[6][:, k:k + 1])
                last.then_inc(S("xT_ready"), 1)
            for e in range(E2):
                for c in range(2):
                    j = 2 * e + c
                    act_.wait_ge(S("hid6_psum"), j + 1)
                    if e >= 2:
                        act_.wait_ge(S("out6_psum"), NT * (e - 1))
                    act_.activation(hid[e % 2][:, c, :], pb[j % 3][:, 0:N], ACT.Gelu).then_inc(S("hid6_ready"), 1)
            row_roots()
            for t in range(NT):
                copy_T("7", t)
            row_roots()
            row_roots()
            for t in range(NT):
                copy_T("8", t)
            act_.wait_ge(S("logits_psum"), 1)
            act_.activation(scores8[:, :, :], pb[3][:, 0:NT * E3].rearrange("p (t e) -> p t e", t=NT), ACT.Sigmoid).then_inc(S("sigmoid_ready"), 1)
            s4f = slot0[:, :].bitcast(f32).rearrange("p (e c) -> p e c", c=4)

            firstf = first_slot[:, :].bitcast(f32).rearrange("p (e c) -> p e c", e=EF)

            def copy_hT(e):
                act_.wait_ge(S("hT_psum"), e + 1)
                if e >= 2:
                    act_.wait_ge(S("y_psum"), e - 1)
                act_.activation(hT[e % 2], pb[4 + e % 2][:, 0:F3], ACT.Copy).then_inc(S("hT8_ready"), 1)

            def silu(e):
                act_.wait_ge(S("up_psum"), e + 1)
                if e >= 2:
                    act_.wait_ge(S("hmid_ready"), e - 1)
                act_.activation(act[e % 2], pb[2 + e % 2][:, 0:F3], ACT.Silu).then_inc(S("silu_ready"), 1)

            def weigh(e):
                act_.wait_ge(S("y_psum"), e + 1)
                if e == EF:
                    act_.wait_ge(S("slot0_loaded"), 16)
                if e >= NYB:
                    act_.wait_ge(S(f"picks_stored{e % NYB}"), 16 * (e // NYB))
                act_.activation(ysb[e % NYB], pb[6 + e % 2][:, :], ACT.Copy, scale=(firstf if e < EF else s4f)[:, e, 2:3]).then_inc(S("ye_ready"), 1)

            for e in range(E3 + 1):
                if e >= 1:
                    copy_hT(e - 1)
                if e < E3:
                    silu(e)
                if e >= 1:
                    weigh(e - 1)

            rest_w = rest_rec[:, 2:3].bitcast(f32)

            def evacuate_rest(act_, s, e, nth_):
                act_.wait_ge(S("rest_psum"), nth_ * 4 - 3)
                act_.activation(xeT[0], pb[0][:, :].rearrange("p (k n) -> p k n", k=KD), ACT.Copy).then_inc(S("rest_evacuated"), 1)
                act_.wait_ge(S("rest_psum"), nth_ * 4 - 2)
                act_.activation(act[0], pb[2][:, 0:F3], ACT.Silu).then_inc(S("rest_evacuated"), 1)
                act_.wait_ge(S("rest_psum"), nth_ * 4 - 1)
                act_.activation(hT[0], pb[4][:, 0:F3], ACT.Copy).then_inc(S("rest_evacuated"), 1)
                act_.wait_ge(S("rest_psum"), nth_ * 4)
                act_.activation(ysb[0], pb[6][:, :], ACT.Copy, scale=rest_w).then_inc(S("rest_evacuated"), 1)

            rest(act_, evacuate_rest)

        @block.vector
        def _(dve):
            issued = [0]

            def go(ins):
                issued[0] += 1
                return ins.then_inc(S("dve_step"), 1)

            def settle():
                dve.wait_ge(S("dve_step"), issued[0])

            def one(ins):
                go(ins)
                settle()

            def bc(ap, shape):
                return ap.to_broadcast(shape)

            ts, tt, stt = dve.tensor_scalar, dve.tensor_tensor, dve.scalar_tensor_tensor
            st = V_("st", 18).rearrange("p (t c) -> p t c", t=NT)
            mv = V_("mv", 6).rearrange("p (t c) -> p t c", t=NT)
            rstd = V_("rstd", 3)

            asked = [0]

            def roots(ins):
                asked[0] += 1
                ins.then_inc(S("root_asked"), 1)
                settle()
                dve.wait_ge(S("root_ready"), asked[0])

            def norm_into_x(y, scr, gamma, stage):
                settle()
                for t in range(NT):
                    last = dve.bn_aggr(mv[:, t, :], st[:, t, :])
                    if t < NT - 1:
                        go(last)
                roots(last)
                go(dve.reciprocal(rstd, rstd))
                for t in range(NT):
                    go(stt(scr[:, t, :], y[:, t, :], mv[:, t, 0:1], gamma, ALU.subtract, ALU.mult))
                settle()
                for t in range(NT):
                    stt(x3[:, t, :], scr[:, t, :], rstd[:, t:t + 1], x3[:, t, :], ALU.mult, ALU.add).then_inc(S("x_ready"), 1)
                dve.wait_ge(S("x_ready"), NT * stage + NT)

            def layernorm(src, dst, norm=None):
                for t in range(NT):
                    go(dve.bn_stats(st[:, t, :], src[:, t, :]))
                settle()
                for t in range(NT):
                    last = dve.bn_aggr(mv[:, t, :], st[:, t, :])
                    if t < NT - 1:
                        go(last)
                roots(last)
                one(dve.reciprocal(rstd, rstd))
                for t in range(NT):
                    ins = ts(dst[:, t, :], src[:, t, :], mv[:, t, 0:1], rstd[:, t:t + 1], ALU.subtract, ALU.mult)
                    if norm is None:
                        go(ins)
                    else:
                        ins.then_inc(S("xn_ready"), 1)
                if norm is None:
                    settle()
                else:
                    dve.wait_ge(S("xn_ready"), nth(norm, NT))

            dve.wait_ge(S("edges_loaded"), 32)
            go(dve.tensor_copy(src_f, src_i))
            go(dve.tensor_copy(dst_f, dst_i))
            go(dve.tensor_copy(src_h, src_i))
            go(dve.tensor_copy(dst_h, dst_i))
            settle()
            one(stt(key_f, src_f, float(N), dst_f, ALU.mult, ALU.add))
            dve.wait_ge(S("consts_ready"), 1)
            go(ts(ident16[:, 0:P], ident[:, :], float(N), None, ALU.mult))
            dve.tensor_copy(ident16[:, P:2 * P], ident[:, :]).then_inc(S("ident16_ready"), 1)
            settle()
            dve.wait_ge(S("ident16_ready"), 1)
            dve.engine_nop().then_inc(S("edge_h_ready"), 1)
            dve.engine_nop().then_inc(S("edge_idx_ready"), 1)
            dve.wait_ge(S("x_loaded"), 16)
            layernorm(x3, xn3, "1")
            dve.wait_ge(S("rows0_loaded"), 96)
            waL, waR = V_("waL", P), V_("waR", P)
            go(ts(waL, war, SLOPE, None, ALU.mult))
            go(ts(waR, war, 1.0 - SLOPE, None, ALU.mult))
            settle()
            heads = "p (h c) -> p h c"
            lsc3 = lsc.rearrange(heads, h=H)
            waL3 = bc(waL[:, None, :], [P, H, P])

            def linear_part(row, bias, ready):
                one(tt(lsc3, row[:, 0:2 * D].rearrange(heads, h=H), waL3, ALU.mult))
                one(dve.tensor_reduce(row[:, 2 * D:ROW], lsc3, AX, ALU.add))
                if bias is not None:
                    one(ts(row[:, 2 * D:ROW], row[:, 2 * D:ROW], bias, None, ALU.add))
                dve.engine_nop().then_inc(ready, 1)

            for t in range(NT):
                for b in range(4):
                    if b >= 2:
                        half = b - 2
                        dve.wait_ge(S("dst_rows_psum"), 2 * t + half + 1)
                        if t and half == 0:
                            dve.wait_ge(S("dst_rows_stored"), 16 * t)
                        tt(ab[1][:, D * half:D * half + D], pb[(5, 0)[half]][:, :], bwr[:, D * half:D * half + D], ALU.add).then_inc(S("dst_half_ready"), 1)
                    if b == 1:
                        dve.wait_ge(S("src_half_ready"), 2 * t + 2)
                        linear_part(ab[0], None, S("src_rows_ready"))
                    if b == 3:
                        dve.wait_ge(S("dst_half_ready"), 2 * t + 2)
                        linear_part(ab[1], bar, S("dst_rows_ready"))
            wabs, dup0_f = V_("wabs", 2), V_("dup0_f", ET // 4)
            for t in range(ET):
                if t >= 2:
                    dve.wait_ge(S("onehot_used"), t - 1)
                go(ts(oh[:, t % 2, 0, :], iota_h[:, :], src_f[:, t:t + 1], None, ALU.is_equal))
                ts(oh[:, t % 2, 1, :], iota_h[:, :], dst_f[:, t:t + 1], None, ALU.is_equal).then_inc(S("onehot_ready"), 1)
                settle()
                if t % 4 == 0:
                    g = t // 4
                    dve.wait_ge(S("key_psum"), g + 1)
                    keys = pb[6 + g % 2]
                    for j in range(4):
                        e = t + j
                        lo = P * (j - 1) if j else 0
                        go(stt(lsc[:, 256 * j:256 * j + P * (j + 1) - lo], keys[:, lo:P * (j + 1)], key_f[:, e:e + 1],
                               before_s[:, 0:2 * P] if j else tri, ALU.is_equal, ALU.mult, accum_out=dup_f[:, e:e + 1]))
                    if g:
                        go(stt(lsc[:, P:2 * P], pb[7 - g % 2][:, 3 * P:4 * P], key_f[:, t:t + 1], ones,
                               ALU.is_equal, ALU.mult, accum_out=dup0_f[:, g:g + 1]))
                        settle()
                        go(tt(dup_f[:, t:t + 1], dup_f[:, t:t + 1], dup0_f[:, g:g + 1], ALU.add))
                    settle()
                    stt(row_i[:, t:t + 4], dup_f[:, t:t + 4], 262144.0, key_f[:, t:t + 4], ALU.mult, ALU.add).then_inc(S("dup_used"), 1)
                    dve.wait_ge(S("dup_used"), g + 1)
                if t % 4 == 3 and t // 4 < NT:
                    v = t // 4
                    dve.wait_ge(S("V_psum"), v + 1)
                    tt(V[:, v, :], pb[3 + v][:, :], bvr, ALU.add).then_inc(S("V_ready"), 1)
                if t == 16:
                    dve.wait_ge(S("bit_w_loaded"), 32)
                    dve.tensor_reduce(wabs[:, 0:1], wu, AX, ALU.add, apply_absolute_value=True).then_inc(S("bit_abs_ready"), 1)
                    dve.tensor_reduce(wabs[:, 1:2], wd, AX, ALU.add, apply_absolute_value=True).then_inc(S("bit_abs_ready"), 1)
                j = t % NGA
                dve.wait_ge(S(f"edge_rows{j}"), 32 * (t // NGA + 1))
                for h in range(H):
                    go(stt(lsc[:, P * h:P * h + P], ga[j][:, P * h:P * h + P], 0.0, waR, ALU.max, ALU.mult,
                           accum_out=w_e3[:, t, h:h + 1]))
                settle()
                one(tt(w_e3[:, t, :], w_e3[:, t, :], ga[j][:, 2 * D:ROW], ALU.add))
                dve.engine_nop().then_inc(S("w_ready"), 1)
            dve.wait_ge(S("onehot_used"), ET)
            for s in range(NT):
                go(dve.tensor_copy(cnt[:, s, :], pb[s][:, 0:N]))
            settle()
            go(dve.tensor_copy(cntI_s[:, :], cnt_s[:, :]))
            outdeg = V_("outdeg", 3)
            go(dve.tensor_reduce(outdeg, cnt, AX, ALU.add))
            settle()
            for s in range(NT):
                go(tt(cntI[:, s, P * s:P * s + P], cntI[:, s, P * s:P * s + P], ident[:, :], ALU.add))
            settle()
            dve.engine_nop().then_inc(S("cnt_ready"), 1)
            for t in range(NT):
                go(ts(xn3[:, t, :], xn3[:, t, :], 1.0, None, ALU.subtract))
                go(tt(x3[:, t, :], x3[:, t, :], b0r, ALU.add))
            nmax, psum_ = V_("nmax", 24), V_("psum_", 24)
            dis, dinv, wsc, half_sc = V_("dis", 3), V_("dinv", 3), V_("wsc", 2), V_("half_sc", 4)

            def row_max(i):
                dve.wait_ge(S(f"read_back{i}"), 16)
                m = nmax[:, H * i:H * i + H]
                one(dve.tensor_reduce(m, mt[i].rearrange("p n h -> p h n"), AX, ALU.max))
                ts(m, m, NEG_FLOOR, -1.0, ALU.max, ALU.mult).then_inc(S("row_max_ready"), 1)

            def copy_probsT(i, h):
                u = H * i + h
                dve.wait_ge(S("probsT_psum"), u + 1)
                dve.tensor_copy(probsT[h][:, :, P * i:P * i + P], pb[u % 3][:, 0:N].rearrange("p (c n) -> p c n", c=NT)).then_inc(S("probsT_ready"), 1)

            row_max(0)
            row_max(1)
            for h in range(H):
                copy_probsT(0, h)
            row_max(2)
            for h in range(H):
                copy_probsT(1, h)
            copy_probsT(2, 0)
            dve.wait_ge(S("deg_psum"), 1)
            go(dve.tensor_copy(dis, outdeg))
            go(dve.tensor_copy(dinv, pb[6][:, 0:3]))
            asked[0] += 1
            dve.tensor_copy(dinv_bc[:, :], pb[7][:, 0:N]).then_inc(S("root_asked"), 1)
            copy_probsT(2, 1)
            go(ts(rdeg_bc[:, :], pb[7][:, 0:N], 1.0, None, ALU.max))
            go(ts(wsc, pb[6][:, 8:10], 1.0 / (D * F1), EPS, ALU.mult, ALU.max))
            settle()
            go(ts(half_sc[:, 0:2], wsc, 0.5, None, ALU.mult))
            go(ts(half_sc[:, 2:4], wsc, -0.5, None, ALU.mult))
            copy_probsT(2, 2)
            settle()
            for j, w in enumerate((wu, wd)):
                q = wq[:, 1024 * j:1024 * j + 1024]
                go(ts(q, w, half_sc[:, j:j + 1], None, ALU.is_gt))
                one(ts(w, w, half_sc[:, 2 + j:3 + j], None, ALU.is_lt))
                tt(q, q, w, ALU.subtract).then_inc(S("wq_ready"), 1)
                copy_probsT(2, 3 + j)
            copy_probsT(2, 5)
            dve.wait_ge(S("root_ready"), asked[0])
            go(dve.reciprocal(dis, dis))
            go(dve.reciprocal(dinv, dinv))
            go(dve.reciprocal(dinv_bc[:, :], dinv_bc[:, :]))
            copy_probsT(2, 6)
            settle()
            go(dve.reciprocal(rdeg_bc[:, :], rdeg_bc[:, :]))
            copy_probsT(2, 7)
            rs = V_("rs", 24)
            one(ts(rs, psum_, 1e-30, None, ALU.max))
            one(dve.reciprocal(rs, rs))
            for t in range(NT):
                dve.wait_ge(S("attended_back"), t + 1)
                one(tt(y0[:, t, :].rearrange(heads, h=H), pb[t][:, :].rearrange(heads, h=H), bc(rs[:, H * t:H * t + H, None], [P, H, HD]), ALU.mult))
                ts(ye[:, t, :], y0[:, t, :], 0.0, None, ALU.min).then_inc(S("ymin_ready"), 1)
                go(stt(yr[:, t, :], y0[:, t, :], 0.0, xn3[:, t, :], ALU.max, ALU.add))
            for t in range(NT):
                dve.wait_ge(S("yexp_ready"), t + 1)
                one(tt(y0[:, t, :], ye[:, t, :], yr[:, t, :], ALU.add))
                go(dve.bn_stats(st[:, t, :], y0[:, t, :]))
            norm_into_x(y0, yr, g0r, 0)

            layernorm(x3, xn3)
            dve.engine_nop().then_inc(S("shifter_in_ready"), 1)
            first = V_("first", 144).rearrange("p (t c) -> p t c", t=NT)
            for t in range(NT):
                go(stt(first[:, t, :], xn3[:, t, 64:112], 0.5, fall48[:, :], ALU.is_gt, ALU.mult))
            settle()
            far, idx = V_("far", 9), V_("idx", 9)
            one(dve.tensor_reduce(far, V_("first", 144).rearrange("p (c i) -> p c i", i=16), AX, ALU.max))
            one(ts(idx, far, -1.0, 16.0, ALU.mult, ALU.add))
            one(stt(idx, far, 0.0, idx, ALU.is_gt, ALU.mult))
            idx3 = idx.rearrange("p (t c) -> p t c", t=NT)
            idx_i = V_("idx_i", 9).bitcast(i32)
            one(dve.tensor_copy(idx_i, idx))
            ii = idx_i.rearrange("p (t c) -> p t c", t=NT)
            val, left, right = (V_(n_, 3).bitcast(i32) for n_ in ("val", "left", "right"))
            sa_i = V_("sa_i", 3).bitcast(i32)
            mark, shl, shr, both, amp = (V_(n_, 3) for n_ in ("mark", "shl", "shr", "both", "amp"))
            go(dve.tensor_copy(sa_i, ii[:, :, 2]))
            go(ts(mark, xn3[:, :, 0], 0.5, None, ALU.is_gt))
            go(ts(shl, xn3[:, :, 39], 0.5, None, ALU.is_gt))
            go(ts(shr, xn3[:, :, 40], 0.5, None, ALU.is_gt))
            one(ts(val, ii[:, :, 1], 4, None, ALU.logical_shift_left))
            one(tt(val, val, ii[:, :, 0], ALU.bitwise_or))
            go(tt(left, val, sa_i, ALU.logical_shift_left))
            go(tt(right, val, sa_i, ALU.logical_shift_right))
            go(tt(both, shl, shr, ALU.mult))
            settle()
            go(tt(shr, shr, both, ALU.subtract))
            go(tt(shl, shl, mark, ALU.mult))
            go(ts(left, left, 255, None, ALU.bitwise_and))
            settle()
            go(tt(shr, shr, mark, ALU.mult))
            leftf, rightf, res = (V_(n_, 3) for n_ in ("leftf", "rightf", "res"))
            go(dve.tensor_copy(leftf, left))
            go(dve.tensor_copy(rightf, right))
            settle()
            go(tt(leftf, leftf, shl, ALU.mult))
            go(tt(rightf, rightf, shr, ALU.mult))
            go(tt(amp, shl, shr, ALU.add))
            settle()
            go(tt(res, leftf, rightf, ALU.add))
            go(ts(amp, amp, 2.0, None, ALU.mult))
            settle()
            one(dve.tensor_copy(val, res))
            go(ts(left, val, 15, None, ALU.bitwise_and))
            go(ts(right, val, 4, None, ALU.logical_shift_right))
            settle()
            rlo, rhi = V_("rlo", 3), V_("rhi", 3)
            go(dve.tensor_copy(rlo, left))
            go(dve.tensor_copy(rhi, right))
            settle()
            for t in range(NT):
                for o, nib in ((0, rlo), (16, rhi)):
                    go(ts(first[:, t, o:o + 16], iota64[:, 0:16], nib[:, t:t + 1], amp[:, t:t + 1], ALU.is_equal, ALU.mult))
            settle()
            dve.wait_ge(S("shifter_added"), NT)
            tt(x3[:, :, 128:160], x3[:, :, 128:160], first[:, :, 0:32], ALU.add).then_inc(S("x_ready"), NT)
            dve.wait_ge(S("x_ready"), NT * 1 + NT)

            layernorm(x3, xn3, "3")
            dve.wait_ge(S("rows_loaded"), 96)
            nshift, gsum, gsq, gmul, gadd = (V_(n_, 4) for n_ in ("nshift", "gsum", "gsq", "gmul", "gadd"))
            for l in range(3):
                for t in range(NT):
                    dve.wait_ge(S("hw_psum"), NT * l + t + 1)
                    if l and t == 0:
                        dve.wait_ge(S("agg_psum"), KD * l)
                    ts(xws[:, t, :], pb[3 + t][:, :], dinv[:, t:t + 1], None, ALU.mult).then_inc(S("hw_ready"), 1)
                for k in range(KD):
                    dve.wait_ge(S("agg_psum"), KD * l + k + 1)
                    tt(gT[:, k, :], pb[(0, 1, 2, 6)[k]][:, 0:N], dinv_bc[:, :], ALU.mult).then_inc(S("scaled_ready"), 1)
                for k in range(KD):
                    dve.wait_ge(S("relu_ready"), KD * l + k + 1)
                    stt(nshift[:, k:k + 1], gsum[:, k:k + 1], -1.0 / N, bcol[5][:, k:k + 1], ALU.mult, ALU.mult).then_inc(S("shift_ready"), 1)
                dve.wait_ge(S("square_ready"), KD * (l + 1))
                roots(ts(gmul, gsq, 1.0 / N, None, ALU.mult))
                one(dve.reciprocal(gmul, gmul))
                one(tt(gmul, gmul, bcol[3], ALU.mult))
                one(tt(gadd, nshift, gmul, ALU.mult))
                one(tt(gadd, gadd, bcol[4], ALU.add))
                for k in range(KD):
                    ts(xT[:, k, :], gT[:, k, :], gmul[:, k:k + 1], gadd[:, k:k + 1], ALU.mult, ALU.add).then_inc(S("hT_ready"), 1)
            for t in range(NT):
                dve.wait_ge(S("h_out_psum"), t + 1)
                tt(x3[:, t, :], x3[:, t, :], pb[3 + t][:, :], ALU.add).then_inc(S("x_ready"), 1)
            dve.wait_ge(S("x_ready"), NT * 2 + NT)

            layernorm(x3, xn3)
            amax, xsc, isc, amax2, hsc = (V_(n_, 3) for n_ in ("amax", "xsc", "isc", "amax2", "hsc"))

            def quantise(v3, m, scale, q3, top_ready, f):
                one(dve.tensor_reduce(m, v3, AX, ALU.max, apply_absolute_value=True))
                one(ts(m, m, EPS, None, ALU.max))
                one(dve.reciprocal(scale, m))
                one(ts(scale, scale, 127.0, None, ALU.mult))
                for t in range(NT):
                    go(ts(v3[:, t, :], v3[:, t, :], scale[:, t:t + 1], ROUND, ALU.mult, ALU.add))
                settle()
                for t in range(NT):
                    go(ts(v3[:, t, :], v3[:, t, :], ROUND, 127.0, ALU.subtract, ALU.min))
                settle()
                for t in range(NT):
                    ts(q3[:, t, :], v3[:, t, :], -128.0, None, ALU.max).then_inc(top_ready, 1)

            quantise(xn3, amax, xsc, xq, S("xq_ready"), D)
            one(dve.reciprocal(isc, xsc))
            one(ts(isc, isc, wsc[:, 0:1], None, ALU.mult))
            for t in range(NT):
                dve.wait_ge(S("up_bit_psum"), t + 1)
                go(ts(hb[:, t, :], pb[3 + t][:, 0:F1], isc[:, t:t + 1], 0.0, ALU.mult, ALU.max))
            settle()
            hb2 = WK[:, 1536:2304]
            hr2, hd2 = xT_s[:, 0:768], xT_s[:, 768:1536]
            one(ts(hr2, hb2, ROUND, None, ALU.add))
            one(ts(hr2, hr2, ROUND, 127.0, ALU.subtract, ALU.min))
            one(tt(hd2, hr2, hb2, ALU.subtract))
            one(tt(hb2, hb2, hd2, ALU.add))
            quantise(hb, amax2, hsc, hq, S("hq_ready"), F1)
            one(dve.reciprocal(isc, hsc))
            one(ts(isc, isc, wsc[:, 1:2], None, ALU.mult))
            for t in range(NT):
                dve.wait_ge(S("down_bit_psum"), t + 1)
                stt(x3[:, t, :], pb[3 + t][:, :], isc[:, t:t + 1], x3[:, t, :], ALU.mult, ALU.add).then_inc(S("x_ready"), 1)
            dve.wait_ge(S("x_ready"), NT * 3 + NT)

            layernorm(x3, xn3, "5")
            for t in range(NT):
                dve.wait_ge(S("hw5_psum"), t + 1)
                one(tt(xws[:, t, :], pb[3 + t][:, :], b2r, ALU.add))
                ts(xws[:, t, :], xws[:, t, :], dis[:, t:t + 1], None, ALU.mult).then_inc(S("hw5_ready"), 1)
            for t in range(NT):
                dve.wait_ge(S("agg5_psum"), t + 1)
                one(ts(xn3[:, t, :], pb[t][:, :], dis[:, t:t + 1], 0.0, ALU.mult, ALU.max))
                tt(x3[:, t, :], x3[:, t, :], xn3[:, t, :], ALU.add).then_inc(S("x_ready"), 1)
            dve.wait_ge(S("x_ready"), NT * 4 + NT)

            layernorm(x3, xn3, "6")
            dve.wait_ge(S("gate6_psum"), 1)
            raw6, nm6, ex6, es6 = V_("raw6", 24), V_("nm6", 3), V_("ex6", 24), V_("es6", 3)
            t8_ = "p (t e) -> p t e"
            one(dve.tensor_copy(raw6.rearrange(t8_, t=NT)[:, :, 0:E2], pb[6][:, 0:24].rearrange(t8_, t=NT)[:, :, 0:E2]))
            go(dve.memset(ex6, -1.0))
            one(dve.tensor_reduce(nm6, raw6.rearrange(t8_, t=NT)[:, :, 0:E2], AX, ALU.max, negate=True))
            dve.engine_nop().then_inc(S("raw6_ready"), 1)
            layernorm(xn3, y6, "6b")
            dve.wait_ge(S("ex6_ready"), NT)
            one(dve.reciprocal(es6, es6))
            top6, gm6, den6 = V_("top6", 24), V_("gm6", 24), V_("den6", 3)
            for t in range(NT):
                e8 = ex6[:, 8 * t:8 * t + 8]
                one(ts(e8, e8, es6[:, t:t + 1], None, ALU.mult))
                one(dve.max(top6[:, 8 * t:8 * t + 8], e8))
                one(dve.max_index(smi[:, 8 * t:8 * t + 8], top6[:, 8 * t:8 * t + 8], e8))
                one(tt(den6[:, t:t + 1], top6[:, 8 * t:8 * t + 1], top6[:, 8 * t + 1:8 * t + 2], ALU.add))
                one(ts(den6[:, t:t + 1], den6[:, t:t + 1], 1e-9, None, ALU.add))
                one(dve.reciprocal(den6[:, t:t + 1], den6[:, t:t + 1]))
                one(tt(den6[:, t:t + 1], den6[:, t:t + 1], top6[:, 8 * t:8 * t + 1], ALU.mult))
                go(dve.tensor_copy(idx[:, t:t + 1], smi[:, 8 * t:8 * t + 1]))
                settle()
                one(ts(gm6[:, 8 * t:8 * t + 8], iota64[:, 0:8], idx[:, t:t + 1], den6[:, t:t + 1], ALU.is_equal, ALU.mult))
            for e in range(E2):
                for t in range(NT):
                    j = NT * e + t
                    dve.wait_ge(S("out6_psum"), j + 1)
                    stt(x3[:, t, :], pb[(3, 4, 5, 7)[j % 4]][:, :], gm6[:, 8 * t + e:8 * t + e + 1], x3[:, t, :],
                        ALU.mult, ALU.add).then_inc(S("out6_used"), 1)
                    dve.wait_ge(S("out6_used"), j + 1)
            for t in range(NT):
                dve.engine_nop().then_inc(S("x_ready"), 1)
            dve.engine_nop().then_inc(S("x6_done"), 1)

            layernorm(x3, xn3, "7")
            dve.engine_nop().then_inc(S("gate_done6"), 1)
            for t in range(NT):
                go(tt(x3[:, t, :], x3[:, t, :], be3r, ALU.add))
            for k in range(KD):
                dve.wait_ge(S("neigh_psum"), k + 1)
                tt(gT[:, k, :], pb[3 + k][:, 0:N], rdeg_bc[:, :], ALU.mult).then_inc(S("neighT_ready"), 1)
            for t in range(NT):
                dve.wait_ge(S("sage_psum"), t + 1)
                tt(y6[:, t, :], pb[t][:, :], b3r, ALU.add).then_inc(S("sage_used"), 1)
            dve.wait_ge(S("sage_used"), NT)
            for t in range(NT):
                go(dve.bn_stats(st[:, t, :], y6[:, t, :]))
            norm_into_x(y6, ye7, g3r, 6)

            layernorm(x3, xn3, "8")
            dve.wait_ge(S("sigmoid_ready"), 1)
            one(tt(biased, scores8, bc(gateb[:, None, :], [P, NT, E3]), ALU.add))
            b2 = WK[:, 192:384]
            for g in range(NT * G3):
                go(dve.max(top_in_group[:, g, :], b2[:, 8 * g:8 * g + 8]))
            settle()
            gsc, rank = V_("gsc", 24), V_("rank", 24)
            one(tt(gsc, top_in_group[:, :, 0], top_in_group[:, :, 1], ALU.add))
            be, ti = (v.rearrange("p (g m) -> p g m", g=G3) for v in (beats, ties))
            for t in range(NT):
                g8 = gsc[:, G3 * t:G3 * t + G3]
                other, own = bc(g8[:, None, :], [P, G3, G3]), bc(g8[:, :, None], [P, G3, G3])
                go(tt(be, other, own, ALU.is_gt))
                one(tt(ti, other, own, ALU.is_equal))
                one(tt(ties, ties, tri8[:, :], ALU.mult))
                one(tt(beats, beats, ties, ALU.add))
                one(dve.tensor_reduce(rank[:, G3 * t:G3 * t + G3], be, AX, ALU.add))
            one(ts(rank, rank, float(TOPG), 1e30, ALU.is_ge, ALU.mult))
            grp = "p (g m) -> p g m"
            one(tt(WK[:, 704:896].rearrange(grp, m=8), b2.rearrange(grp, m=8), bc(rank[:, :, None], [P, NT * G3, 8]), ALU.subtract))
            top8, idx8f = V_("top8", 24), V_("idx8f", 24)
            for t in range(NT):
                v8 = top8[:, 8 * t:8 * t + 8]
                one(dve.max(v8, masked[:, t, :]))
                go(dve.max_index(smi[:, 8 * t:8 * t + 8], v8, masked[:, t, :]))
                go(dve.match_replace(replaced[:, t, :], v8, masked[:, t, :], NEG))
            settle()
            go(dve.tensor_copy(idx8f, smi[:, 0:24]))
            go(ts(WK[:, 1088:1280], WK[:, 896:1088], -2e38, None, ALU.is_lt))
            settle()
            dve.tensor_copy(WK[:, 1536:1632].bitcast(bf16), WK[:, 1088:1280]).then_inc(S("picked_ready"), 1)
            one(tt(WK[:, 1088:1280], WK[:, 1088:1280], WK[:, 0:192], ALU.mult))
            wsum = V_("wsum", 3)
            one(dve.tensor_reduce(wsum, selw, AX, ALU.add))
            one(dve.reciprocal(wsum, wsum))
            for t in range(NT):
                go(ts(selw[:, t, :], selw[:, t, :], wsum[:, t:t + 1], ROUTED_SCALE, ALU.mult, ALU.mult))
            settle()
            id3 = idx8f.rearrange("p (t k) -> p t k", t=NT)
            for t in range(NT):
                go(tt(kth[:, t], bc(id3[:, t, None, :], [P, EF, K3]), bc(iota64[:, 0:EF, None], [P, EF, K3]), ALU.is_equal))
            settle()
            for t in range(NT):
                go(tt(kth[:, t], kth[:, t], bc(iota64[:, None, 0:K3], [P, EF, K3]), ALU.mult))
            settle()
            kcol = V_("kcol", NT * EF)
            one(dve.tensor_reduce(kcol, kth_s.rearrange("p (c k) -> p c k", k=K3), AX, ALU.add))
            go(tt(first_rec4[:, :, :, 1], first_rec4[:, :, :, 1], kcol.rearrange("p (t e) -> p t e", t=NT), ALU.add))
            go(dve.tensor_copy(first_rec4[:, :, :, 2], selw[:, :, 0:EF]))
            dve.wait_ge(S("place_psum"), 1)
            ps4 = pb[4][:, 0:E3 * NT].rearrange("p (t e) -> p t e", t=NT)
            one(stt(place1, ps4[:, :, 0:EF], 1.0, picked[:, :, 0:EF], ALU.add, ALU.mult))

            def onehots(lo, hi):
                for e in range(lo, hi):
                    for t in range(NT):
                        ts(first_oh[:, e, t, :], iota_h[:, 1:P + 1], place1[:, t, e:e + 1], None, ALU.is_equal).then_inc(S("first_onehot"), 1)

            def first_slots(lo, hi):
                dve.wait_ge(S("first_slots_psum"), hi)
                v = pb[5][:, 0:4 * EF].rearrange("p (e c) -> p e c", e=EF)[:, lo:hi]
                go(ts(first_slot3[:, lo:hi, 0], v[:, :, 0], float(N), None, ALU.add))
                go(ts(first_slot3[:, lo:hi, 1], v[:, :, 1], float(N * K3), None, ALU.add))
                dve.tensor_copy(first_slot[:, :].bitcast(f32).rearrange("p (e c) -> p e c", e=EF)[:, lo:hi, 2], v[:, :, 2]).then_inc(S("first_slots_ready"), 1)

            def copy_xeT(e):
                dve.wait_ge(S("xe_psum"), e + 1)
                if e >= 2:
                    dve.wait_ge(S("up_psum"), e - 1)
                dve.tensor_copy(R2[:, 3072 + D * (e % 2):3072 + D * (e % 2) + D], pb[e % 2][:, :]).then_inc(S("xeT_ready"), 1)

            def gate_hidden(e):
                dve.wait_ge(S("silu_ready"), e + 1)
                if e >= 2:
                    dve.wait_ge(S("hT_psum"), e - 1)
                tt(hmid[e % 2], act[e % 2], pb[2 + e % 2][:, F3:2 * F3], ALU.mult).then_inc(S("hmid_ready"), 1)

            onehots(0, 2)
            for t in range(NT):
                go(stt(place[:, t, :], pb[4][:, E3 * t:E3 * t + E3], float(E3), iota64[:, :], ALU.mult, ALU.add))
            first_slots(0, 2)
            onehots(2, 4)
            first_slots(2, 4)
            copy_xeT(0)
            onehots(4, EF)
            settle()
            one(dve.tensor_reduce(V_("most", 1), pb[4][:, E3 * NT:E3 * NT + E3], AX, ALU.max))
            dve.tensor_copy(most[:, :], V_("most", 1)).then_inc(S("most_ready"), 1)
            recf = rec[:, :].bitcast(f32).rearrange("p (t k c) -> p t k c", t=NT, k=K3)

            def picks(t):
                for k in range(K3):
                    c = K3 * t + k
                    o = 128 * k
                    go(stt(xT_s[:, o:o + E3], iota64[:, :], idx8f[:, c:c + 1], place[:, t, :], ALU.is_equal, ALU.mult, accum_out=pick_row_f[:, c:c + 1]))
                    go(stt(xT_s[:, o + E3:o + 2 * E3], iota64[:, :], idx8f[:, c:c + 1], selw[:, t, :], ALU.is_equal, ALU.mult, accum_out=recf[:, t, k, 2:3]))
                settle()
                dve.tensor_copy(pick_row[:, K3 * t:K3 * t + K3], pick_row_f[:, K3 * t:K3 * t + K3]).then_inc(S("picks_ready"), 1)

            for e in range(E3):
                if e < NT:
                    picks(e)
                if e + 1 < E3:
                    copy_xeT(e + 1)
                gate_hidden(e)
                if e == 0:
                    first_slots(4, EF)

            def gate_rest(dve, s, e, nth_):
                dve.wait_ge(S("rest_evacuated"), nth_ * 4 - 2)
                tt(hmid[0], act[0], pb[2][:, F3:2 * F3], ALU.mult).then_inc(S("rest_hmid"), 1)

            rest(dve, gate_rest)
            for t in range(NT):
                dve.wait_ge(S(f"read_back{t}"), 32)
                y = ypick[t]
                for w in (4, 2, 1):
                    one(tt(y[:, 0:D * w], y[:, 0:D * w], y[:, D * w:2 * D * w], ALU.add))
                tt(x3[:, t, :], x3[:, t, :], y[:, 0:D], ALU.add).then_inc(S("x_ready"), 1)


def kernel(x, src, dst, **w):
    import numpy as np
    import concourse.bacc as bacc
    from concourse.bass_utils import run_bass_kernel_spmd as run

    def col(v):
        return np.asarray(v).reshape(KD, P).T

    g = {k: np.asarray(v) for k, v in w.items()}
    arrays = {
        "x": np.asarray(x), "src": np.asarray(src), "dst": np.asarray(dst),
        "L0_Ww": g["L0_gnn_Ww"], "L0_bw": g["L0_gnn_bw"], "L0_Wv": g["L0_gnn_Wv"], "L0_bv": g["L0_gnn_bv"],
        "L0_gamma": g["L0_gnn_gamma"], "L0_beta": g["L0_gnn_beta"], "L0_Wa": g["L0_gnn_Wa"].reshape(-1), "L0_ba": g["L0_gnn_ba"],
        "L1_W0": g["L1_gnn_W0"], "L1_W1": g["L1_gnn_W1"], "L1_W2": g["L1_gnn_W2"],
        "L1_wu": g["L1_ffn_w_up"].T, "L1_wd": g["L1_ffn_w_down"].T,
        "L2_W": g["L2_gnn_W"].T, "L2_b": g["L2_gnn_b"],
        "L2_w_gating": g["L2_ffn_w_gating"], "L2_w1": g["L2_ffn_w1"], "L2_w2": g["L2_ffn_w2"],
        "L3_self": g["L3_gnn_W_self"].T, "L3_neigh": g["L3_gnn_W_neigh"].T,
        "L3_bias": g["L3_gnn_bias"], "L3_gamma": g["L3_gnn_gamma"], "L3_beta": g["L3_gnn_beta"],
        "L3_gate_w": g["L3_ffn_gate_w"].T, "L3_gate_b": g["L3_ffn_gate_b"],
        "L3_w1": g["L3_ffn_w1"], "L3_w3": g["L3_ffn_w3"], "L3_w2": g["L3_ffn_w2"],
        "fcols": np.concatenate([col(g[k]) for k in (
            "L1_gnn_b0", "L1_gnn_b1", "L1_gnn_b2", "L1_gnn_gn_weight", "L1_gnn_gn_bias", "L1_gnn_gn_mean_scale",
            "L2_ffn_gamma")], axis=1),
    }
    arrays = {k: np.ascontiguousarray(v) for k, v in arrays.items()}
    nc = bacc.Bacc("TRN2", target_bir_lowering=False, num_devices=1)
    ins = {k: nc.dram_tensor(k, v.shape, mybir.dt.from_np(v.dtype), kind="ExternalInput").ap() for k, v in arrays.items()}
    out = nc.dram_tensor("out", (N, D), f32, kind="ExternalOutput").ap()
    build(nc, ins, out)
    r = run(nc, [arrays], core_ids=[0])
    return r.results[0]["out"]
```

```python
from contextlib import ExitStack

import concourse.bass as bass
from concourse import mybir

N = 384
D = 512
E = 6144
P = 128
NT = N // P
KD = D // P
ET = E // P
H = 8
HD = D // H
HW = 2 * HD
F1 = 256
E2, F2 = 6, 256
E3, F3 = 64, 256
G3, TOPG, K3 = 8, 4, 8
ROUTED_SCALE = 2.5
LN_EPS = 1e-5
EPS = 1e-5
NEG = -3.0e38
NEG_FLOOR = -1.0e37
ROUND = 1.5 * 2.0 ** 23
SLOPE = 0.01
ROW = 2 * D + H
NGA = 6
NWB = 8
NYB = 4
EF = 9
NPR = 6
NXG = 6

f32 = mybir.dt.float32
bf16 = mybir.dt.bfloat16
f16 = mybir.dt.float16
i32 = mybir.dt.int32
u32 = mybir.dt.uint32
SRC_PART = (slice(0, P * (NT - 1)), slice(P * (NT - 1), N))
NORMS = ("1", "3", "5", "6", "6b", "7", "8")


def nth(norm, tiles):
    return NT * NORMS.index(norm) + tiles


ALU = mybir.AluOpType
ACT = mybir.ActivationFunctionType
AX = mybir.AxisListType.X


def build(nc, a, out):
    ctx = ExitStack()
    with ctx:
        def sb(name, cols, dt=f32):
            return ctx.enter_context(nc.sbuf_tensor(name, [P, cols], dt))

        sems = {}

        def S(name):
            if name not in sems:
                sems[name] = ctx.enter_context(nc.semaphore(name))
            return sems[name]

        tab_src = nc.dram_tensor("tab_src", (N, ROW), f32, kind="Internal").ap()
        tab_dst = nc.dram_tensor("tab_dst", (N, ROW), f32, kind="Internal").ap()
        score = nc.dram_tensor("score", (N * N, H), f32, kind="Internal").ap()
        tok_tab = nc.dram_tensor("tok_tab", (N, D), f32, kind="Internal").ap()
        slot_tab = nc.dram_tensor("slot_tab", (N * E3, 4), i32, kind="Internal").ap()
        pick_out = nc.dram_tensor("pick_out", (N * K3, D), f32, kind="Internal").ap()

        R1 = sb("R1", 18432)
        R2 = sb("R2", 18688)
        WK = R1[:, 15360:18432]
        x_s = sb("x_s", NT * D)
        xn_s = sb("xn_s", NT * D)
        xT_s = sb("xT_s", KD * N)
        cnt_s = sb("cnt_s", NT * N)
        cntI_s = sb("cntI_s", NT * N)
        rows = sb("rows", 4 * D)
        cols = sb("cols", 28)
        gateb = sb("gateb", E3)
        ident = sb("ident", P)
        ident16 = sb("ident16", 2 * P, f16)
        identb = sb("identb", P, bf16)
        onesb = sb("onesb", P, bf16)
        before_s = sb("before_s", 2 * P)
        ones, tri = before_s[:, 0:P], before_s[:, P:2 * P]
        trib = sb("trib", P, bf16)
        iota_h = sb("iota_h", N, f16)
        iota64 = sb("iota64", E3)
        fall48 = sb("fall48", 48)
        wq = sb("wq", 2 * KD * F1, bf16)
        dinv_bc = sb("dinv_bc", N)
        rdeg_bc = sb("rdeg_bc", N)
        e_i = sb("e_i", 3 * ET, i32)
        e_f = sb("e_f", 4 * ET)
        e_h = sb("e_h", 2 * ET, f16)
        w_e = sb("w_e", ET * H)
        slot0 = sb("slot0", E3 * 4, i32)
        rest_rec = sb("rest_rec", 4, i32)
        most = sb("most", 1, i32)
        rec = sb("rec", NT * K3 * 4, i32)
        sm = sb("sm", 1024)
        smi = sb("smi", 32, u32)

        x3 = x_s[:, :].rearrange("p (t d) -> p t d", t=NT)
        xn3 = xn_s[:, :].rearrange("p (t d) -> p t d", t=NT)
        xT = xT_s[:, :].rearrange("p (k n) -> p k n", k=KD)
        cnt = cnt_s[:, :].rearrange("p (t n) -> p t n", t=NT)
        cntI = cntI_s[:, :].rearrange("p (t n) -> p t n", t=NT)
        src_i, dst_i, row_i = (e_i[:, j * ET:(j + 1) * ET] for j in range(3))
        src_f, dst_f, key_f, dup_f = (e_f[:, j * ET:(j + 1) * ET] for j in range(4))
        src_h, dst_h = e_h[:, 0:ET], e_h[:, ET:2 * ET]
        w_e3 = w_e[:, :].rearrange("p (t h) -> p t h", h=H)
        rec4 = rec[:, :].rearrange("p (t k c) -> p t k c", t=NT, k=K3)

        def r1(o, n):
            return R1[:, o:o + n]

        Ww = r1(0, 8192).rearrange("p (c n) -> p c n", c=8)
        Wv = r1(8192, 2048).rearrange("p (k n) -> p k n", k=KD)
        
        ab = [r1(16320 + ROW * j, ROW) for j in range(2)]
        ga = [r1(10240 + ROW * j, ROW) for j in range(NGA - 2)] + ab
        lsc = r1(14400, 1024)
        mt = [r1(3072 * j, 3072).rearrange("p (n h) -> p n h", h=H) for j in range(NT)]
        probs = [r1(9216 + N * j, N) for j in range(3)] + [R2[:, 5632 + N * j:5632 + N * j + N] for j in (0,)] + [
            R2[:, 11264 + N * j:11264 + N * j + N] for j in range(2)]
        probsT = [v.rearrange("p (c n) -> p c n", c=NT) for v in
                  [xT_s[:, 0:NT * N]] + [r1(10368 + NT * N * j, NT * N) for j in range(H - 1)]]
        wbuf = [r1(3072 * j, 3072) for j in range(5)] + [R2[:, 7680 + 3072 * j:10752 + 3072 * j] for j in range(3)]
        w13 = [w[:, 0:2048].rearrange("p (k n) -> p k n", k=KD) for w in wbuf]
        w2e = [w[:, 2048:3072].rearrange("p (c n) -> p c n", c=2) for w in wbuf]
        ypick = [r1(4096 * j, 4096) for j in range(NT)]
        L1W = R2[:, 0:6144].rearrange("p (l k n) -> p l k n", l=3, k=KD)
        F2W2 = R2[:, 0:6144].rearrange("p (e c n) -> p e c n", e=E2, c=2)
        F2W1 = R2[:, 6144:12288].rearrange("p (e k n) -> p e k n", e=E2, k=KD)
        L2W = R2[:, 12288:14336].rearrange("p (k n) -> p k n", k=KD)
        L3S = R2[:, 14336:16384].rearrange("p (k n) -> p k n", k=KD)
        L3N = R2[:, 16384:18432].rearrange("p (k n) -> p k n", k=KD)
        gateW = R2[:, 18432:18688].rearrange("p (k n) -> p k n", k=KD)
        B0 = 6144
        V = R2[:, B0:B0 + 1536].rearrange("p (t d) -> p t d", t=NT)
        wu = R2[:, B0 + 1536:B0 + 2560]
        wd = R2[:, B0 + 2560:B0 + 3584]
        bvr = R2[:, B0 + 3584:B0 + 4096]
        g0r = R2[:, B0 + 4096:B0 + 4608]
        b0r = R2[:, B0 + 4608:B0 + 5120]
        bwr = R2[:, B0 + 5120:B0 + 6144]
        oh = R2[:, 0:768].bitcast(bf16).rearrange("p (b s n) -> p b s n", b=2, s=2)
        attT = R1[:, 0:1536].rearrange("p (k n) -> p k n", k=KD)
        war = R2[:, 768:896]
        bar = R2[:, 896:897]
        y0 = R2[:, 1024:2560].rearrange("p (t d) -> p t d", t=NT)
        ye = R2[:, 2560:4096].rearrange("p (t d) -> p t d", t=NT)
        yr = R2[:, 4096:5632].rearrange("p (t d) -> p t d", t=NT)
        xws = WK[:, 0:1536].rearrange("p (t d) -> p t d", t=NT)
        gT = WK[:, 1536:3072].rearrange("p (k n) -> p k n", k=KD)
        y6 = R2[:, 12288:13824].rearrange("p (t d) -> p t d", t=NT)
        ye7 = R2[:, 4096:5632].rearrange("p (t d) -> p t d", t=NT)
        hid = [WK[:, 768 * j:768 * j + 768].rearrange("p (c n) -> p c n", c=2) for j in range(2)]
        xg = [R2[:, D * j:D * j + D] for j in range(NXG)]
        xeT = [R2[:, 3072 + D * j:3072 + D * j + D].rearrange("p (k n) -> p k n", k=KD) for j in range(2)]
        act = [R2[:, 4096 + F3 * j:4096 + F3 * j + F3] for j in range(2)]
        hmid = [R2[:, 4608 + F3 * j:4608 + F3 * j + F3] for j in range(2)]
        hT = [R2[:, 5120 + F3 * j:5120 + F3 * j + F3] for j in range(2)]
        ysb = [R2[:, 5632 + D * j:5632 + D * j + D] for j in range(NYB)]

        b2r, b3r, g3r, be3r = (rows[:, D * j:D * j + D] for j in range(4))
        bcol = [cols[:, KD * j:KD * j + KD] for j in range(7)]

        xq = WK[:, 0:768].bitcast(bf16).rearrange("p (t d) -> p t d", t=NT)
        xqT = WK[:, 768:1536].bitcast(bf16).rearrange("p (k n) -> p k n", k=KD)
        hb = WK[:, 1536:2304].rearrange("p (t f) -> p t f", t=NT)
        hq = WK[:, 2304:2688].bitcast(bf16).rearrange("p (t f) -> p t f", t=NT)
        hqT = WK[:, 2688:3072].bitcast(bf16).rearrange("p (c n) -> p c n", c=2)
        hr, hd = (xT_s[:, 768 * j:768 * j + 768].rearrange("p (t f) -> p t f", t=NT) for j in range(2))
        wuq = wq[:, 0:1024].rearrange("p (k n) -> p k n", k=KD)
        wdq = wq[:, 1024:2048].rearrange("p (c n) -> p c n", c=2)
        wg_s = sb("wg_s", KD * E2)
        wg = wg_s[:, :].rearrange("p (k n) -> p k n", k=KD)
        first_rec = sb("first_rec", NT * EF * 4)
        first_rec4 = first_rec[:, :].rearrange("p (t e c) -> p t e c", t=NT, e=EF)
        first_slot = sb("first_slot", EF * 4, i32)
        first_slot3 = first_slot[:, :].rearrange("p (e c) -> p e c", e=EF)
        tri8 = sb("tri8", G3 * G3)
        te = "p (t e) -> p t e"
        scores8, biased, masked, replaced, selw, place = (
            WK[:, o:o + NT * E3].rearrange(te, t=NT) for o in (0, 192, 704, 896, 1088, 1280))
        top_in_group = WK[:, 384:576].rearrange("p (g m) -> p g m", m=8)
        beats, ties = WK[:, 1952:2144], WK[:, 2144:2336]
        picked = WK[:, 1536:1632].bitcast(bf16).rearrange(te, t=NT)
        place1 = WK[:, 1688:1688 + NT * EF].rearrange("p (t e) -> p t e", t=NT)
        kth_s = WK[:, 1728:1728 + NT * EF * K3]
        kth = kth_s.rearrange("p (t e k) -> p t e k", t=NT, e=EF)
        first_oh = R2[:, 4096:4096 + NT * EF * P].rearrange("p (e t n) -> p e t n", e=EF, t=NT)
        pick_row_f = WK[:, 1632:1656]
        pick_row = WK[:, 1664:1688].bitcast(i32)
        pb = [ctx.enter_context(nc.psum_tensor(f"bank{j}", [P, 512], f32)) for j in range(8)]

        pbh = [b[:, :].bitcast(bf16) for b in pb]
        sq_scr = pb[7][:, 0:N]

        small = {}
        used = [0]

        def V_(name, n):
            if name not in small:
                small[name] = sm[:, used[0]:used[0] + n]
                used[0] += n
                assert used[0] <= 1024
            return small[name]

        xin, srcd, dstd = a["x"], a["src"], a["dst"]
        tiles = "(t p) d -> p t d"
        chunks = "(k p) n -> p k n"

        def rest(eng, one_expert, after=None):
            eng.wait_ge(S("most_ready"), 1)
            fullest = eng.value_load(most[0:1, 0:1], min_val=0, max_val=N)
            with eng.If(fullest > P):
                for s in range(1, NT):
                    with eng.Fori(0, E3) as e:
                        one_expert(eng, s, e, e + (E3 * (s - 1) + 1))
                if after is not None:
                    after()

        block = ctx.enter_context(nc.Block())

        @block.sync
        def _(sp):
            sp.dma_start(x3, xin.rearrange(tiles, p=P)).then_inc(S("x_loaded"), 16)
            sp.dma_start(src_i, srcd.rearrange("(p t) -> p t", p=P)).then_inc(S("edges_loaded"), 16)
            sp.dma_start(dst_i, dstd.rearrange("(p t) -> p t", p=P)).then_inc(S("edges_loaded"), 16)
            ww = a["L0_Ww"].rearrange("(c p) n -> p c n", p=P)
            sp.dma_start(Ww[:, 0:4, :], ww[:, 0:4, :]).then_inc(S("Ww_loaded_src"), 16)
            sp.dma_start(Ww[:, 4:8, :], ww[:, 4:8, :]).then_inc(S("Ww_loaded_dst"), 16)
            for row, name in ((bwr, "L0_bw"), (bvr, "L0_bv"), (g0r, "L0_gamma"), (b0r, "L0_beta"),
                              (war, "L0_Wa"), (bar, "L0_ba")):
                sp.dma_start(row, a[name].partition_broadcast(P)).then_inc(S("rows0_loaded"), 16)
            sp.dma_start(Wv, a["L0_Wv"].rearrange(chunks, p=P)).then_inc(S("Wv_loaded"), 16)
            sp.dma_start(wu.rearrange("p (k n) -> p k n", k=KD), a["L1_wu"].rearrange(chunks, p=P)).then_inc(S("bit_w_loaded"), 16)
            sp.dma_start(wd.rearrange("p (k n) -> p k n", k=2), a["L1_wd"].rearrange(chunks, p=P)).then_inc(S("bit_w_loaded"), 16)
            for t in range(NT):
                sp.wait_ge(S("src_rows_ready"), 2 * t + 2)
                sp.dma_start(tab_src[P * t:P * t + P, :], ab[0]).then_inc(S("src_rows_stored"), 16)
                sp.wait_ge(S("dst_rows_ready"), 2 * t + 2)
                sp.dma_start(tab_dst[P * t:P * t + P, :], ab[1]).then_inc(S("dst_rows_stored"), 16)
                if t == 0:
                    sp.wait_ge(S("no_edge_ready"), 1)
                    fill = score.rearrange("n h -> (n h)").rearrange("(q p c) -> q p c", p=P, c=1024)
                    for q in range(9):
                        sp.dma_start(fill[q], ga[0][:, 0:1024]).then_inc(S("score_filled"), 16)
                    sp.wait_ge(S("no_token_ready"), 4)
                    slots = slot_tab.rearrange("(s p e) c -> s p (e c)", s=NT, p=P)
                    for q in range(NT):
                        sp.dma_start(slots[q], slot0[:, :]).then_inc(S("slots_filled"), 16)
            sp.wait_ge(S("V_ready"), NT)
            for j in range(2):
                sp.wait_ge(S(f"scores_stored{j}"), 8 * ET)
            for i in range(NT):
                sp.dma_start(mt[i], score[N * P * i:N * P * (i + 1), :].rearrange("(p n) h -> p n h", p=P)).then_inc(S(f"read_back{i}"), 16)
            for j, name in enumerate(("L2_b", "L3_bias", "L3_gamma", "L3_beta")):
                sp.dma_start(rows[:, D * j:D * j + D], a[name].partition_broadcast(P)).then_inc(S("rows_loaded"), 16)
            sp.dma_start(gateb[:, :], a["L3_gate_b"].partition_broadcast(P)).then_inc(S("rows_loaded"), 16)
            sp.dma_start(wg, a["L2_w_gating"].rearrange(chunks, p=P)).then_inc(S("weights_loaded"), 16)
            sp.dma_start(cols[:, :], a["fcols"]).then_inc(S("rows_loaded"), 16)
            sp.dma_start(L2W, a["L2_W"].rearrange(chunks, p=P)).then_inc(S("weights_loaded"), 16)
            sp.dma_start(L3S, a["L3_self"].rearrange(chunks, p=P)).then_inc(S("weights_loaded"), 16)
            sp.dma_start(L3N, a["L3_neigh"].rearrange(chunks, p=P)).then_inc(S("weights_loaded"), 16)
            sp.dma_start(gateW, a["L3_gate_w"].rearrange(chunks, p=P)).then_inc(S("weights_loaded"), 16)
            sp.wait_ge(S("x_ready"), NT * 0 + NT)
            for l in range(3):
                sp.dma_start(L1W[:, l], a[f"L1_W{l}"].rearrange(chunks, p=P)).then_inc(S(f"L1W{l}_loaded"), 16)
            sp.wait_ge(S("wq_ready"), 2)
            sp.dma_start(F2W1, a["L2_w1"].rearrange("e (k p) n -> p e k n", p=P)).then_inc(S("F2W1_loaded"), 16)

            def load_expert(e):
                j = e % NWB
                for c, name in enumerate(("L3_w1", "L3_w3")):
                    sp.dma_start(w13[j][:, :, F3 * c:F3 * c + F3], a[name][e].rearrange(chunks, p=P)).then_inc(S(f"expert_w{j}"), 16)
                sp.dma_start(w2e[j], a["L3_w2"][e].rearrange("(c p) n -> p c n", p=P)).then_inc(S(f"expert_w{j}"), 16)

            for e in range(5):
                load_expert(e)
            sp.wait_ge(S("h_out_psum"), NT)
            sp.dma_start(F2W2, a["L2_w2"].rearrange("e (c p) n -> p e c n", p=P)).then_inc(S("F2W2_loaded"), 16)
            sp.wait_ge(S("x_ready"), NT * 7)
            for e in range(5, NWB):
                load_expert(e)
            for t in range(NT):
                sp.wait_ge(S("xn_ready"), nth("8", t + 1))
                sp.dma_start(tok_tab[P * t:P * t + P, :], xn3[:, t]).then_inc(S("tokens_stored"), 16)
            for e in range(NWB, E3):
                if e == EF + 4:
                    sp.wait_ge(S("slots_written"), 16 * NT * K3)
                    sp.dma_start(slot0[:, :], slots[0]).then_inc(S("slot0_loaded"), 16)
                sp.wait_ge(S("y_psum"), e - NWB + 1)
                if e - 4 >= EF:
                    sp.wait_ge(S(f"tokens_gathered{(e - 4) % NXG}"), 16 * ((e - 4) // NXG + 1))
                load_expert(e)
            sp.wait_ge(S("y_psum"), E3)

            def load_rest(sp, s, e, nth_):
                sp.wait_ge(S("rest_turn"), nth_)
                sp.dma_start(rest_rec[:, :], slot_tab.rearrange("(s p e) c -> s p e c", s=NT, p=P)[s, :, bass.ds(e, 1), :]).then_inc(S("rest_loaded"), 16)
                for c, name in enumerate(("L3_w1", "L3_w3")):
                    sp.dma_start(w13[0][:, :, F3 * c:F3 * c + F3], a[name][bass.ds(e, 1)].rearrange("e (k p) n -> p (e k) n", p=P)).then_inc(S("rest_loaded"), 16)
                sp.dma_start(w2e[0], a["L3_w2"][bass.ds(e, 1)].rearrange("e (c p) n -> p (e c) n", p=P)).then_inc(S("rest_loaded"), 16)

            rest(sp, load_rest, lambda: sp.wait_ge(S("rest_turn"), E3 * (NT - 1) + 1))
            for j in range(NYB):
                sp.wait_ge(S(f"picks_stored{j}"), 16 * len(range(j, E3, NYB)))
            sp.wait_ge(S("y_psum"), E3)
            for half in range(2):
                for t in range(NT):
                    four = slice(4 * D * half, 4 * D * half + 4 * D)
                    rows_ = pick_out[P * K3 * t:P * K3 * (t + 1), :].rearrange("(p k) d -> p (k d)", k=K3)
                    sp.dma_start(ypick[t][:, four], rows_[:, four]).then_inc(S(f"last_picks{t}") if half else S(f"read_back{t}"), 16)
            for t in range(NT):
                sp.wait_ge(S("x_ready"), NT * 7 + t + 1)
                sp.dma_start(out[P * t:P * t + P, :], x3[:, t]).then_inc(S("out_stored"), 16)
            sp.wait_ge(S("out_stored"), 16 * NT)

        @block.gpsimd
        def _(pool):
            done = [0]

            def step(ins):
                done[0] += 1
                ins.then_inc(S("pool_step"), 1)
                pool.wait_ge(S("pool_step"), done[0])

            imprecise = dict(allow_small_or_imprecise_dtypes=True)
            pool.memset(ga[0], NEG).then_inc(S("no_edge_ready"), 1)
            step(pool.memset(ident[:, :], 0.0))
            step(pool.affine_select(out=ident[:, :], in_=ident[:, :], compare_op=ALU.not_equal, fill=1.0, base=0,
                                    pattern=[[-1, P]], channel_multiplier=1))
            step(pool.memset(ones[:, :], 1.0))
            step(pool.affine_select(out=tri[:, :], in_=ones[:, :], compare_op=ALU.is_gt, fill=0.0, base=0,
                                    pattern=[[-1, P]], channel_multiplier=1))
            step(pool.affine_select(out=trib[:, :], in_=ones[:, :], compare_op=ALU.is_gt, fill=0.0, base=0,
                                    pattern=[[1, P]], channel_multiplier=-1))
            step(pool.tensor_copy(identb[:, :], ident[:, :]))
            step(pool.tensor_copy(onesb[:, :], ones[:, :]))
            step(pool.iota(iota_h[:, :], pattern=[[1, N]], base=0, channel_multiplier=0, **imprecise))
            step(pool.iota(iota64[:, :], pattern=[[1, E3]], base=0, channel_multiplier=0, **imprecise))
            step(pool.iota(fall48[:, :], pattern=[[0, 3], [-1, 16]], base=16, channel_multiplier=0, **imprecise))
            step(pool.memset(tri8[:, :], 1.0))
            t8 = tri8[:, :].rearrange("p (g m) -> p g m", g=G3)
            step(pool.affine_select(out=t8, in_=t8, compare_op=ALU.is_gt, fill=0.0, base=0,
                                    pattern=[[1, G3], [-1, G3]], channel_multiplier=0))
            s4 = slot0[:, :].rearrange("p (e c) -> p e c", c=4)
            for c, value in enumerate((N, N * K3, 0, 0)):
                pool.memset(s4[:, :, c], value).then_inc(S("no_token_ready"), 1)
            step(pool.memset(rec[:, :], 0))
            step(pool.iota(first_rec4[:, :, :, 0], pattern=[[P, NT], [0, EF]], base=-N, channel_multiplier=1, **imprecise))
            step(pool.iota(first_rec4[:, :, :, 1], pattern=[[P * K3, NT], [0, EF]], base=-N * K3, channel_multiplier=K3, **imprecise))
            step(pool.memset(V_("zero", 1), 0.0))
            step(pool.iota(rec4[:, :, :, 0], pattern=[[P, NT], [0, K3]], base=0, channel_multiplier=1))
            pool.iota(rec4[:, :, :, 1], pattern=[[P * K3, NT], [1, K3]], base=0, channel_multiplier=K3).then_inc(S("consts_ready"), 1)

            pool.wait_ge(S("edge_idx_ready"), 1)
            pool.wait_ge(S("score_filled"), 16 * 9)
            pool.wait_ge(S("src_rows_stored"), 16 * NT)

            def gather_src(t):
                j = t % NGA
                if t >= NGA:
                    pool.wait_ge(S("w_ready"), t - NGA + 1)
                pool.indirect_dma_start(out=ga[j], out_offset=None, in_=tab_src[:, :],
                                        in_offset=bass.IndirectOffsetOnAxis(ap=src_i[:, t:t + 1], axis=0)).then_inc(S(f"edge_rows{j}"), 16)

            def add_dst(t):
                j = t % NGA
                pool.wait_ge(S(f"edge_rows{j}"), 32 * (t // NGA) + 16)
                pool.indirect_dma_start(out=ga[j], out_offset=None, in_=tab_dst[:, :],
                                        in_offset=bass.IndirectOffsetOnAxis(ap=dst_i[:, t:t + 1], axis=0),
                                        compute_op=ALU.add).then_inc(S(f"edge_rows{j}"), 16)

            def scatter_score(t):
                pool.wait_ge(S("w_ready"), t + 1)
                if t >= 2:
                    pool.wait_ge(S(f"scores_stored{t % 2}"), 16 * (t // 2))
                pool.indirect_dma_start(out=score[:, :], out_offset=bass.IndirectOffsetOnAxis(ap=row_i[:, t:t + 1], axis=0),
                                        in_=w_e3[:, t, :], in_offset=None, bounds_check=N * N - 1,
                                        oob_is_err=False).then_inc(S(f"scores_stored{t % 2}"), 16)

            for t in range(4):
                gather_src(t)
            pool.wait_ge(S("dst_rows_stored"), 16 * NT)
            for t in range(ET):
                if 4 <= t + 3 < ET:
                    gather_src(t + 3)
                add_dst(t)
                if t >= 3:
                    scatter_score(t - 3)
            for t in range(ET - 3, ET):
                scatter_score(t)
            pool.wait_ge(S("half_sc_ready"), 1)
            half_sc = V_("half_sc", 4)
            for j, w in enumerate((wu, wd)):
                q = wq[:, 1024 * j:1024 * j + 1024]
                step(pool.tensor_scalar(q, w, half_sc[:, j:j + 1], None, ALU.is_gt))
                step(pool.tensor_scalar(w, w, half_sc[:, 2 + j:3 + j], None, ALU.is_lt))
                pool.tensor_tensor(out=q, in0=q, in1=w, op=ALU.subtract).then_inc(S("wq_ready"), 1)
            pool.wait_ge(S("shifter_in_ready"), 1)
            for t in range(NT):
                pool.tensor_tensor(out=x3[:, t, :], in0=x3[:, t, :], in1=xn3[:, t, :], op=ALU.add).then_inc(S("shifter_added"), 1)
            pool.wait_ge(S("x_ready"), NT * 6)
            for j in range(NXG):
                pool.memset(xg[j], 0.0).then_inc(S("xg_cleared"), 1)
            pool.wait_ge(S("tokens_stored"), 16 * NT)
            pool.wait_ge(S("xg_cleared"), NXG)

            def slots_of(e):
                return first_slot3 if e < EF else s4

            def gather_tokens(e):
                j = e % NXG
                if e >= NXG:
                    pool.wait_ge(S("xe_psum"), e - NXG + 1)
                pool.indirect_dma_start(out=xg[j], out_offset=None, in_=tok_tab[:, :],
                                        in_offset=bass.IndirectOffsetOnAxis(ap=slots_of(e)[:, e, 0:1], axis=0),
                                        bounds_check=N - 1, oob_is_err=False).then_inc(S(f"tokens_gathered{j}"), 16)

            def scatter_picks(e):
                j = e % NYB
                pool.wait_ge(S("ye_ready"), e + 1)
                pool.indirect_dma_start(out=pick_out[:, :], out_offset=bass.IndirectOffsetOnAxis(ap=slots_of(e)[:, e, 1:2], axis=0),
                                        in_=ysb[j], in_offset=None, bounds_check=N * K3 - 1,
                                        oob_is_err=False).then_inc(S(f"picks_stored{j}"), 16)

            def scatter_records(t, k):
                if t == 0 and k == 0:
                    pool.wait_ge(S("slots_filled"), 16 * NT)
                if k == 0:
                    pool.wait_ge(S("picks_ready"), t + 1)
                c = t * K3 + k
                pool.indirect_dma_start(out=slot_tab[:, :], out_offset=bass.IndirectOffsetOnAxis(ap=pick_row[:, c:c + 1], axis=0),
                                        in_=rec4[:, t, k, :], in_offset=None).then_inc(S("slots_written"), 16)

            pool.wait_ge(S("first_slots_ready"), 1)
            for e in range(4):
                if e % 2 == 0:
                    pool.wait_ge(S("first_slots_ready"), e // 2 + 1)
                gather_tokens(e)
            for t in range(NT):
                for k in range(K3):
                    scatter_records(t, k)
                    if t == 1 and k == 5 or t == 2 and k == 3:
                        scatter_picks(t - 1)
                        gather_tokens(t + 5)
                if t == 0:
                    pool.wait_ge(S("first_slots_ready"), 3)
                    gather_tokens(4)
                    gather_tokens(5)
            scatter_picks(2)
            gather_tokens(8)
            pool.wait_ge(S("slot0_loaded"), 16)
            for e in range(EF, E3):
                gather_tokens(e)
                scatter_picks(e - NXG)
            for e in range(E3 - NXG, E3):
                scatter_picks(e)

            def hold(j):
                return pool.tensor_tensor(out=V_("held", 3)[:, j:j + 1], in0=V_("zero", 1), in1=V_("zero", 1), op=ALU.add)

            def move_rest(pool, s, e, nth_):
                pool.wait_ge(S("rest_loaded"), nth_ * 64)
                hold(0)
                pool.indirect_dma_start(out=xg[0], out_offset=None, in_=tok_tab[:, :],
                                        in_offset=bass.IndirectOffsetOnAxis(ap=rest_rec[:, 0:1], axis=0),
                                        bounds_check=N - 1, oob_is_err=False).then_inc(S("rest_gathered"), 16)
                pool.wait_ge(S("rest_evacuated"), nth_ * 4)
                hold(1)
                pool.indirect_dma_start(out=pick_out[:, :], out_offset=bass.IndirectOffsetOnAxis(ap=rest_rec[:, 1:2], axis=0),
                                        in_=ysb[0], in_offset=None, bounds_check=N * K3 - 1,
                                        oob_is_err=False).then_inc(S("rest_stored"), 16)
                pool.wait_ge(S("rest_stored"), nth_ * 16)
                hold(2).then_inc(S("rest_turn"), 1)

            for j in range(NYB):
                pool.wait_ge(S(f"picks_stored{j}"), 16 * len(range(j, E3, NYB)))
            pool.wait_ge(S("xe_psum"), E3)
            hold(2).then_inc(S("rest_turn"), 1)
            rest(pool, move_rest)


        @block.tensor
        def _(pe):
            def transposes(norm, t, src=xn3):
                pe.wait_ge(S("xn_ready"), nth(norm, t + 1))
                for k in range(KD):
                    last = pe.transpose(pb[t][:, P * k:P * k + P], src[:, t, P * k:P * k + P], ident[:, :])
                return last

            def project(t, bank, lhsT, rhs, cols_=slice(0, 512), chunks_=range(KD)):
                for k in chunks_:
                    last = pe.matmul(pb[bank][:, cols_], lhsT[:, k, P * t:P * t + P], rhs[:, k, :],
                                     start=(k == chunks_[0]), stop=(k == chunks_[-1]))
                return last

            pe.wait_ge(S("consts_ready"), 1)
            for t in range(NT):
                transposes("1", t).then_inc(S("xT_psum"), 1)
            for t in range(NT):
                for b in range(4):
                    half = b % 2
                    rows_ready = S("src_half_ready") if b < 2 else S("dst_half_ready")
                    if t == 0 and half == 0:
                        pe.wait_ge(S("Ww_loaded_src") if b < 2 else S("Ww_loaded_dst"), 16)
                    if b == 3 and t == 0:
                        pe.wait_ge(S("xT_ready"), nth("1", NT))
                    pe.wait_ge(S("xT_ready"), nth("1", t + 1))
                    if t:
                        pe.wait_ge(rows_ready, 2 * (t - 1) + half + 1)
                    w = Ww[:, 4 * (b // 2):4 * (b // 2) + 4, D * half:D * half + D]
                    project(t, (3, 4, 5, 0)[b], xT, w).then_inc(S("src_rows_psum") if b < 2 else S("dst_rows_psum"), 1)
            pe.wait_ge(S("edge_idx_ready"), 1)
            pe.wait_ge(S("Wv_loaded"), 16)
            pe.wait_ge(S("src_half_ready"), 2 * NT)
            pe.wait_ge(S("dst_half_ready"), 2 * NT)
            for e in range(ET):
                if e % 4 == 0:
                    g = e // 4
                    if g >= 2:
                        pe.wait_ge(S("dup_used"), g)
                    for j in range(4):
                        o = pb[6 + g % 2][:, P * j:P * j + P]
                        pe.matmul(o, src_h[:, e + j:e + j + 1].to_broadcast([P, P]), ident16[:, 0:P], start=True, stop=False)
                        last = pe.matmul(o, dst_h[:, e + j:e + j + 1].to_broadcast([P, P]), ident16[:, P:2 * P], start=False, stop=True)
                    last.then_inc(S("key_psum"), 1)
                if e % 4 == 2 and e // 4 < NT:
                    project(e // 4, 3 + e // 4, xT, Wv).then_inc(S("V_psum"), 1)
                pe.wait_ge(S("onehot_ready"), e + 1)
                for s in range(NT):
                    last = pe.matmul(pb[s][:, 0:N], oh[:, e % 2, 0, P * s:P * s + P], oh[:, e % 2, 1, :],
                                     start=(e == 0), stop=(e == ET - 1))
                last.then_inc(S("onehot_used"), 1)
            pe.wait_ge(S("cnt_ready"), 1)
            pe.wait_ge(S("dup_used"), 12)
            for t in range(NT):
                for s in range(NT):
                    pe.matmul(pb[6][:, t:t + 1], cnt[:, s, P * t:P * t + P], ones[:, 0:1], start=(s == 0), stop=(s == NT - 1))
            for s in range(NT):
                pe.matmul(pb[7][:, 0:N], ones[:, :], cnt[:, s, :], start=(s == 0), stop=(s == NT - 1))
            pe.wait_ge(S("bit_abs_ready"), 2)
            pe.matmul(pb[6][:, 8:10], ones[:, :], V_("wabs", 2), start=True, stop=True).then_inc(S("deg_psum"), 1)
            pe.wait_ge(S("V_ready"), NT)

            def wait_transposed(u):
                if u // H == 1:
                    pe.wait_ge(S("middle_probsT_ready"), u - H + 1)
                else:
                    pe.wait_ge(S("probsT_ready"), (u if u < H else u - H) + 1)

            def transpose_probs(u):
                i, h = divmod(u, H)
                pe.wait_ge(S("probs_ready"), u + 1)
                if u >= 3:
                    wait_transposed(u - 3)
                for c in range(NT):
                    last = pe.transpose(pb[u % 3][:, P * c:P * c + P], probs[u % NPR][:, P * c:P * c + P], ident[:, :])
                last.then_inc(S("probsT_psum"), 1)

            def attend(part, h):
                unit = H * part + h
                if part == 0:
                    wait_transposed(h)
                wait_transposed(H * (part + 1) + h)
                if unit >= 3:
                    pe.wait_ge(S("attended_ready"), unit - 2)
                pair = h // 2
                for c in range(NT):
                    last = pe.matmul(pb[3 + unit % 3][:, SRC_PART[part]], V[:, c, P * pair:P * pair + P], probsT[h][:, c, SRC_PART[part]],
                                     start=(c == 0), stop=(c == NT - 1))
                last.then_inc(S("attended_psum"), 1)

            for u in range(H + 2):
                transpose_probs(u)
            for unit in range(2 * H):
                if unit + 2 < 2 * H:
                    transpose_probs(H + unit + 2)
                attend(*divmod(unit, H))
            pe.wait_ge(S("attended_ready"), 2 * H)
            for t in range(NT):
                if t == 0:
                    pe.wait_ge(S("probsT_ready"), 2 * H)
                for k in range(KD):
                    last = pe.transpose(pb[t][:, P * k:P * k + P], attT[:, k, P * t:P * t + P], ident[:, :])
                last.then_inc(S("attended_back"), 1)

            for t in range(NT):
                transposes("3", t).then_inc(S("xT_psum"), 1)
            for l in range(3):
                pe.wait_ge(S(f"L1W{l}_loaded"), 16)
                if l == 0:
                    for t in range(NT):
                        pe.wait_ge(S("xT_ready"), nth("3", t + 1))
                        project(t, 3 + t, xT, L1W[:, l]).then_inc(S("hw_psum"), 1)
                else:
                    for k in range(KD):
                        pe.wait_ge(S("hT_ready"), KD * (l - 1) + k + 1)
                        for t in range(NT):
                            last = pe.matmul(pb[3 + t][:, :], xT[:, k, P * t:P * t + P], L1W[:, l, k, :], start=(k == 0), stop=(k == KD - 1))
                            if k == KD - 1:
                                last.then_inc(S("hw_psum"), 1)
                pe.wait_ge(S("hw_ready"), NT * (l + 1))
                for k in range(KD):
                    for s in range(NT):
                        last = pe.matmul(pb[(0, 1, 2, 6)[k]][:, 0:N], xws[:, s, P * k:P * k + P], cntI[:, s, :],
                                         start=(s == 0), stop=(s == NT - 1))
                    last.then_inc(S("agg_psum"), 1)
            for k in range(KD):
                pe.wait_ge(S("hT_ready"), 2 * KD + k + 1)
                for t in range(NT):
                    last = pe.transpose(pb[3 + t][:, P * k:P * k + P], xT[:, k, P * t:P * t + P], ident[:, :])
                    if k == KD - 1:
                        last.then_inc(S("h_out_psum"), 1)

            for t in range(NT):
                pe.wait_ge(S("xq_ready"), t + 1)
                for k in range(KD):
                    last = pe.transpose(pbh[t][:, P * k:P * k + P], xq[:, t, P * k:P * k + P], identb[:, :])
                last.then_inc(S("xqT_psum"), 1)
            pe.wait_ge(S("wq_ready"), 2)
            for t in range(NT):
                pe.wait_ge(S("xqT_ready"), t + 1)
                if t == 0:
                    pe.wait_ge(S("x_ready"), NT * 2 + NT)
                for k in range(KD):
                    last = pe.matmul(pb[3 + t][:, 0:F1], xqT[:, k, P * t:P * t + P], wuq[:, k, :], start=(k == 0), stop=(k == KD - 1))
                last.then_inc(S("up_bit_psum"), 1)
            for t in range(NT):
                pe.wait_ge(S("hq_ready"), t + 1)
                for c in range(2):
                    last = pe.transpose(pbh[t][:, P * c:P * c + P], hq[:, t, P * c:P * c + P], identb[:, :])
                last.then_inc(S("hqT_psum"), 1)
            for t in range(NT):
                pe.wait_ge(S("hqT_ready"), t + 1)
                for c in range(2):
                    last = pe.matmul(pb[3 + t][:, :], hqT[:, c, P * t:P * t + P], wdq[:, c, :], start=(c == 0), stop=(c == 1))
                last.then_inc(S("down_bit_psum"), 1)

            for t in range(NT):
                transposes("5", t).then_inc(S("xT_psum"), 1)
            pe.wait_ge(S("weights_loaded"), 80)
            pe.wait_ge(S("x_ready"), NT * 3 + NT)
            for t in range(NT):
                pe.wait_ge(S("xT_ready"), nth("5", t + 1))
                project(t, 3 + t, xT, L2W).then_inc(S("hw5_psum"), 1)
            pe.wait_ge(S("hw5_ready"), NT)
            for t in range(NT):
                for s in range(NT):
                    last = pe.matmul(pb[t][:, :], cntI[:, s, P * t:P * t + P], xws[:, s, :], start=(s == 0), stop=(s == NT - 1))
                last.then_inc(S("agg5_psum"), 1)

            pe.wait_ge(S("rows_loaded"), 96)
            pe.wait_ge(S("weights_loaded"), 80)
            for t in range(NT):
                if t == 0:
                    pe.wait_ge(S("x_ready"), NT * 4 + NT)
                transposes("6", t).then_inc(S("xT_psum"), 1)
            for t in range(NT):
                pe.wait_ge(S("xT_ready"), nth("6", t + 1))
                for k in range(KD):
                    last = pe.matmul(pb[6][:, 8 * t:8 * t + E2], xT[:, k, P * t:P * t + P], wg[:, k, :], start=(k == 0), stop=(k == KD - 1))
            last.then_inc(S("gate6_psum"), 1)
            for t in range(NT):
                transposes("6b", t, y6).then_inc(S("xT_psum"), 1)
            pe.wait_ge(S("F2W1_loaded"), 16)
            pe.wait_ge(S("xT_ready"), nth("6b", NT))

            def hidden6(e):
                for c in range(2):
                    j = 2 * e + c
                    if j >= 3:
                        pe.wait_ge(S("hid6_ready"), j - 2)
                    for k in range(KD):
                        last = pe.matmul(pb[j % 3][:, 0:N], F2W1[:, e, k, P * c:P * c + P], xT[:, k, :], start=(k == 0), stop=(k == KD - 1))
                    last.then_inc(S("hid6_psum"), 1)

            hidden6(0)
            for e in range(E2):
                if e + 1 < E2:
                    hidden6(e + 1)
                if e == 0:
                    pe.wait_ge(S("F2W2_loaded"), 16)
                pe.wait_ge(S("hid6_ready"), 2 * e + 2)
                for t in range(NT):
                    j = NT * e + t
                    if j >= 4:
                        pe.wait_ge(S("out6_used"), j - 3)
                    for c in range(2):
                        last = pe.matmul(pb[(3, 4, 5, 7)[j % 4]][:, :], hid[e % 2][:, c, P * t:P * t + P], F2W2[:, e, c, :], start=(c == 0), stop=(c == 1))
                    last.then_inc(S("out6_psum"), 1)

            for t in range(NT):
                transposes("7", t).then_inc(S("xT_psum"), 1)
            pe.wait_ge(S("x_ready"), NT * 6)
            for k in range(KD):
                for s in range(NT):
                    last = pe.matmul(pb[3 + k][:, 0:N], xn3[:, s, P * k:P * k + P], cnt[:, s, :], start=(s == 0), stop=(s == NT - 1))
                last.then_inc(S("neigh_psum"), 1)
            pe.wait_ge(S("weights_loaded"), 80)
            pe.wait_ge(S("xT_ready"), nth("7", NT))
            for t in range(NT):
                for k in range(KD):
                    pe.matmul(pb[t][:, :], xT[:, k, P * t:P * t + P], L3S[:, k, :], start=(k == 0), stop=False)
                for k in range(KD):
                    pe.wait_ge(S("neighT_ready"), k + 1)
                    last = pe.matmul(pb[t][:, :], gT[:, k, P * t:P * t + P], L3N[:, k, :], start=False, stop=(k == KD - 1))
                last.then_inc(S("sage_psum"), 1)

            for t in range(NT):
                if t == 0:
                    pe.wait_ge(S("sage_used"), NT)
                transposes("8", t).then_inc(S("xT_psum"), 1)
            pe.wait_ge(S("weights_loaded"), 80)
            for t in range(NT):
                pe.wait_ge(S("xT_ready"), nth("8", t + 1))
                for k in range(KD):
                    last = pe.matmul(pb[3][:, E3 * t:E3 * t + E3], xT[:, k, P * t:P * t + P], gateW[:, k, :], start=(k == 0), stop=(k == KD - 1))
            last.then_inc(S("logits_psum"), 1)
            pe.wait_ge(S("picked_ready"), 1)
            for t in range(NT):
                for s in range(t + 1):
                    last = pe.matmul(pb[4][:, E3 * t:E3 * t + E3], (trib if s == t else onesb)[:, :], picked[:, s, :], start=(s == 0), stop=(s == t))
            for s in range(NT):
                last = pe.matmul(pb[4][:, E3 * NT:E3 * NT + E3], onesb[:, :], picked[:, s, :], start=(s == 0), stop=(s == NT - 1))
            last.then_inc(S("place_psum"), 1)
            def first_slots(lo, hi):
                for e in range(lo, hi):
                    pe.wait_ge(S("first_onehot"), NT * (e + 1))
                    for t in range(NT):
                        last = pe.matmul(pb[5][:, 4 * e:4 * e + 3], first_oh[:, e, t, :], first_rec4[:, t, e, 0:3], start=(t == 0), stop=(t == NT - 1))
                    last.then_inc(S("first_slots_psum"), 1)

            def transpose_tokens(e):
                pe.wait_ge(S(f"tokens_gathered{e % NXG}"), 16 * (e // NXG + 1))
                if e >= 2:
                    pe.wait_ge(S("xeT_ready"), e - 1)
                for k in range(KD):
                    last = pe.transpose(pb[e % 2][:, P * k:P * k + P], xg[e % NXG][:, P * k:P * k + P], ident[:, :])
                last.then_inc(S("xe_psum"), 1)

            def up(e):
                pe.wait_ge(S(f"expert_w{e % NWB}"), 48 * (e // NWB + 1))
                pe.wait_ge(S("xeT_ready"), e + 1)
                if e >= 2:
                    pe.wait_ge(S("hmid_ready"), e - 1)
                for k in range(KD):
                    last = pe.matmul(pb[2 + e % 2][:, :], xeT[e % 2][:, k, :], w13[e % NWB][:, k, :], start=(k == 0), stop=(k == KD - 1))
                last.then_inc(S("up_psum"), 1)

            def transpose_hidden(e):
                pe.wait_ge(S("hmid_ready"), e + 1)
                if e >= 2:
                    pe.wait_ge(S("hT8_ready"), e - 1)
                for c in range(2):
                    last = pe.transpose(pb[4 + e % 2][:, P * c:P * c + P], hmid[e % 2][:, P * c:P * c + P], ident[:, :])
                last.then_inc(S("hT_psum"), 1)

            def down(e):
                pe.wait_ge(S("hT8_ready"), e + 1)
                if e >= 2:
                    pe.wait_ge(S("ye_ready"), e - 1)
                for c in range(2):
                    last = pe.matmul(pb[6 + e % 2][:, :], hT[e % 2][:, P * c:P * c + P], w2e[e % NWB][:, c, :], start=(c == 0), stop=(c == 1))
                last.then_inc(S("y_psum"), 1)

            first_slots(0, 4)
            transpose_tokens(0)
            for e in range(E3 + 1):
                if e + 1 < E3:
                    transpose_tokens(e + 1)
                if e >= 1:
                    transpose_hidden(e - 1)
                if e < E3:
                    up(e)
                if e == 0:
                    first_slots(4, EF)
                if e >= 1:
                    down(e - 1)

            def multiply_rest(pe, s, e, nth_):
                pe.wait_ge(S("rest_gathered"), nth_ * 16)
                for k in range(KD):
                    last = pe.transpose(pb[0][:, P * k:P * k + P], xg[0][:, P * k:P * k + P], ident[:, :])
                last.then_inc(S("rest_psum"), 1)
                pe.wait_ge(S("rest_evacuated"), nth_ * 4 - 3)
                for k in range(KD):
                    last = pe.matmul(pb[2][:, :], xeT[0][:, k, :], w13[0][:, k, :], start=(k == 0), stop=(k == KD - 1))
                last.then_inc(S("rest_psum"), 1)
                pe.wait_ge(S("rest_hmid"), nth_)
                for c in range(2):
                    last = pe.transpose(pb[4][:, P * c:P * c + P], hmid[0][:, P * c:P * c + P], ident[:, :])
                last.then_inc(S("rest_psum"), 1)
                pe.wait_ge(S("rest_evacuated"), nth_ * 4 - 1)
                for c in range(2):
                    last = pe.matmul(pb[6][:, :], hT[0][:, P * c:P * c + P], w2e[0][:, c, :], start=(c == 0), stop=(c == 1))
                last.then_inc(S("rest_psum"), 1)

            pe.wait_ge(S("ye_ready"), E3)
            rest(pe, multiply_rest)

        @block.scalar
        def _(act_):
            def copy_T(norm, t):
                act_.wait_ge(S("xT_psum"), nth(norm, t + 1))
                act_.activation(xT[:, :, P * t:P * t + P], pb[t][:, :].rearrange("p (k n) -> p k n", k=KD), ACT.Copy).then_inc(S("xT_ready"), 1)

            rooted = [0]

            def roots(*values):
                rooted[0] += 1
                act_.wait_ge(S("root_asked"), rooted[0])
                for n_, (o, v, plus) in enumerate(values):
                    last = act_.activation(o, v, ACT.Sqrt, bias=plus)
                    if n_ < len(values) - 1:
                        last.then_inc(S("early_roots"), 1)
                if len(values) > 1:
                    act_.wait_ge(S("early_roots"), len(values) - 1)
                last.then_inc(S("root_ready"), 1)

            def row_roots():
                for t in range(NT):
                    roots((V_("rstd", 3)[:, t:t + 1], V_("mv", 6)[:, 2 * t + 1:2 * t + 2], LN_EPS))

            row_roots()
            for t in range(NT):
                copy_T("1", t)
            for t in range(NT):
                for half in range(2):
                    act_.wait_ge(S("src_rows_psum"), 2 * t + half + 1)
                    if t and half == 0:
                        act_.wait_ge(S("src_rows_stored"), 16 * t)
                    act_.activation(ab[0][:, D * half:D * half + D], pb[3 + half][:, :], ACT.Copy).then_inc(S("src_half_ready"), 1)
            def copy_attended(part, h):
                unit = H * part + h
                act_.wait_ge(S("attended_psum"), unit + 1)
                own = slice(HD * (h % 2), HD * (h % 2) + HD)
                act_.activation(attT[own, h // 2, SRC_PART[part]], pb[3 + unit % 3][own, SRC_PART[part]], ACT.Copy).then_inc(S("attended_ready"), 1)

            for u in range(NT * H):
                i, h = divmod(u, H)
                if i == NT - 1:
                    act_.wait_ge(S("probsT_psum"), H + h + 1)
                    act_.activation(probsT[h][:, :, P:2 * P], pb[(H + h) % 3][:, 0:N].rearrange("p (c n) -> p c n", c=NT), ACT.Copy).then_inc(S("middle_probsT_ready"), 1)
                    if h:
                        copy_attended(0, h - 1)
                act_.wait_ge(S("row_max_ready"), i + 1)
                if u >= NPR:
                    act_.wait_ge(S("probsT_psum"), u - NPR + 1)
                act_.activation(probs[u % NPR], mt[i][:, :, h], ACT.Exp, bias=V_("nmax", 24)[:, u:u + 1],
                                accum_out=V_("psum_", 24)[:, u:u + 1]).then_inc(S("probs_ready"), 1)
            copy_attended(0, H - 1)
            dv = V_("dis", 3), V_("dinv", 3), dinv_bc[:, :]
            roots(*((v, v, 1.0) for v in dv))
            for h in range(H):
                copy_attended(1, h)
            for t in range(NT):
                act_.wait_ge(S("ymin_ready"), t + 1)
                act_.activation(ye[:, t], ye[:, t], ACT.Exp).then_inc(S("yexp_ready"), 1)
            row_roots()
            row_roots()
            row_roots()
            for t in range(NT):
                copy_T("3", t)
            for l in range(3):
                act_.wait_ge(S("hw_psum"), NT * l + 2)
                act_.activation(xws[:, 1, :], pb[4][:, :], ACT.Copy, scale=V_("dinv", 3)[:, 1:2]).then_inc(S("hw_ready"), 1)
                for k in range(KD):
                    act_.wait_ge(S("scaled_ready"), KD * l + k + 1)
                    act_.activation(gT[:, k, :], gT[:, k, :], ACT.Relu, bias=bcol[l][:, k:k + 1],
                                    accum_out=V_("gsum", 4)[:, k:k + 1]).then_inc(S("relu_ready"), 1)
                    act_.wait_ge(S("shift_ready"), KD * l + k + 1)
                    act_.activation(sq_scr[:, :], gT[:, k, :], ACT.Square, bias=V_("nshift", 4)[:, k:k + 1],
                                    accum_out=V_("gsq", 4)[:, k:k + 1]).then_inc(S("square_ready"), 1)
                    act_.wait_ge(S("square_ready"), KD * l + k + 1)
                    act_.activation(V_("gmul", 4)[:, k:k + 1], V_("gsq", 4)[:, k:k + 1], ACT.Sqrt, scale=1.0 / N,
                                    bias=EPS).then_inc(S("graph_root_ready"), 1)
            row_roots()
            for t in range(NT):
                act_.wait_ge(S("xqT_psum"), t + 1)
                act_.activation(xqT[:, :, P * t:P * t + P], pbh[t][:, 0:512].rearrange("p (k n) -> p k n", k=KD), ACT.Copy).then_inc(S("xqT_ready"), 1)
            for t in range(NT):
                act_.wait_ge(S("hqT_psum"), t + 1)
                act_.activation(hqT[:, :, P * t:P * t + P], pbh[t][:, 0:256].rearrange("p (k n) -> p k n", k=2), ACT.Copy).then_inc(S("hqT_ready"), 1)
            row_roots()
            for t in range(NT):
                copy_T("5", t)
            row_roots()
            for t in range(NT):
                copy_T("6", t)
            row_roots()
            for t in (0, 2):
                act_.wait_ge(S("xT_psum"), nth("6b", t + 1))
                act_.wait_ge(S("gate6_psum"), 1)
                for k in range(KD):
                    last = act_.activation(xT[:, k, P * t:P * t + P], pb[t][:, P * k:P * k + P], ACT.Copy, scale=bcol[6][:, k:k + 1])
                last.then_inc(S("xT_ready"), 1)
            act_.wait_ge(S("raw6_ready"), 1)
            for t in range(NT):
                act_.activation(V_("ex6", 24)[:, 8 * t:8 * t + E2], V_("raw6", 24)[:, 8 * t:8 * t + E2], ACT.Exp,
                                bias=V_("nm6", 3)[:, t:t + 1], accum_out=V_("es6", 3)[:, t:t + 1]).then_inc(S("ex6_ready"), 1)
            for e in range(E2):
                for c in range(2):
                    j = 2 * e + c
                    act_.wait_ge(S("hid6_psum"), j + 1)
                    if e >= 2:
                        act_.wait_ge(S("out6_psum"), NT * (e - 1))
                    act_.activation(hid[e % 2][:, c, :], pb[j % 3][:, 0:N], ACT.Gelu).then_inc(S("hid6_ready"), 1)
            row_roots()
            for t in range(NT):
                copy_T("7", t)
            row_roots()
            row_roots()
            for t in range(NT):
                copy_T("8", t)
            act_.wait_ge(S("logits_psum"), 1)
            act_.activation(scores8[:, :, :], pb[3][:, 0:NT * E3].rearrange("p (t e) -> p t e", t=NT), ACT.Sigmoid).then_inc(S("sigmoid_ready"), 1)
            s4f = slot0[:, :].bitcast(f32).rearrange("p (e c) -> p e c", c=4)

            firstf = first_slot[:, :].bitcast(f32).rearrange("p (e c) -> p e c", e=EF)

            def copy_hT(e):
                act_.wait_ge(S("hT_psum"), e + 1)
                if e >= 2:
                    act_.wait_ge(S("y_psum"), e - 1)
                act_.activation(hT[e % 2], pb[4 + e % 2][:, 0:F3], ACT.Copy).then_inc(S("hT8_ready"), 1)

            def silu(e):
                act_.wait_ge(S("up_psum"), e + 1)
                if e >= 2:
                    act_.wait_ge(S("hmid_ready"), e - 1)
                act_.activation(act[e % 2], pb[2 + e % 2][:, 0:F3], ACT.Silu).then_inc(S("silu_ready"), 1)

            def weigh(e):
                act_.wait_ge(S("y_psum"), e + 1)
                if e == EF:
                    act_.wait_ge(S("slot0_loaded"), 16)
                if e >= NYB:
                    act_.wait_ge(S(f"picks_stored{e % NYB}"), 16 * (e // NYB))
                act_.activation(ysb[e % NYB], pb[6 + e % 2][:, :], ACT.Copy, scale=(firstf if e < EF else s4f)[:, e, 2:3]).then_inc(S("ye_ready"), 1)

            for e in range(E3 + 1):
                if e >= 1:
                    copy_hT(e - 1)
                if e < E3:
                    silu(e)
                if e >= 1:
                    weigh(e - 1)

            rest_w = rest_rec[:, 2:3].bitcast(f32)

            def evacuate_rest(act_, s, e, nth_):
                act_.wait_ge(S("rest_psum"), nth_ * 4 - 3)
                act_.activation(xeT[0], pb[0][:, :].rearrange("p (k n) -> p k n", k=KD), ACT.Copy).then_inc(S("rest_evacuated"), 1)
                act_.wait_ge(S("rest_psum"), nth_ * 4 - 2)
                act_.activation(act[0], pb[2][:, 0:F3], ACT.Silu).then_inc(S("rest_evacuated"), 1)
                act_.wait_ge(S("rest_psum"), nth_ * 4 - 1)
                act_.activation(hT[0], pb[4][:, 0:F3], ACT.Copy).then_inc(S("rest_evacuated"), 1)
                act_.wait_ge(S("rest_psum"), nth_ * 4)
                act_.activation(ysb[0], pb[6][:, :], ACT.Copy, scale=rest_w).then_inc(S("rest_evacuated"), 1)

            rest(act_, evacuate_rest)

        @block.vector
        def _(dve):
            issued = [0]

            def go(ins):
                issued[0] += 1
                return ins.then_inc(S("dve_step"), 1)

            def settle():
                dve.wait_ge(S("dve_step"), issued[0])

            def one(ins):
                go(ins)
                settle()

            def bc(ap, shape):
                return ap.to_broadcast(shape)

            ts, tt, stt = dve.tensor_scalar, dve.tensor_tensor, dve.scalar_tensor_tensor
            st = V_("st", 18).rearrange("p (t c) -> p t c", t=NT)
            mv = V_("mv", 6).rearrange("p (t c) -> p t c", t=NT)
            rstd = V_("rstd", 3)

            asked = [0]

            def roots(ins):
                asked[0] += 1
                ins.then_inc(S("root_asked"), 1)
                settle()
                dve.wait_ge(S("root_ready"), asked[0])

            def settle_but(n):
                dve.wait_ge(S("dve_step"), issued[0] - n)

            def aggregate(t):
                dve.bn_aggr(mv[:, t, :], st[:, t, :]).then_inc(S("root_asked"), 1)
                asked[0] += 1

            def x_tile_ready(stage):
                return lambda t: dve.wait_ge(S("x_ready"), NT * stage + t + 1)

            def scaled_norm(y, scr, gamma, produce):
                for t in range(NT):
                    produce(t)
                    settle()
                    one(dve.bn_stats(st[:, t, :], y[:, t, :]))
                    aggregate(t)
                    dve.wait_ge(S("root_asked"), asked[0])
                    go(stt(scr[:, t, :], y[:, t, :], mv[:, t, 0:1], gamma, ALU.subtract, ALU.mult))
                dve.wait_ge(S("root_ready"), asked[0])
                go(dve.reciprocal(rstd, rstd))

            def add_norm(scr):
                def add(t):
                    settle_but(0)
                    stt(x3[:, t, :], scr[:, t, :], rstd[:, t:t + 1], x3[:, t, :], ALU.mult, ALU.add).then_inc(S("x_ready"), 1)
                return add

            def layernorm(src, dst, norm=None, produce=None, produced=None):
                for step in range(NT + 2):
                    if step < NT and produce is not None:
                        produce(step)
                    if 1 <= step <= NT:
                        if produced is not None:
                            produced(step - 1)
                        go(dve.bn_stats(st[:, step - 1, :], src[:, step - 1, :]))
                    if step >= 2:
                        settle_but(1 if step <= NT else 0)
                        aggregate(step - 2)
                first_root = asked[0] - NT
                for step in range(NT + 1):
                    t = step - 1
                    if step < NT:
                        dve.wait_ge(S("root_ready"), first_root + step + 1)
                        go(dve.reciprocal(rstd[:, step:step + 1], rstd[:, step:step + 1]))
                    if t >= 0:
                        settle_but(1 if step < NT else 0)
                        ins = ts(dst[:, t, :], src[:, t, :], mv[:, t, 0:1], rstd[:, t:t + 1], ALU.subtract, ALU.mult)
                        if norm is None:
                            go(ins)
                        else:
                            ins.then_inc(S("xn_ready"), 1)
                if norm is None:
                    settle()
                else:
                    dve.wait_ge(S("xn_ready"), nth(norm, NT))

            dve.wait_ge(S("x_loaded"), 16)
            layernorm(x3, xn3, "1")
            dve.wait_ge(S("edges_loaded"), 32)
            go(dve.tensor_copy(src_f, src_i))
            go(dve.tensor_copy(dst_f, dst_i))
            go(dve.tensor_copy(src_h, src_i))
            go(dve.tensor_copy(dst_h, dst_i))
            settle()
            one(stt(key_f, src_f, float(N), dst_f, ALU.mult, ALU.add))
            dve.wait_ge(S("consts_ready"), 1)
            go(ts(ident16[:, 0:P], ident[:, :], float(N), None, ALU.mult))
            dve.tensor_copy(ident16[:, P:2 * P], ident[:, :]).then_inc(S("ident16_ready"), 1)
            settle()
            dve.wait_ge(S("ident16_ready"), 1)
            dve.engine_nop().then_inc(S("edge_idx_ready"), 1)
            dve.wait_ge(S("rows0_loaded"), 96)
            waL, waR = V_("waL", P), V_("waR", P)
            go(ts(waL, war, SLOPE, None, ALU.mult))
            go(ts(waR, war, 1.0 - SLOPE, None, ALU.mult))
            settle()
            heads = "p (h c) -> p h c"
            waL3 = bc(waL[:, None, :], [P, H // 2, P])

            def linear_part(row, half, ready, bias=None):
                own, o = lsc[:, D * half:D * half + D].rearrange(heads, h=H // 2), 2 * D + H // 2 * half
                share = row[:, o:o + H // 2]
                one(tt(own, row[:, D * half:D * half + D].rearrange(heads, h=H // 2), waL3, ALU.mult))
                if bias is None:
                    ins = dve.tensor_reduce(share, own, AX, ALU.add)
                else:
                    one(dve.tensor_reduce(share, own, AX, ALU.add))
                    ins = ts(share, share, bias, None, ALU.add)
                ins.then_inc(ready, 1)

            for t in range(NT):
                for half in range(2):
                    dve.wait_ge(S("src_half_ready"), 2 * t + half + 1)
                    if t:
                        dve.wait_ge(S("src_rows_stored"), 16 * t)
                    linear_part(ab[0], half, S("src_rows_ready"))
                for half in range(2):
                    dve.wait_ge(S("dst_rows_psum"), 2 * t + half + 1)
                    if t:
                        dve.wait_ge(S("dst_rows_stored"), 16 * t)
                    tt(ab[1][:, D * half:D * half + D], pb[(5, 0)[half]][:, :], bwr[:, D * half:D * half + D], ALU.add).then_inc(S("dst_half_ready"), 1)
                    dve.wait_ge(S("dst_half_ready"), 2 * t + half + 1)
                    linear_part(ab[1], half, S("dst_rows_ready"), bar)
            wabs, dup0_f = V_("wabs", 2), V_("dup0_f", ET // 4)
            for t in range(ET):
                if t >= 2:
                    dve.wait_ge(S("onehot_used"), t - 1)
                go(ts(oh[:, t % 2, 0, :], iota_h[:, :], src_f[:, t:t + 1], None, ALU.is_equal))
                ts(oh[:, t % 2, 1, :], iota_h[:, :], dst_f[:, t:t + 1], None, ALU.is_equal).then_inc(S("onehot_ready"), 1)
                settle()
                if t % 4 == 0:
                    g = t // 4
                    dve.wait_ge(S("key_psum"), g + 1)
                    keys = pb[6 + g % 2]
                    for j in range(4):
                        e = t + j
                        lo = P * (j - 1) if j else 0
                        go(stt(lsc[:, 256 * j:256 * j + P * (j + 1) - lo], keys[:, lo:P * (j + 1)], key_f[:, e:e + 1],
                               before_s[:, 0:2 * P] if j else tri, ALU.is_equal, ALU.mult, accum_out=dup_f[:, e:e + 1]))
                    if g:
                        go(stt(lsc[:, P:2 * P], pb[7 - g % 2][:, 3 * P:4 * P], key_f[:, t:t + 1], ones,
                               ALU.is_equal, ALU.mult, accum_out=dup0_f[:, g:g + 1]))
                        settle()
                        go(tt(dup_f[:, t:t + 1], dup_f[:, t:t + 1], dup0_f[:, g:g + 1], ALU.add))
                    settle()
                    stt(row_i[:, t:t + 4], dup_f[:, t:t + 4], 262144.0, key_f[:, t:t + 4], ALU.mult, ALU.add).then_inc(S("dup_used"), 1)
                    dve.wait_ge(S("dup_used"), g + 1)
                if t % 4 == 3 and t // 4 < NT:
                    v = t // 4
                    dve.wait_ge(S("V_psum"), v + 1)
                    tt(V[:, v, :], pb[3 + v][:, :], bvr, ALU.add).then_inc(S("V_ready"), 1)
                if t == 16:
                    dve.wait_ge(S("bit_w_loaded"), 32)
                    dve.tensor_reduce(wabs[:, 0:1], wu, AX, ALU.add, apply_absolute_value=True).then_inc(S("bit_abs_ready"), 1)
                    dve.tensor_reduce(wabs[:, 1:2], wd, AX, ALU.add, apply_absolute_value=True).then_inc(S("bit_abs_ready"), 1)
                j = t % NGA
                dve.wait_ge(S(f"edge_rows{j}"), 32 * (t // NGA + 1))
                for h in range(H):
                    go(stt(lsc[:, P * h:P * h + P], ga[j][:, P * h:P * h + P], 0.0, waR, ALU.max, ALU.mult,
                           accum_out=w_e3[:, t, h:h + 1]))
                settle()
                one(tt(w_e3[:, t, :], w_e3[:, t, :], ga[j][:, 2 * D:ROW], ALU.add))
                dve.engine_nop().then_inc(S("w_ready"), 1)
            dve.wait_ge(S("onehot_used"), ET)
            for s in range(NT):
                go(dve.tensor_copy(cnt[:, s, :], pb[s][:, 0:N]))
            settle()
            go(dve.tensor_copy(cntI_s[:, :], cnt_s[:, :]))
            outdeg = V_("outdeg", 3)
            go(dve.tensor_reduce(outdeg, cnt, AX, ALU.add))
            settle()
            for s in range(NT):
                go(tt(cntI[:, s, P * s:P * s + P], cntI[:, s, P * s:P * s + P], ident[:, :], ALU.add))
            settle()
            dve.engine_nop().then_inc(S("cnt_ready"), 1)
            for t in range(NT):
                go(ts(xn3[:, t, :], xn3[:, t, :], 1.0, None, ALU.subtract))
                go(tt(x3[:, t, :], x3[:, t, :], b0r, ALU.add))
            nmax, psum_ = V_("nmax", 24), V_("psum_", 24)
            dis, dinv, wsc, half_sc = V_("dis", 3), V_("dinv", 3), V_("wsc", 2), V_("half_sc", 4)

            def row_max(i):
                dve.wait_ge(S(f"read_back{i}"), 16)
                m = nmax[:, H * i:H * i + H]
                one(dve.tensor_reduce(m, mt[i].rearrange("p n h -> p h n"), AX, ALU.max))
                ts(m, m, NEG_FLOOR, -1.0, ALU.max, ALU.mult).then_inc(S("row_max_ready"), 1)

            def copy_probsT(i, h):
                u = H * i + h
                dve.wait_ge(S("probsT_psum"), u + 1)
                dve.tensor_copy(probsT[h][:, :, P * i:P * i + P], pb[u % 3][:, 0:N].rearrange("p (c n) -> p c n", c=NT)).then_inc(S("probsT_ready"), 1)

            row_max(0)
            row_max(1)
            for h in range(H):
                copy_probsT(0, h)
            row_max(2)
            copy_probsT(2, 0)
            dve.wait_ge(S("deg_psum"), 1)
            go(dve.tensor_copy(dis, outdeg))
            go(dve.tensor_copy(dinv, pb[6][:, 0:3]))
            asked[0] += 1
            dve.tensor_copy(dinv_bc[:, :], pb[7][:, 0:N]).then_inc(S("root_asked"), 1)
            copy_probsT(2, 1)
            go(ts(rdeg_bc[:, :], pb[7][:, 0:N], 1.0, None, ALU.max))
            go(ts(wsc, pb[6][:, 8:10], 1.0 / (D * F1), EPS, ALU.mult, ALU.max))
            settle()
            go(ts(half_sc[:, 0:2], wsc, 0.5, None, ALU.mult))
            ts(half_sc[:, 2:4], wsc, -0.5, None, ALU.mult).then_inc(S("half_sc_ready"), 1)
            copy_probsT(2, 2)
            for h in (3, 4):
                copy_probsT(2, h)
            copy_probsT(2, 5)
            dve.wait_ge(S("root_ready"), asked[0])
            go(dve.reciprocal(dis, dis))
            go(dve.reciprocal(dinv, dinv))
            copy_probsT(2, 6)
            settle()
            copy_probsT(2, 7)
            rs = V_("rs", 24)
            one(ts(rs, psum_, 1e-30, None, ALU.max))
            one(dve.reciprocal(rs, rs))
            for t in range(NT):
                dve.wait_ge(S("attended_back"), t + 1)
                one(tt(y0[:, t, :].rearrange(heads, h=H), pb[t][:, :].rearrange(heads, h=H), bc(rs[:, H * t:H * t + H, None], [P, H, HD]), ALU.mult))
                ts(ye[:, t, :], y0[:, t, :], 0.0, None, ALU.min).then_inc(S("ymin_ready"), 1)
                go(stt(yr[:, t, :], y0[:, t, :], 0.0, xn3[:, t, :], ALU.max, ALU.add))
            def elu(t):
                dve.wait_ge(S("yexp_ready"), t + 1)
                go(tt(y0[:, t, :], ye[:, t, :], yr[:, t, :], ALU.add))

            scaled_norm(y0, yr, g0r, elu)

            layernorm(x3, xn3, produce=add_norm(yr), produced=x_tile_ready(0))
            dve.engine_nop().then_inc(S("shifter_in_ready"), 1)
            first = V_("first", 144).rearrange("p (t c) -> p t c", t=NT)
            for t in range(NT):
                go(stt(first[:, t, :], xn3[:, t, 64:112], 0.5, fall48[:, :], ALU.is_gt, ALU.mult))
            settle()
            far, idx = V_("far", 9), V_("idx", 9)
            one(dve.tensor_reduce(far, V_("first", 144).rearrange("p (c i) -> p c i", i=16), AX, ALU.max))
            one(ts(idx, far, -1.0, 16.0, ALU.mult, ALU.add))
            one(stt(idx, far, 0.0, idx, ALU.is_gt, ALU.mult))
            idx_i = V_("idx_i", 9).bitcast(i32)
            one(dve.tensor_copy(idx_i, idx))
            ii = idx_i.rearrange("p (t c) -> p t c", t=NT)
            val, left, right = (V_(n_, 3).bitcast(i32) for n_ in ("val", "left", "right"))
            sa_i = V_("sa_i", 3).bitcast(i32)
            mark, shl, shr, both, amp = (V_(n_, 3) for n_ in ("mark", "shl", "shr", "both", "amp"))
            go(dve.tensor_copy(sa_i, ii[:, :, 2]))
            go(ts(mark, xn3[:, :, 0], 0.5, None, ALU.is_gt))
            go(ts(shl, xn3[:, :, 39], 0.5, None, ALU.is_gt))
            go(ts(shr, xn3[:, :, 40], 0.5, None, ALU.is_gt))
            one(ts(val, ii[:, :, 1], 4, None, ALU.logical_shift_left))
            one(tt(val, val, ii[:, :, 0], ALU.bitwise_or))
            go(tt(left, val, sa_i, ALU.logical_shift_left))
            go(tt(right, val, sa_i, ALU.logical_shift_right))
            go(tt(both, shl, shr, ALU.mult))
            settle()
            go(tt(shr, shr, both, ALU.subtract))
            go(tt(shl, shl, mark, ALU.mult))
            go(ts(left, left, 255, None, ALU.bitwise_and))
            settle()
            go(tt(shr, shr, mark, ALU.mult))
            leftf, rightf, res = (V_(n_, 3) for n_ in ("leftf", "rightf", "res"))
            go(dve.tensor_copy(leftf, left))
            go(dve.tensor_copy(rightf, right))
            settle()
            go(tt(leftf, leftf, shl, ALU.mult))
            go(tt(rightf, rightf, shr, ALU.mult))
            go(tt(amp, shl, shr, ALU.add))
            settle()
            go(tt(res, leftf, rightf, ALU.add))
            go(ts(amp, amp, 2.0, None, ALU.mult))
            settle()
            one(dve.tensor_copy(val, res))
            go(ts(left, val, 15, None, ALU.bitwise_and))
            go(ts(right, val, 4, None, ALU.logical_shift_right))
            settle()
            rlo, rhi = V_("rlo", 3), V_("rhi", 3)
            go(dve.tensor_copy(rlo, left))
            go(dve.tensor_copy(rhi, right))
            settle()
            for t in range(NT):
                for o, nib in ((0, rlo), (16, rhi)):
                    go(ts(first[:, t, o:o + 16], iota64[:, 0:16], nib[:, t:t + 1], amp[:, t:t + 1], ALU.is_equal, ALU.mult))
            settle()
            dve.wait_ge(S("shifter_added"), NT)
            tt(x3[:, :, 128:160], x3[:, :, 128:160], first[:, :, 0:32], ALU.add).then_inc(S("x_ready"), NT)
            dve.wait_ge(S("x_ready"), NT * 1 + NT)

            layernorm(x3, xn3, "3")
            dve.wait_ge(S("rows_loaded"), 96)
            nshift, gsum, gsq, gmul, gadd = (V_(n_, 4) for n_ in ("nshift", "gsum", "gsq", "gmul", "gadd"))
            def scale_aggregate(l, k):
                dve.wait_ge(S("agg_psum"), KD * l + k + 1)
                tt(gT[:, k, :], pb[(0, 1, 2, 6)[k]][:, 0:N], dinv_bc[:, :], ALU.mult).then_inc(S("scaled_ready"), 1)

            def shift(l, k):
                dve.wait_ge(S("relu_ready"), KD * l + k + 1)
                stt(nshift[:, k:k + 1], gsum[:, k:k + 1], -1.0 / N, bcol[5][:, k:k + 1], ALU.mult, ALU.mult).then_inc(S("shift_ready"), 1)

            def graph_norm(l, k):
                m, add = gmul[:, k:k + 1], gadd[:, k:k + 1]
                dve.wait_ge(S("graph_root_ready"), KD * l + k + 1)
                one(dve.reciprocal(m, m))
                one(tt(m, m, bcol[3][:, k:k + 1], ALU.mult))
                one(stt(add, nshift[:, k:k + 1], m, bcol[4][:, k:k + 1], ALU.mult, ALU.add))
                ts(xT[:, k, :], gT[:, k, :], m, add, ALU.mult, ALU.add).then_inc(S("hT_ready"), 1)

            one(dve.reciprocal(dinv_bc[:, :], dinv_bc[:, :]))
            one(dve.reciprocal(rdeg_bc[:, :], rdeg_bc[:, :]))
            for l in range(3):
                for t in (0, 2):
                    dve.wait_ge(S("hw_psum"), NT * l + t + 1)
                    ts(xws[:, t, :], pb[3 + t][:, :], dinv[:, t:t + 1], None, ALU.mult).then_inc(S("hw_ready"), 1)
                for k in range(KD):
                    scale_aggregate(l, k)
                    shift(l, k)
                    if k:
                        graph_norm(l, k - 1)
                graph_norm(l, KD - 1)

            def add_convolved(t):
                dve.wait_ge(S("h_out_psum"), t + 1)
                tt(x3[:, t, :], x3[:, t, :], pb[3 + t][:, :], ALU.add).then_inc(S("x_ready"), 1)


            layernorm(x3, xn3, None, add_convolved, x_tile_ready(2))
            amax, xsc, isc, amax2, hsc = (V_(n_, 3) for n_ in ("amax", "xsc", "isc", "amax2", "hsc"))

            def quantise(v3, m, scale, q3, top_ready, f):
                one(dve.tensor_reduce(m, v3, AX, ALU.max, apply_absolute_value=True))
                one(ts(m, m, EPS, None, ALU.max))
                one(dve.reciprocal(scale, m))
                one(ts(scale, scale, 127.0, None, ALU.mult))
                for t in range(NT):
                    go(ts(v3[:, t, :], v3[:, t, :], scale[:, t:t + 1], ROUND, ALU.mult, ALU.add))
                settle()
                for t in range(NT):
                    go(ts(v3[:, t, :], v3[:, t, :], ROUND, 127.0, ALU.subtract, ALU.min))
                settle()
                for t in range(NT):
                    ts(q3[:, t, :], v3[:, t, :], -128.0, None, ALU.max).then_inc(top_ready, 1)

            quantise(xn3, amax, xsc, xq, S("xq_ready"), D)
            one(dve.reciprocal(isc, xsc))
            one(ts(isc, isc, wsc[:, 0:1], None, ALU.mult))
            for t in range(NT):
                dve.wait_ge(S("up_bit_psum"), t + 1)
                go(ts(hb[:, t, :], pb[3 + t][:, 0:F1], isc[:, t:t + 1], 0.0, ALU.mult, ALU.max))
            settle()
            hb2 = WK[:, 1536:2304]
            hr2, hd2 = xT_s[:, 0:768], xT_s[:, 768:1536]
            one(ts(hr2, hb2, ROUND, None, ALU.add))
            one(ts(hr2, hr2, ROUND, 127.0, ALU.subtract, ALU.min))
            one(tt(hd2, hr2, hb2, ALU.subtract))
            one(tt(hb2, hb2, hd2, ALU.add))
            quantise(hb, amax2, hsc, hq, S("hq_ready"), F1)
            one(dve.reciprocal(isc, hsc))
            one(ts(isc, isc, wsc[:, 1:2], None, ALU.mult))
            def add_bit_linear(t):
                dve.wait_ge(S("down_bit_psum"), t + 1)
                stt(x3[:, t, :], pb[3 + t][:, :], isc[:, t:t + 1], x3[:, t, :], ALU.mult, ALU.add).then_inc(S("x_ready"), 1)


            layernorm(x3, xn3, "5", add_bit_linear, x_tile_ready(3))
            for t in range(NT):
                dve.wait_ge(S("hw5_psum"), t + 1)
                one(tt(xws[:, t, :], pb[3 + t][:, :], b2r, ALU.add))
                ts(xws[:, t, :], xws[:, t, :], dis[:, t:t + 1], None, ALU.mult).then_inc(S("hw5_ready"), 1)
            def add_graph5(t):
                dve.wait_ge(S("agg5_psum"), t + 1)
                one(ts(xn3[:, t, :], pb[t][:, :], dis[:, t:t + 1], 0.0, ALU.mult, ALU.max))
                tt(x3[:, t, :], x3[:, t, :], xn3[:, t, :], ALU.add).then_inc(S("x_ready"), 1)


            layernorm(x3, xn3, "6", add_graph5, x_tile_ready(4))
            layernorm(xn3, y6, "6b")
            for k in range(KD):
                if k == 0:
                    dve.wait_ge(S("gate6_psum"), 1)
                    dve.wait_ge(S("xT_psum"), nth("6b", 2))
                ins = ts(xT[:, k, P:2 * P], pb[1][:, P * k:P * k + P], bcol[6][:, k:k + 1], None, ALU.mult)
            ins.then_inc(S("xT_ready"), 1)
            raw6, nm6, ex6, es6 = V_("raw6", 24), V_("nm6", 3), V_("ex6", 24), V_("es6", 3)
            t8_ = "p (t e) -> p t e"
            one(dve.tensor_copy(raw6.rearrange(t8_, t=NT)[:, :, 0:E2], pb[6][:, 0:24].rearrange(t8_, t=NT)[:, :, 0:E2]))
            go(dve.memset(ex6, -1.0))
            one(dve.tensor_reduce(nm6, raw6.rearrange(t8_, t=NT)[:, :, 0:E2], AX, ALU.max, negate=True))
            dve.engine_nop().then_inc(S("raw6_ready"), 1)
            dve.wait_ge(S("ex6_ready"), NT)
            one(dve.reciprocal(es6, es6))
            top6, gm6, den6 = V_("top6", 24), V_("gm6", 24), V_("den6", 3)
            for t in range(NT):
                e8 = ex6[:, 8 * t:8 * t + 8]
                one(ts(e8, e8, es6[:, t:t + 1], None, ALU.mult))
                one(dve.max(top6[:, 8 * t:8 * t + 8], e8))
                one(dve.max_index(smi[:, 8 * t:8 * t + 8], top6[:, 8 * t:8 * t + 8], e8))
                one(tt(den6[:, t:t + 1], top6[:, 8 * t:8 * t + 1], top6[:, 8 * t + 1:8 * t + 2], ALU.add))
                one(ts(den6[:, t:t + 1], den6[:, t:t + 1], 1e-9, None, ALU.add))
                one(dve.reciprocal(den6[:, t:t + 1], den6[:, t:t + 1]))
                one(tt(den6[:, t:t + 1], den6[:, t:t + 1], top6[:, 8 * t:8 * t + 1], ALU.mult))
                go(dve.tensor_copy(idx[:, t:t + 1], smi[:, 8 * t:8 * t + 1]))
                settle()
                one(ts(gm6[:, 8 * t:8 * t + 8], iota64[:, 0:8], idx[:, t:t + 1], den6[:, t:t + 1], ALU.is_equal, ALU.mult))
            def add_expert6(e, t):
                j = NT * e + t
                dve.wait_ge(S("out6_psum"), j + 1)
                if e:
                    dve.wait_ge(S("out6_used"), j - NT + 1)
                stt(x3[:, t, :], pb[(3, 4, 5, 7)[j % 4]][:, :], gm6[:, 8 * t + e:8 * t + e + 1], x3[:, t, :],
                    ALU.mult, ALU.add).then_inc(S("out6_used"), 1)

            for e in range(E2 - 1):
                for t in range(NT):
                    add_expert6(e, t)

            layernorm(x3, xn3, "7", lambda t: add_expert6(E2 - 1, t), lambda t: dve.wait_ge(S("out6_used"), NT * (E2 - 1) + t + 1))
            dve.engine_nop().then_inc(S("x_ready"), NT)
            for t in range(NT):
                go(tt(x3[:, t, :], x3[:, t, :], be3r, ALU.add))
            for k in range(KD):
                dve.wait_ge(S("neigh_psum"), k + 1)
                tt(gT[:, k, :], pb[3 + k][:, 0:N], rdeg_bc[:, :], ALU.mult).then_inc(S("neighT_ready"), 1)
            def add_bias7(t):
                dve.wait_ge(S("sage_psum"), t + 1)
                tt(y6[:, t, :], pb[t][:, :], b3r, ALU.add).then_inc(S("sage_used"), 1)
                dve.wait_ge(S("sage_used"), t + 1)

            scaled_norm(y6, ye7, g3r, add_bias7)

            layernorm(x3, xn3, "8", add_norm(ye7), x_tile_ready(6))
            dve.wait_ge(S("sigmoid_ready"), 1)
            one(tt(biased, scores8, bc(gateb[:, None, :], [P, NT, E3]), ALU.add))
            b2 = WK[:, 192:384]
            for g in range(NT * G3):
                go(dve.max(top_in_group[:, g, :], b2[:, 8 * g:8 * g + 8]))
            settle()
            gsc, rank = V_("gsc", 24), V_("rank", 24)
            one(tt(gsc, top_in_group[:, :, 0], top_in_group[:, :, 1], ALU.add))
            g3 = gsc.rearrange("p (t g) -> p t g", t=NT)
            other, own = bc(g3[:, :, None, :], [P, NT, G3, G3]), bc(g3[:, :, :, None], [P, NT, G3, G3])
            be, ti = (v.rearrange("p (t g m) -> p t g m", t=NT, g=G3) for v in (beats, ties))
            go(tt(be, other, own, ALU.is_gt))
            one(tt(ti, other, own, ALU.is_equal))
            tie3 = "p (t c) -> p t c"
            one(tt(ties.rearrange(tie3, t=NT), ties.rearrange(tie3, t=NT), bc(tri8[:, None, :], [P, NT, G3 * G3]), ALU.mult))
            one(tt(beats, beats, ties, ALU.add))
            one(dve.tensor_reduce(rank, beats.rearrange("p (c m) -> p c m", m=G3), AX, ALU.add))
            one(ts(rank, rank, float(TOPG), 1e30, ALU.is_ge, ALU.mult))
            grp = "p (g m) -> p g m"
            one(tt(WK[:, 704:896].rearrange(grp, m=8), b2.rearrange(grp, m=8), bc(rank[:, :, None], [P, NT * G3, 8]), ALU.subtract))
            top8, idx8f = V_("top8", 24), V_("idx8f", 24)
            for t in range(NT):
                v8 = top8[:, 8 * t:8 * t + 8]
                one(dve.max(v8, masked[:, t, :]))
                go(dve.max_index(smi[:, 8 * t:8 * t + 8], v8, masked[:, t, :]))
                go(dve.match_replace(replaced[:, t, :], v8, masked[:, t, :], NEG))
            settle()
            go(dve.tensor_copy(idx8f, smi[:, 0:24]))
            go(ts(WK[:, 1088:1280], WK[:, 896:1088], -2e38, None, ALU.is_lt))
            settle()
            dve.tensor_copy(WK[:, 1536:1632].bitcast(bf16), WK[:, 1088:1280]).then_inc(S("picked_ready"), 1)
            one(tt(WK[:, 1088:1280], WK[:, 1088:1280], WK[:, 0:192], ALU.mult))
            wsum = V_("wsum", 3)
            one(dve.tensor_reduce(wsum, selw, AX, ALU.add))
            one(dve.reciprocal(wsum, wsum))
            for t in range(NT):
                go(ts(selw[:, t, :], selw[:, t, :], wsum[:, t:t + 1], ROUTED_SCALE, ALU.mult, ALU.mult))
            settle()
            id3 = idx8f.rearrange("p (t k) -> p t k", t=NT)
            for t in range(NT):
                go(tt(kth[:, t], bc(id3[:, t, None, :], [P, EF, K3]), bc(iota64[:, 0:EF, None], [P, EF, K3]), ALU.is_equal))
            settle()
            for t in range(NT):
                go(tt(kth[:, t], kth[:, t], bc(iota64[:, None, 0:K3], [P, EF, K3]), ALU.mult))
            settle()
            kcol = V_("kcol", NT * EF)
            one(dve.tensor_reduce(kcol, kth_s.rearrange("p (c k) -> p c k", k=K3), AX, ALU.add))
            go(tt(first_rec4[:, :, :, 1], first_rec4[:, :, :, 1], kcol.rearrange("p (t e) -> p t e", t=NT), ALU.add))
            go(dve.tensor_copy(first_rec4[:, :, :, 2], selw[:, :, 0:EF]))
            dve.wait_ge(S("place_psum"), 1)
            ps4 = pb[4][:, 0:E3 * NT].rearrange("p (t e) -> p t e", t=NT)
            one(stt(place1, ps4[:, :, 0:EF], 1.0, picked[:, :, 0:EF], ALU.add, ALU.mult))

            def onehots(lo, hi):
                for e in range(lo, hi):
                    for t in range(NT):
                        ts(first_oh[:, e, t, :], iota_h[:, 1:P + 1], place1[:, t, e:e + 1], None, ALU.is_equal).then_inc(S("first_onehot"), 1)

            def first_slots(lo, hi):
                dve.wait_ge(S("first_slots_psum"), hi)
                v = pb[5][:, 0:4 * EF].rearrange("p (e c) -> p e c", e=EF)[:, lo:hi]
                go(ts(first_slot3[:, lo:hi, 0], v[:, :, 0], float(N), None, ALU.add))
                go(ts(first_slot3[:, lo:hi, 1], v[:, :, 1], float(N * K3), None, ALU.add))
                dve.tensor_copy(first_slot[:, :].bitcast(f32).rearrange("p (e c) -> p e c", e=EF)[:, lo:hi, 2], v[:, :, 2]).then_inc(S("first_slots_ready"), 1)

            def copy_xeT(e):
                dve.wait_ge(S("xe_psum"), e + 1)
                if e >= 2:
                    dve.wait_ge(S("up_psum"), e - 1)
                dve.tensor_copy(R2[:, 3072 + D * (e % 2):3072 + D * (e % 2) + D], pb[e % 2][:, :]).then_inc(S("xeT_ready"), 1)

            def gate_hidden(e):
                dve.wait_ge(S("silu_ready"), e + 1)
                if e >= 2:
                    dve.wait_ge(S("hT_psum"), e - 1)
                tt(hmid[e % 2], act[e % 2], pb[2 + e % 2][:, F3:2 * F3], ALU.mult).then_inc(S("hmid_ready"), 1)

            onehots(0, 2)
            for t in range(NT):
                go(stt(place[:, t, :], pb[4][:, E3 * t:E3 * t + E3], float(E3), iota64[:, :], ALU.mult, ALU.add))
            first_slots(0, 2)
            onehots(2, 4)
            first_slots(2, 4)
            copy_xeT(0)
            onehots(4, EF)
            settle()
            one(dve.tensor_reduce(V_("most", 1), pb[4][:, E3 * NT:E3 * NT + E3], AX, ALU.max))
            dve.tensor_copy(most[:, :], V_("most", 1)).then_inc(S("most_ready"), 1)
            recf = rec[:, :].bitcast(f32).rearrange("p (t k c) -> p t k c", t=NT, k=K3)

            def picks(t):
                for k in range(K3):
                    c = K3 * t + k
                    o = 128 * k
                    go(stt(xT_s[:, o:o + E3], iota64[:, :], idx8f[:, c:c + 1], place[:, t, :], ALU.is_equal, ALU.mult, accum_out=pick_row_f[:, c:c + 1]))
                    go(stt(xT_s[:, o + E3:o + 2 * E3], iota64[:, :], idx8f[:, c:c + 1], selw[:, t, :], ALU.is_equal, ALU.mult, accum_out=recf[:, t, k, 2:3]))
                settle()
                dve.tensor_copy(pick_row[:, K3 * t:K3 * t + K3], pick_row_f[:, K3 * t:K3 * t + K3]).then_inc(S("picks_ready"), 1)

            for e in range(E3):
                if e < NT:
                    picks(e)
                if e + 1 < E3:
                    copy_xeT(e + 1)
                gate_hidden(e)
                if e == 0:
                    first_slots(4, EF)

            def gate_rest(dve, s, e, nth_):
                dve.wait_ge(S("rest_evacuated"), nth_ * 4 - 2)
                tt(hmid[0], act[0], pb[2][:, F3:2 * F3], ALU.mult).then_inc(S("rest_hmid"), 1)

            rest(dve, gate_rest)
            for half in range(2):
                for t in range(NT):
                    dve.wait_ge(S(f"read_back{t}"), 32) if half == 0 else dve.wait_ge(S(f"last_picks{t}"), 16)
                    y = ypick[t][:, 4 * D * half:4 * D * half + 4 * D]
                    for w in (2, 1):
                        one(tt(y[:, 0:D * w], y[:, 0:D * w], y[:, D * w:2 * D * w], ALU.add))
                    if half:
                        tt(x3[:, t, :], x3[:, t, :], y[:, 0:D], ALU.add).then_inc(S("x_ready"), 1)
                    else:
                        one(tt(x3[:, t, :], x3[:, t, :], y[:, 0:D], ALU.add))


def kernel(x, src, dst, **w):
    import numpy as np
    import concourse.bacc as bacc
    from concourse.bass_utils import run_bass_kernel_spmd as run

    def col(v):
        return np.asarray(v).reshape(KD, P).T

    g = {k: np.asarray(v) for k, v in w.items()}
    arrays = {
        "x": np.asarray(x), "src": np.asarray(src), "dst": np.asarray(dst),
        "L0_Ww": g["L0_gnn_Ww"], "L0_bw": g["L0_gnn_bw"], "L0_Wv": g["L0_gnn_Wv"], "L0_bv": g["L0_gnn_bv"],
        "L0_gamma": g["L0_gnn_gamma"], "L0_beta": g["L0_gnn_beta"], "L0_Wa": g["L0_gnn_Wa"].reshape(-1), "L0_ba": g["L0_gnn_ba"],
        "L1_W0": g["L1_gnn_W0"], "L1_W1": g["L1_gnn_W1"], "L1_W2": g["L1_gnn_W2"],
        "L1_wu": g["L1_ffn_w_up"].T, "L1_wd": g["L1_ffn_w_down"].T,
        "L2_W": g["L2_gnn_W"].T, "L2_b": g["L2_gnn_b"],
        "L2_w_gating": g["L2_ffn_w_gating"], "L2_w1": g["L2_ffn_w1"], "L2_w2": g["L2_ffn_w2"],
        "L3_self": g["L3_gnn_W_self"].T, "L3_neigh": g["L3_gnn_W_neigh"].T,
        "L3_bias": g["L3_gnn_bias"], "L3_gamma": g["L3_gnn_gamma"], "L3_beta": g["L3_gnn_beta"],
        "L3_gate_w": g["L3_ffn_gate_w"].T, "L3_gate_b": g["L3_ffn_gate_b"],
        "L3_w1": g["L3_ffn_w1"], "L3_w3": g["L3_ffn_w3"], "L3_w2": g["L3_ffn_w2"],
        "fcols": np.concatenate([col(g[k]) for k in (
            "L1_gnn_b0", "L1_gnn_b1", "L1_gnn_b2", "L1_gnn_gn_weight", "L1_gnn_gn_bias", "L1_gnn_gn_mean_scale",
            "L2_ffn_gamma")], axis=1),
    }
    arrays = {k: np.ascontiguousarray(v) for k, v in arrays.items()}
    nc = bacc.Bacc("TRN2", target_bir_lowering=False, num_devices=1)
    ins = {k: nc.dram_tensor(k, v.shape, mybir.dt.from_np(v.dtype), kind="ExternalInput").ap() for k, v in arrays.items()}
    out = nc.dram_tensor("out", (N, D), f32, kind="ExternalOutput").ap()
    build(nc, ins, out)
    r = run(nc, [arrays], core_ids=[0])
    return r.results[0]["out"]
```
